# Optimizing a Trainium2 kernel written in Bass

```python
import numpy as np
import jax
import jax.numpy as jnp

def _softmax(x, axis=-1):
    return jax.nn.softmax(x, axis=axis)

def _gelu(x):
    return jax.nn.gelu(x, approximate=True)

def _silu(x):
    return jax.nn.silu(x)

def _sigmoid(x):
    return jax.nn.sigmoid(x)

def _layernorm(x, axis=-1, eps=1e-05):
    m = jnp.mean(x, axis=axis, keepdims=True)
    v = jnp.var(x, axis=axis, keepdims=True)
    return (x - m) / jnp.sqrt(v + eps)

def _scatter_add(tgt, idx, src, axis=0):
    return tgt.at[idx].add(src)

def _segment_sum(src, seg, n):
    return jax.ops.segment_sum(src, seg, n)
kernel_name = 'mk_early_fusion_embed_d1_tok_img1024_r4_b71e93'

def setup_inputs(seed: int=0):
    np.random.seed(seed)
    _w = jnp.asarray

    def _rec_inputs():
        import jax
        import jax.numpy as jnp
        _rk = jax.random.key(seed)
        x = -0.00016672 + 0.999947 * jax.random.normal(jax.random.fold_in(_rk, 1), (64, 3, 64, 64), jnp.float32)
        x_txt = jax.random.randint(jax.random.fold_in(_rk, 51), (64, 128), 0, 267694, jnp.int32)
        return (x, x_txt)
    x, x_txt = _rec_inputs()

    def _L0_tok_setup():
        import jax, jax.numpy as jnp
        import numpy as np
        IMG = 96
        PATCH = 16
        CIN = 3
        DIM = 256
        B = 64
        key = jax.random.key(seed)
        k1, k2 = jax.random.split(key)
        x = jax.random.normal(k1, (B, CIN, IMG, IMG), dtype=jnp.float32)
        W = jax.random.normal(k2, (DIM, PATCH * PATCH * CIN), dtype=jnp.float32) * 0.02
        return {'x': x, 'W': W}
    _L0_tok_all = _L0_tok_setup()
    _L0_tok_in = {k: v for k, v in _L0_tok_all.items() if k in ('W',)}
    del _L0_tok_all

    def _L0_txt_setup():
        import jax, jax.numpy as jnp
        import numpy as np
        N_CLASSES = 267735
        CUTOFFS_EXT = [0, 5000, 10000, 50000, N_CLASSES]
        D_MODEL = 256
        REDUCTION = 4
        key = jax.random.key(seed)
        ks = jax.random.split(key, 9)
        B, S = (8, 1024)
        indices = jax.random.randint(ks[0], (B, S), 0, N_CLASSES, dtype=jnp.int64 if jax.config.jax_enable_x64 else jnp.int32)
        inp = {'indices': indices}
        d = D_MODEL
        for i in range(4):
            count = CUTOFFS_EXT[i + 1] - CUTOFFS_EXT[i]
            inp[f'emb{i}'] = jax.random.normal(ks[1 + i], (count, d), dtype=jnp.float32)
            inp[f'W{i}'] = jax.random.normal(ks[5 + i], (D_MODEL, d), dtype=jnp.float32) * 0.02
            d = d // REDUCTION
        return inp
    _L0_txt_all = _L0_txt_setup()
    _L0_txt_in = {k: v for k, v in _L0_txt_all.items() if k in ('emb0', 'emb1', 'emb2', 'emb3', 'W0', 'W1', 'W2', 'W3')}
    del _L0_txt_all

    def _L0_attn_setup():
        import jax, jax.numpy as jnp
        import numpy as np
        DIM = 256
        D_INNER = 256
        N_STATE = 32
        N_BLOCKS = 4
        TOP_K = 2
        ROUTER_TEMP = 1.0
        INIT_BETA_BIAS = 2.0
        BATCH = 16
        T = 512

        def _xavier(key, shape):
            fan_out, fan_in = shape
            lim = jnp.sqrt(6.0 / (fan_in + fan_out))
            return jax.random.uniform(key, shape, jnp.float32, -lim, lim)

        def _cell_scan(x_rnn, W_router, W_kv, W_beta, b_beta, W_q):
            Tt, batch, D = x_rnn.shape
            n, nb = (N_STATE, N_BLOCKS)
            xf = x_rnn.reshape(Tt * batch, D)
            logits = (xf @ W_router.T).reshape(Tt, batch, nb) / ROUTER_TEMP
            kv = (xf @ W_kv.T).reshape(Tt, batch, nb, 2, n)
            beta = jax.nn.sigmoid((xf @ W_beta.T).reshape(Tt, batch, nb, n) + b_beta)
            q = (xf @ W_q.T).reshape(Tt, batch, n)
            S0 = jnp.zeros((batch, nb, n, n), x_rnn.dtype)
            rows = jnp.arange(batch)[:, None]

            def step(S, inp):
                logits_t, k_t, v_t, beta_t, q_t = inp
                _, idx = jax.lax.top_k(logits_t, TOP_K)
                mask = jnp.zeros_like(logits_t).at[rows, idx].set(1.0)
                sm = jax.nn.softmax(logits_t, axis=-1)
                uw = mask * sm
                uw = uw / (uw.sum(-1, keepdims=True) + 1e-08)
                kn = k_t / (jnp.linalg.norm(k_t, axis=-1, keepdims=True) + 1e-06)
                retrieved = jnp.einsum('bnij,bnj->bni', S, kn)
                delta = v_t - retrieved
                outer = delta[..., :, None] * kn[..., None, :]
                S_upd = jnp.tanh(beta_t[..., None] * S + outer)
                w = uw[..., None, None]
                S_new = (1.0 - w) * S + w * S_upd
                Sq = jnp.einsum('bnij,bj->bni', S_new, q_t)
                block_out = Sq * (Sq * jax.nn.sigmoid(Sq))
                out_t = jnp.einsum('bn,bnd->bd', sm, block_out)
                return (S_new, out_t)
            S_final, outs = jax.lax.scan(step, S0, (logits, kv[..., 0, :], kv[..., 1, :], beta, q))
            return (outs, S_final)

        def _reference_tuple_inner(x, W_in, W_router, W_kv, W_beta, b_beta, W_q, W_out):
            x_proj = jax.nn.silu(x @ W_in.T)
            x_rnn = jnp.transpose(x_proj, (1, 0, 2))
            cell_out, S_final = _cell_scan(x_rnn, W_router, W_kv, W_beta, b_beta, W_q)
            y = jnp.transpose(cell_out, (1, 0, 2)) @ W_out.T
            return (y, S_final)
        key = jax.random.key(seed)
        ks = jax.random.split(key, 7)
        x = jax.random.normal(ks[0], (BATCH, T, DIM), jnp.float32)
        W_in = _xavier(ks[1], (D_INNER, DIM))
        W_router = _xavier(ks[2], (N_BLOCKS, D_INNER))
        W_kv = _xavier(ks[3], (N_BLOCKS * 2 * N_STATE, D_INNER))
        W_beta = _xavier(ks[4], (N_BLOCKS * N_STATE, D_INNER))
        b_beta = jnp.full((N_BLOCKS, N_STATE), INIT_BETA_BIAS, jnp.float32)
        W_q = _xavier(ks[5], (N_STATE, D_INNER))
        W_out = _xavier(ks[6], (DIM, N_STATE))
        return {'x': x, 'W_in': W_in, 'W_router': W_router, 'W_kv': W_kv, 'W_beta': W_beta, 'b_beta': b_beta, 'W_q': W_q, 'W_out': W_out}
    _L0_attn_all = _L0_attn_setup()
    _L0_attn_in = {k: v for k, v in _L0_attn_all.items() if k in ('W_in', 'W_router', 'W_kv', 'W_beta', 'b_beta', 'W_q', 'W_out')}
    del _L0_attn_all

    def _L0_ffn_setup():
        import jax, jax.numpy as jnp
        import numpy as np
        TOP_K = 2
        key = jax.random.key(seed)
        ks = jax.random.split(key, 6)
        B, S, D, BN, E = (32, 512, 256, 64, 8)
        return {'x': jax.random.normal(ks[0], (B, S, D), dtype=jnp.float32), 'gate_w': jax.random.normal(ks[1], (E, D), dtype=jnp.float32) * 0.02, 'down_w': jax.random.normal(ks[2], (E, BN, D), dtype=jnp.float32) * 0.02, 'down_b': jax.random.normal(ks[3], (E, BN), dtype=jnp.float32) * 0.02, 'up_w': jax.random.normal(ks[4], (E, D, BN), dtype=jnp.float32) * 0.02, 'up_b': jax.random.normal(ks[5], (E, D), dtype=jnp.float32) * 0.02}
    _L0_ffn_all = _L0_ffn_setup()
    _L0_ffn_in = {k: v for k, v in _L0_ffn_all.items() if k in ('gate_w', 'down_w', 'down_b', 'up_w', 'up_b')}
    del _L0_ffn_all
    return {'x': x, 'x_txt': x_txt, 'L0_tok_W': _L0_tok_in['W'], 'L0_txt_emb0': _L0_txt_in['emb0'], 'L0_txt_emb1': _L0_txt_in['emb1'], 'L0_txt_emb2': _L0_txt_in['emb2'], 'L0_txt_emb3': _L0_txt_in['emb3'], 'L0_txt_W0': _L0_txt_in['W0'], 'L0_txt_W1': _L0_txt_in['W1'], 'L0_txt_W2': _L0_txt_in['W2'], 'L0_txt_W3': _L0_txt_in['W3'], 'L0_attn_W_in': _L0_attn_in['W_in'], 'L0_attn_W_router': _L0_attn_in['W_router'], 'L0_attn_W_kv': _L0_attn_in['W_kv'], 'L0_attn_W_beta': _L0_attn_in['W_beta'], 'L0_attn_b_beta': _L0_attn_in['b_beta'], 'L0_attn_W_q': _L0_attn_in['W_q'], 'L0_attn_W_out': _L0_attn_in['W_out'], 'L0_ffn_gate_w': _L0_ffn_in['gate_w'], 'L0_ffn_down_w': _L0_ffn_in['down_w'], 'L0_ffn_down_b': _L0_ffn_in['down_b'], 'L0_ffn_up_w': _L0_ffn_in['up_w'], 'L0_ffn_up_b': _L0_ffn_in['up_b']}

def reference(x, x_txt, L0_tok_W, L0_txt_emb0, L0_txt_emb1, L0_txt_emb2, L0_txt_emb3, L0_txt_W0, L0_txt_W1, L0_txt_W2, L0_txt_W3, L0_attn_W_in, L0_attn_W_router, L0_attn_W_kv, L0_attn_W_beta, L0_attn_b_beta, L0_attn_W_q, L0_attn_W_out, L0_ffn_gate_w, L0_ffn_down_w, L0_ffn_down_b, L0_ffn_up_w, L0_ffn_up_b):
    import jax
    import jax.numpy as jnp

    def _L0_tok_ref(x, W):
        import jax, jax.numpy as jnp
        import numpy as np
        IMG = 96
        PATCH = 16
        CIN = 3
        DIM = 256
        B = 64
        B_, C, H, Wd = x.shape
        p = PATCH
        nh, nw = (H // p, Wd // p)
        patches = x.reshape(B_, C, nh, p, nw, p)
        patches = patches.transpose(0, 2, 4, 1, 3, 5)
        patches = patches.reshape(B_, nh * nw, C * p * p)
        return jnp.einsum('bnd,kd->bnk', patches, W)

    def _L0_txt_ref(indices, emb0, emb1, emb2, emb3, W0, W1, W2, W3):
        import jax, jax.numpy as jnp
        import numpy as np
        N_CLASSES = 267735
        CUTOFFS_EXT = [0, 5000, 10000, 50000, N_CLASSES]
        D_MODEL = 256
        REDUCTION = 4
        embs = [emb0, emb1, emb2, emb3]
        Ws = [W0, W1, W2, W3]
        out = jnp.zeros(indices.shape + (D_MODEL,), dtype=emb0.dtype)
        for i in range(4):
            lo, hi = (CUTOFFS_EXT[i], CUTOFFS_EXT[i + 1])
            mask = (indices >= lo) & (indices < hi)
            rel = jnp.clip(indices - lo, 0, hi - lo - 1)
            xx = jnp.einsum('bsd,ed->bse', embs[i][rel], Ws[i])
            out = jnp.where(mask[..., None], xx, out)
        return out

    def _L0_attn_ref(x, W_in, W_router, W_kv, W_beta, b_beta, W_q, W_out):
        import jax, jax.numpy as jnp
        import numpy as np
        DIM = 256
        D_INNER = 256
        N_STATE = 32
        N_BLOCKS = 4
        TOP_K = 2
        ROUTER_TEMP = 1.0
        INIT_BETA_BIAS = 2.0
        BATCH = 16
        T = 512

        def _xavier(key, shape):
            fan_out, fan_in = shape
            lim = jnp.sqrt(6.0 / (fan_in + fan_out))
            return jax.random.uniform(key, shape, jnp.float32, -lim, lim)

        def _cell_scan(x_rnn, W_router, W_kv, W_beta, b_beta, W_q):
            Tt, batch, D = x_rnn.shape
            n, nb = (N_STATE, N_BLOCKS)
            xf = x_rnn.reshape(Tt * batch, D)
            logits = (xf @ W_router.T).reshape(Tt, batch, nb) / ROUTER_TEMP
            kv = (xf @ W_kv.T).reshape(Tt, batch, nb, 2, n)
            beta = jax.nn.sigmoid((xf @ W_beta.T).reshape(Tt, batch, nb, n) + b_beta)
            q = (xf @ W_q.T).reshape(Tt, batch, n)
            S0 = jnp.zeros((batch, nb, n, n), x_rnn.dtype)
            rows = jnp.arange(batch)[:, None]

            def step(S, inp):
                logits_t, k_t, v_t, beta_t, q_t = inp
                _, idx = jax.lax.top_k(logits_t, TOP_K)
                mask = jnp.zeros_like(logits_t).at[rows, idx].set(1.0)
                sm = jax.nn.softmax(logits_t, axis=-1)
                uw = mask * sm
                uw = uw / (uw.sum(-1, keepdims=True) + 1e-08)
                kn = k_t / (jnp.linalg.norm(k_t, axis=-1, keepdims=True) + 1e-06)
                retrieved = jnp.einsum('bnij,bnj->bni', S, kn)
                delta = v_t - retrieved
                outer = delta[..., :, None] * kn[..., None, :]
                S_upd = jnp.tanh(beta_t[..., None] * S + outer)
                w = uw[..., None, None]
                S_new = (1.0 - w) * S + w * S_upd
                Sq = jnp.einsum('bnij,bj->bni', S_new, q_t)
                block_out = Sq * (Sq * jax.nn.sigmoid(Sq))
                out_t = jnp.einsum('bn,bnd->bd', sm, block_out)
                return (S_new, out_t)
            S_final, outs = jax.lax.scan(step, S0, (logits, kv[..., 0, :], kv[..., 1, :], beta, q))
            return (outs, S_final)

        def _reference_tuple_inner(x, W_in, W_router, W_kv, W_beta, b_beta, W_q, W_out):
            x_proj = jax.nn.silu(x @ W_in.T)
            x_rnn = jnp.transpose(x_proj, (1, 0, 2))
            cell_out, S_final = _cell_scan(x_rnn, W_router, W_kv, W_beta, b_beta, W_q)
            y = jnp.transpose(cell_out, (1, 0, 2)) @ W_out.T
            return (y, S_final)
        return _reference_tuple_inner(x, W_in, W_router, W_kv, W_beta, b_beta, W_q, W_out)[0]

    def _L0_ffn_ref(x, gate_w, down_w, down_b, up_w, up_b):
        import jax, jax.numpy as jnp
        import numpy as np
        TOP_K = 2
        pooled = x.mean(axis=1)
        gate = jax.nn.softmax(pooled @ gate_w.T, axis=-1)
        top_w, top_i = jax.lax.top_k(gate, TOP_K)
        top_w = top_w / (top_w.sum(axis=-1, keepdims=True) + 1e-08)
        Wd = down_w[top_i]
        bd = down_b[top_i]
        Wu = up_w[top_i]
        bu = up_b[top_i]
        h = jax.nn.gelu(jnp.einsum('bsd,bkcd->bksc', x, Wd) + bd[:, :, None, :], approximate=False)
        h = h * top_w[:, :, None, None]
        out = jnp.einsum('bksc,bkdc->bsd', h, Wu)
        out = out + (top_w[:, :, None] * bu).sum(axis=1)[:, None, :]
        return out
    h = _L0_tok_ref(x, L0_tok_W)
    h = jnp.concatenate([h, _L0_txt_ref(x_txt, L0_txt_emb0, L0_txt_emb1, L0_txt_emb2, L0_txt_emb3, L0_txt_W0, L0_txt_W1, L0_txt_W2, L0_txt_W3)], axis=1)
    h = h + _L0_attn_ref(_layernorm(h, axis=-1), L0_attn_W_in, L0_attn_W_router, L0_attn_W_kv, L0_attn_W_beta, L0_attn_b_beta, L0_attn_W_q, L0_attn_W_out)
    h = h + _L0_ffn_ref(_layernorm(h, axis=-1), L0_ffn_gate_w, L0_ffn_down_w, L0_ffn_down_b, L0_ffn_up_w, L0_ffn_up_b)
    return h

_drawn_inputs = setup_inputs


def setup_inputs(seed=0):
    import zlib

    import numpy as np

    out = dict(_drawn_inputs(seed))
    spreads = {'L0_attn_b_beta': (2.0, 0.2)}
    factors = {'L0_ffn_down_b': 8.0}
    for name, (base, spread) in spreads.items():
        noise = np.random.default_rng([zlib.crc32(name.encode()), seed]).standard_normal(out[name].shape)
        drawn = base * np.exp(spread * noise) if base else spread * noise
        out[name] = jnp.asarray(drawn.astype(out[name].dtype))
    for name, factor in factors.items():
        out[name] = (out[name] * factor).astype(out[name].dtype)
    return out
```

```python
from contextlib import ExitStack

import concourse.bass as bass
from concourse import mybir

P = 128
ALU = mybir.AluOpType
ACT = mybir.ActivationFunctionType
AX = mybir.AxisListType
F32 = mybir.dt.float32
I32 = mybir.dt.int32
U32 = mybir.dt.uint32
ds = bass.ds

EPS_LN = 1e-5
PRIMED = 1


def early_fusion_kernel(nc, patches, wtok, idx, embs, wtxt, w_in, w_proj, b_beta, w_out,
                        gate_w, w_down, w_up, up_b, iota8, out):
    IG, _, FK, GT = patches.shape
    TXT_TILES = idx.shape[1]
    B, T, D = out.shape
    DK = D // P
    NS = w_out.shape[1 - 1] // 4
    NP = w_proj.shape[2]
    TG = GT // B
    NT = GT // P
    NG = T // TG
    TG_TXT = TXT_TILES // NT
    TILES = NG * NT
    HB = 2 * NS
    OPW = 3 * HB + NS
    QO, LO = 6 * HB, 6 * HB + NS
    E = up_b.shape[0]
    C = w_down.shape[3]
    ROWS = [e.shape[0] for e in embs]
    WID = [e.shape[1] for e in embs]
    COL = [sum(WID[:i]) for i in range(5)]
    XW = COL[4]
    LOW = [sum(ROWS[:i]) for i in range(4)]
    XK = [(0, P), (P, P), (2 * P, XW - 2 * P)]
    HS = NS * NS
    JQ = 8

    opnd = nc.dram_tensor("operands_dram", [T, 2, B, OPW], F32).ap()
    topi = nc.dram_tensor("top_index_dram", [B, 2], U32).ap()

    with ExitStack() as whole:
        def sb(ctx, name, shape, dt=F32):
            return ctx.enter_context(nc.sbuf_tensor(name, shape, dt))

        def sem(name):
            return whole.enter_context(nc.semaphore(name))

        ps = whole.enter_context(nc.psum_tensor("ps", [P, 8, 512], F32))
        H = sb(whole, "H", [P, TILES, D])
        scal = sb(whole, "scal", [P, T, 8])
        primed = {name: sem(name) for name in (
            "h_ps", "xnT_ps", "xcatT_ready", "p2_ps", "opb_ready", "p1_ps",
            "xpT_ready", "kss_ready", "p2_read_act", "p2_read_dve", "sq_ps", "sqq_ready",
            "state_ready", "xt_ps", "xt_read", "sum_ready",
            "opb_stored0", "opb_stored1")}
        with nc.Block() as block:
            @block.sync
            def _(sp):
                for s in primed.values():
                    sp.sem_inc(s, PRIMED)

        turns_dve, turns_pool = sem("turns_dve"), sem("turns_pool")
        ident = sb(whole, "ident", [P, P])
        fold = sb(whole, "fold", [P, B])
        sel = sb(whole, "sel", [P, 2, P])
        eps_t = sb(whole, "eps_t", [P, 1])

        with ExitStack() as ctx:
            patch_sb = sb(ctx, "patch_sb", [P, IG, FK, GT])
            wtok_sb = sb(ctx, "wtok_sb", [P, FK, D])
            wtxt_sb = sb(ctx, "wtxt_sb", [P, 3, D])
            win_sb = sb(ctx, "win_sb", [P, DK, D])
            wproj_sb = sb(ctx, "wproj_sb", [P, DK, NP])
            bb_sb = sb(ctx, "bb_sb", [P, 2, HB])
            idx_sb = sb(ctx, "idx_sb", [P, TXT_TILES], I32)
            idx_f = sb(ctx, "idx_f", [P, TXT_TILES])
            below = sb(ctx, "below", [P, TXT_TILES])
            rel = sb(ctx, "rel", [P, 4, TXT_TILES], I32)
            rel_g = sb(ctx, "rel_g", [P, 2, 4, NT], I32)
            xcat = sb(ctx, "xcat", [P, 2, NT, XW])
            xcatT = sb(ctx, "xcatT", [P, NT, 3, P])
            stats = sb(ctx, "stats", [P, NT, 6])
            mv = sb(ctx, "mv", [P, NT, 2])
            std = sb(ctx, "std", [P, NT])
            rstd = sb(ctx, "rstd", [P, NT])
            xn = sb(ctx, "xn", [P, NT, D])
            xnT = sb(ctx, "xnT", [P, DK, GT])
            sg = sb(ctx, "sg", [P, DK, GT])
            xpT = sb(ctx, "xpT", [P, DK, GT])
            beta_in = sb(ctx, "beta_in", [P, NT, 2, HB])
            ksq = sb(ctx, "ksq", [P, NT, 2, HB])
            opb = sb(ctx, "opb", [P, 2, NT, 2, OPW])
            router_lg = sb(ctx, "router_lg", [P, TILES, 4])
            kss = sb(ctx, "kss", [P, TILES, 4])
            mx = sb(ctx, "mx", [P, TILES])
            ex = sb(ctx, "ex", [P, TILES, 4])
            tot = sb(ctx, "tot", [P, TILES])
            rank = sb(ctx, "rank", [P, TILES, 4])
            cmp = sb(ctx, "cmp", [P, TILES])
            knorm = sb(ctx, "knorm", [P, TILES, 4])
            wide = sb(ctx, "wide", [P, TILES, 2, 8])

            H_PS = ps[:, 0:2, :].rearrange("p k (j d) -> p (k j) d", d=D)
            XNT_PS = ps[:, 4:4 + DK, :]
            P1_PS = ps[:, 6:6 + DK, :]
            P2_PS = ps[:, 4:4 + NT, :]

            weights_in, idx_in, patch_in = sem("weights_in"), sem("idx_in"), sem("patch_in")
            masks_step, masks_ready = sem("masks_step"), sem("masks_ready")
            idx_step, rel_ready = sem("idx_step"), sem("rel_ready")
            patch_h = sem("patch_h")
            xcat_clear, rel_staged = sem("xcat_clear"), sem("rel_staged")
            gathered = [sem(f"gathered{u}") for u in range(2)]
            xcatT_ps, xcatT_ready = sem("xcatT_ps"), primed["xcatT_ready"]
            h_ps, h_ready = primed["h_ps"], sem("h_ready")
            stats_ready, mv_ready, std_ready, rstd_ready = (sem("stats_ready"), sem("mv_ready"),
                                                            sem("std_ready"), sem("rstd_ready"))
            xn_ready, xnT_ps, xnT_ready = sem("xn_ready"), primed["xnT_ps"], sem("xnT_ready")
            p1_ps, sg_ready, xpT_ready = primed["p1_ps"], sem("sg_ready"), primed["xpT_ready"]
            p2_ps, p2_read_act, p2_read_dve = primed["p2_ps"], primed["p2_read_act"], primed["p2_read_dve"]
            ksq_ready, kss_ready, beta_in_ready = sem("ksq_ready"), primed["kss_ready"], sem("beta_in_ready")
            opb_ready = primed["opb_ready"]
            opb_stored = [primed[f"opb_stored{u}"] for u in range(2)]

            with nc.Block() as block:
                @block.sync
                def _(sp):
                    sp.dma_start(idx_sb[:], idx).then_inc(idx_in, 16)
                    for g in range(IG):
                        sp.dma_start(patch_sb[:, g], patches[g]).then_inc(patch_in, 16)
                    sp.dma_start(wtok_sb[:], wtok).then_inc(patch_in, 16)
                    for k, (c0, n) in enumerate(XK):
                        sp.dma_start(wtxt_sb[0:n, k, :], wtxt[c0:c0 + n, :]).then_inc(weights_in, 16)
                    sp.dma_start(win_sb[:], w_in).then_inc(weights_in, 16)
                    sp.dma_start(wproj_sb[:], w_proj).then_inc(weights_in, 16)
                    sp.dma_start(bb_sb[:], b_beta).then_inc(weights_in, 16)

                    def store(n, u):
                        sp.wait_ge(opb_ready, n + 1 + PRIMED)
                        for tp in range(2):
                            dst = opnd[ds(n * TG, TG)].rearrange("(j tp) h b f -> tp b j h f", tp=2)[tp]
                            for j in range(NT):
                                sp.dma_start(dst[:, j], opb[64 * tp:64 * tp + 64, u, j]).then_inc(opb_stored[u], 16)

                    with sp.Fori(0, NG // 2) as i:
                        for u in range(2):
                            store(i * 2 + u, u)
                    for u in range(2):
                        sp.wait_ge(opb_stored[u], 16 * 2 * NT * (NG // 2) + PRIMED)

                @block.gpsimd
                def _(pool):
                    nc.gpsimd.memset(ident[:], 0.0).then_inc(masks_step, 1)
                    nc.gpsimd.memset(fold[:], 0.0).then_inc(masks_step, 1)
                    nc.gpsimd.memset(sel[:], 0.0).then_inc(masks_step, 1)
                    nc.gpsimd.memset(eps_t[:], EPS_LN).then_inc(masks_ready, 1)
                    pool.wait_ge(masks_step, 3)
                    nc.gpsimd.affine_select(out=ident[:], in_=ident[:], compare_op=ALU.not_equal, fill=1.0,
                                            base=0, pattern=[[-1, P]], channel_multiplier=1).then_inc(masks_ready, 1)
                    nc.gpsimd.affine_select(out=fold[:], in_=fold[:], compare_op=ALU.not_equal, fill=1.0,
                                            base=0, pattern=[[-1, B]], channel_multiplier=1).then_inc(masks_step, 1)
                    pool.wait_ge(masks_step, 4)
                    nc.gpsimd.affine_select(out=fold[:], in_=fold[:], compare_op=ALU.not_equal, fill=1.0,
                                            base=-B, pattern=[[-1, B]], channel_multiplier=1).then_inc(masks_ready, 1)
                    for tp in range(2):
                        s = sel[:, tp, :].rearrange("p (h b) -> p h b", h=2)
                        nc.gpsimd.affine_select(out=s, in_=s, compare_op=ALU.not_equal, fill=1.0, base=-64 * tp,
                                                pattern=[[0, 2], [-1, B]], channel_multiplier=1).then_inc(masks_ready, 1)

                    def gather(n, u, reused):
                        if reused:
                            pool.wait_ge(h_ps, n - 1 + PRIMED)
                            pool.sem_inc(turns_pool, 1)
                        nc.gpsimd.memset(xcat[:, u], 0.0).then_inc(xcat_clear, 1)
                        nc.gpsimd.tensor_copy(rel_g[:, u], rel[:, :, ds(n * NT, NT)]).then_inc(rel_staged, 1)
                        pool.wait_ge(xcat_clear, n + 1)
                        pool.wait_ge(rel_staged, n + 1)
                        pool.sem_inc(turns_pool, 1)
                        for j in range(NT):
                            for t in range(4):
                                nc.gpsimd.indirect_dma_start(
                                    xcat[:, u, j, COL[t]:COL[t + 1]], None, embs[t],
                                    bass.IndirectOffsetOnAxis(ap=rel_g[:, u, t, j:j + 1], axis=0),
                                    bounds_check=ROWS[t] - 1, oob_is_err=False).then_inc(gathered[u], 16)

                    pool.wait_ge(rel_ready, 4)
                    for u in range(2):
                        gather(u, u, False)
                    with pool.Fori(1, TG_TXT // 2) as i:
                        for u in range(2):
                            gather(i * 2 + u, u, True)

                @block.vector
                def _(dve):
                    dve.wait_ge(idx_in, 16)
                    nc.vector.tensor_copy(idx_f[:], idx_sb[:]).then_inc(idx_step, 1)
                    dve.wait_ge(idx_step, 1)
                    for t in range(4):
                        nc.vector.tensor_scalar(below[:], idx_f[:], float(LOW[t]), float(1 << 22),
                                                ALU.is_lt, ALU.mult).then_inc(idx_step, 1)
                        dve.wait_ge(idx_step, 2 + t)
                        nc.vector.scalar_tensor_tensor(rel[:, t, :], idx_f[:], float(LOW[t]), below[:],
                                                       ALU.subtract, ALU.add).then_inc(rel_ready, 1)
                        dve.wait_ge(rel_ready, t + 1)

                    def norm_stats(n):
                        dve.wait_ge(h_ready, n + 1)
                        dve.wait_ge(xn_ready, n)
                        dve.sem_inc(turns_dve, 1)
                        for j in range(NT):
                            nc.vector.bn_stats(stats[:, j, :], H[:, ds(n * NT + j, 1), :].rearrange(
                                "p o d -> p (o d)")).then_inc(stats_ready, 1)
                        dve.wait_ge(stats_ready, n * NT + NT)
                        dve.sem_inc(turns_dve, 1)
                        for j in range(NT):
                            ins = nc.vector.bn_aggr(mv[:, j, :], stats[:, j, :])
                        ins.then_inc(mv_ready, 1)

                    def norm_apply(n):
                        dve.wait_ge(std_ready, n + 1)
                        nc.vector.reciprocal(rstd[:], std[:]).then_inc(rstd_ready, 1)
                        dve.wait_ge(rstd_ready, n + 1)
                        dve.wait_ge(xnT_ps, n + PRIMED)
                        for j in range(NT):
                            ins = nc.vector.tensor_scalar(
                                xn[:, j, :], H[:, ds(n * NT + j, 1), :].rearrange("p o d -> p (o d)"),
                                mv[:, j, 0:1], rstd[:, j:j + 1], ALU.subtract, ALU.mult)
                        ins.then_inc(xn_ready, 1)

                    def text_evacuate(n, j):
                        dve.wait_ge(xcatT_ps, n * NT + j + 1)
                        dve.wait_ge(h_ps, n + PRIMED)
                        nc.vector.tensor_copy(xcatT[:, j, 0:2, :], ps[:, 2 + j % 2, 0:2 * P].rearrange(
                            "p (k c) -> p k c", k=2))
                        nc.vector.tensor_copy(xcatT[0:XK[2][1], j, 2, :],
                                              ps[0:XK[2][1], 2 + j % 2, 2 * P:3 * P]).then_inc(xcatT_ready, 1)

                    def group(n, text, last):
                        if not last:
                            norm_stats(n + 1)
                        if text:
                            text_evacuate(n, 0)
                            text_evacuate(n, 1)
                        dve.wait_ge(sg_ready, n + 1)
                        dve.wait_ge(p2_ps, n + PRIMED)
                        nc.vector.tensor_tensor(xpT[:], P1_PS, sg[:], ALU.mult).then_inc(xpT_ready, 1)
                        if text:
                            text_evacuate(n, 2)
                            text_evacuate(n, 3)
                        dve.wait_ge(p2_read_act, n + 1 + PRIMED)
                        dve.wait_ge(opb_ready, n + PRIMED)
                        for h in range(2):
                            c0 = (3 * h + 2) * HB
                            nc.vector.tensor_tensor(
                                beta_in[:, :, h, :], P2_PS[:, :, c0:c0 + HB],
                                bb_sb[:, h, :].unsqueeze(1).to_broadcast([P, NT, HB]),
                                ALU.add).then_inc(beta_in_ready, 1)
                        nc.vector.tensor_copy(router_lg[:, ds(n * NT, NT), :],
                                              P2_PS[:, :, LO:LO + 4]).then_inc(p2_read_dve, 1)
                        dve.wait_ge(ksq_ready, 2 * n + 2)
                        nc.vector.tensor_reduce(
                            kss[:, ds(n * NT, NT), :].rearrange("p j n -> p (j n)"),
                            ksq[:].rearrange("p j h (n i) -> p (j h n) i", n=2), AX.X,
                            ALU.add).then_inc(kss_ready, 1)
                        if not last:
                            norm_apply(n + 1)

                    norm_stats(0)
                    norm_apply(0)
                    with dve.Fori(0, TG_TXT) as n:
                        group(n, True, False)
                    for n in range(TG_TXT, NG):
                        group(n, False, n == NG - 1)

                @block.scalar
                def _(act):
                    for g in range(IG):
                        act.wait_ge(patch_h, g + 1)
                        nc.scalar.activation(
                            H[:, g * NT:(g + 1) * NT, :],
                            ps[:, 2 * g:2 * g + 2, :].rearrange("p k (j d) -> p (k j) d", d=D),
                            ACT.Copy).then_inc(h_ready, 1)

                    def norm_std(n):
                        act.wait_ge(mv_ready, n + 1)
                        nc.scalar.activation(std[:], mv[:, :, 1], ACT.Sqrt, bias=eps_t[:]).then_inc(std_ready, 1)

                    def group(n, u, text, last):
                        act.wait_ge(xnT_ps, n + 1 + PRIMED)
                        act.wait_ge(p1_ps, n + PRIMED)
                        nc.scalar.activation(xnT[:], XNT_PS, ACT.Copy).then_inc(xnT_ready, 1)
                        if not last:
                            norm_std(n + 1)
                        act.wait_ge(p1_ps, n + 1 + PRIMED)
                        act.wait_ge(xpT_ready, n + PRIMED)
                        nc.scalar.activation(sg[:], P1_PS, ACT.Sigmoid).then_inc(sg_ready, 1)
                        act.wait_ge(p2_ps, n + 1 + PRIMED)
                        act.wait_ge(kss_ready, n + PRIMED)
                        for h in range(2):
                            nc.scalar.activation(ksq[:, :, h, :], P2_PS[:, :, 3 * h * HB:3 * h * HB + HB],
                                                 ACT.Square).then_inc(ksq_ready, 1)
                        act.wait_ge(opb_stored[u], (n - u) * (16 * NT) + PRIMED)
                        for h in range(2):
                            nc.scalar.activation(opb[:, u, :, h, 0:2 * HB],
                                                 P2_PS[:, :, 3 * h * HB:3 * h * HB + 2 * HB], ACT.Copy)
                        for h in range(2):
                            ins = nc.scalar.activation(opb[:, u, :, h, 3 * HB:OPW], P2_PS[:, :, QO:QO + NS], ACT.Copy)
                        ins.then_inc(p2_read_act, 1)
                        act.wait_ge(beta_in_ready, 2 * n + 2)
                        nc.scalar.activation(
                            opb[:, u, :, :, 2 * HB:3 * HB].rearrange("p j h f -> p (j h) f"),
                            beta_in[:].rearrange("p j h f -> p (j h) f"), ACT.Sigmoid).then_inc(opb_ready, 1)
                        if text:
                            act.wait_ge(h_ps, n + 1 + PRIMED)
                            nc.scalar.activation(H[:, ds((n + IG) * NT, NT), :], H_PS, ACT.Copy).then_inc(h_ready, 1)

                    act.wait_ge(masks_ready, 5)
                    norm_std(0)
                    with act.Fori(0, TG_TXT // 2) as i:
                        for u in range(2):
                            group(i * 2 + u, u, True, False)
                    for n in range(TG_TXT, NG):
                        group(n, n % 2, False, n == NG - 1)

                @block.tensor
                def _(pe):
                    pe.wait_ge(patch_in, 16 * (IG + 1))
                    for g in range(IG):
                        for j in range(NT):
                            for k in range(FK):
                                mm = nc.tensor.matmul(ps[:, 2 * g + j // 2, (j % 2) * D:(j % 2) * D + D],
                                                      patch_sb[:, g, k, j * P:(j + 1) * P], wtok_sb[:, k, :],
                                                      start=(k == 0), stop=(k == FK - 1))
                        mm.then_inc(patch_h, 1)
                    pe.wait_ge(masks_ready, 5)
                    pe.wait_ge(weights_in, 16 * (len(XK) + 3))
                    pe.wait_ge(h_ready, IG)

                    def text_transpose(n, j, u):
                        pe.wait_ge(xcatT_ready, n * NT + max(j - 1, 0) + PRIMED)
                        for k, (c0, w) in enumerate(XK):
                            mm = nc.tensor.transpose(ps[0:w, 2 + j % 2, k * P:(k + 1) * P],
                                                     xcat[:, u, j, c0:c0 + w], ident[:])
                        mm.then_inc(xcatT_ps, 1)

                    def text_product(n, j):
                        pe.wait_ge(xcatT_ready, n * NT + j + 1 + PRIMED)
                        for k, (c0, w) in enumerate(XK):
                            mm = nc.tensor.matmul(ps[:, j // 2, (j % 2) * D:(j % 2) * D + D],
                                                  xcatT[0:w, j, k, :], wtxt_sb[0:w, k, :],
                                                  start=(k == 0), stop=(k == len(XK) - 1))
                        return mm

                    def group(n, u, text):
                        pe.wait_ge(xn_ready, n + 1)
                        pe.wait_ge(p2_read_act, n + PRIMED)
                        pe.wait_ge(p2_read_dve, n + PRIMED)
                        for j in range(NT):
                            for k in range(DK):
                                mm = nc.tensor.transpose(ps[:, 4 + k, j * P:(j + 1) * P],
                                                         xn[:, j, k * P:(k + 1) * P], ident[:])
                        mm.then_inc(xnT_ps, 1)
                        if text:
                            pe.wait_ge(gathered[u], (n - u + 2) * (16 * NT * 4 // 2))
                            text_transpose(n, 0, u)
                            text_transpose(n, 1, u)
                        pe.wait_ge(xnT_ready, n + 1)
                        for m in range(DK):
                            for k in range(DK):
                                mm = nc.tensor.matmul(ps[:, 6 + m, :], win_sb[:, k, m * P:(m + 1) * P],
                                                      xnT[:, k, :], start=(k == 0), stop=(k == DK - 1))
                        mm.then_inc(p1_ps, 1)
                        if text:
                            pe.wait_ge(h_ready, n + IG)
                            text_transpose(n, 2, u)
                            text_transpose(n, 3, u)
                            text_product(n, 0)
                            text_product(n, 1)
                        pe.wait_ge(xpT_ready, n + 1 + PRIMED)
                        for j in range(NT):
                            for k in range(DK):
                                mm = nc.tensor.matmul(ps[:, 4 + j, 0:NP], xpT[:, k, j * P:(j + 1) * P],
                                                      wproj_sb[:, k, :], start=(k == 0), stop=(k == DK - 1))
                        mm.then_inc(p2_ps, 1)
                        if text:
                            text_product(n, 2)
                            text_product(n, 3).then_inc(h_ps, 1)

                    with pe.Fori(0, TG_TXT // 2) as i:
                        for u in range(2):
                            group(i * 2 + u, u, True)
                    for n in range(TG_TXT, NG):
                        group(n, n % 2, False)

            router_step, wide_ready, wide_moved = sem("router_step"), sem("wide_ready"), sem("wide_moved")
            logits_centred, exp_ready, knorm_ready = sem("logits_centred"), sem("exp_ready"), sem("knorm_ready")
            CT = TILES // 3
            with nc.Block() as block:
                @block.scalar
                def _(act):
                    nc.scalar.activation(knorm[:], kss[:], ACT.Sqrt).then_inc(knorm_ready, 1)
                    act.wait_ge(logits_centred, 1)
                    nc.scalar.activation(ex[:], ex[:], ACT.Exp).then_inc(exp_ready, 1)

                @block.vector
                def _(dve):
                    steps = [0]

                    def link(ins):
                        steps[0] += 1
                        ins.then_inc(router_step, 1)
                        dve.wait_ge(router_step, steps[0])

                    def per_tile(a):
                        return a.unsqueeze(2).to_broadcast([P, TILES, 4])

                    def halves(c):
                        return wide[:].rearrange("p t h f -> p (t h) f")[:, :, c:c + 2]

                    def pairs(a):
                        return a[:].rearrange("p t (h n) -> p (t h) n", h=2)

                    link(nc.vector.tensor_reduce(mx[:], router_lg[:], AX.X, ALU.max))
                    nc.vector.tensor_tensor(ex[:], router_lg[:], per_tile(mx[:]),
                                            ALU.subtract).then_inc(logits_centred, 1)
                    link(nc.vector.memset(rank[:], 0.0))
                    for m in range(4):
                        for n in range(m + 1, 4):
                            link(nc.vector.tensor_tensor(cmp[:], router_lg[:, :, m], router_lg[:, :, n], ALU.is_ge))
                            link(nc.vector.tensor_tensor(rank[:, :, n], rank[:, :, n], cmp[:], ALU.add))
                            link(nc.vector.scalar_tensor_tensor(rank[:, :, m], rank[:, :, m], 1.0, cmp[:],
                                                                ALU.add, ALU.subtract))
                    link(nc.vector.tensor_scalar(rank[:], rank[:], 2.0, None, ALU.is_lt))
                    dve.wait_ge(exp_ready, 1)
                    link(nc.vector.tensor_reduce(tot[:], ex[:], AX.X, ALU.add))
                    link(nc.vector.reciprocal(tot[:], tot[:]))
                    link(nc.vector.tensor_tensor(ex[:], ex[:], per_tile(tot[:]), ALU.mult))
                    link(nc.vector.tensor_copy(halves(4), pairs(ex)))
                    link(nc.vector.tensor_tensor(ex[:], ex[:], rank[:], ALU.mult))
                    link(nc.vector.tensor_reduce(tot[:], ex[:], AX.X, ALU.add))
                    link(nc.vector.tensor_scalar(tot[:], tot[:], 1e-8, None, ALU.add))
                    link(nc.vector.reciprocal(tot[:], tot[:]))
                    link(nc.vector.tensor_tensor(ex[:], ex[:], per_tile(tot[:]), ALU.mult))
                    link(nc.vector.tensor_copy(halves(0), pairs(ex)))
                    link(nc.vector.tensor_scalar(halves(2), pairs(ex), -1.0, 1.0, ALU.mult, ALU.add))
                    dve.wait_ge(knorm_ready, 1)
                    link(nc.vector.tensor_scalar(knorm[:], knorm[:], 1e-6, None, ALU.add))
                    link(nc.vector.reciprocal(knorm[:], knorm[:]))
                    nc.vector.tensor_copy(halves(6), pairs(knorm)).then_inc(wide_ready, 1)
                    dve.wait_ge(wide_moved, 1)
                    for tp in range(2):
                        for c in range(3):
                            for h in range(2):
                                src = ps[64 * h:64 * h + 64, 3 * tp + c, 0:16 * CT].rearrange(
                                    "p (t h f) -> p t h f", h=2, f=8)[:, :, h, :]
                                dst = scal[64 * h:64 * h + 64, :, :].rearrange("p (t tp) f -> p t tp f", tp=2)[
                                    :, c * CT:(c + 1) * CT, tp, :]
                                nc.vector.tensor_copy(dst, src)

                @block.tensor
                def _(pe):
                    pe.wait_ge(wide_ready, 1)
                    for tp in range(2):
                        for c in range(3):
                            mm = nc.tensor.matmul(ps[:, 3 * tp + c, 0:16 * CT], sel[:, tp, :],
                                                  wide[:, c * CT:(c + 1) * CT].rearrange("p t h f -> p (t h f)"),
                                                  start=True, stop=True)
                    mm.then_inc(wide_moved, 1)

        after = whole.enter_context(ExitStack())
        sq = sb(after, "sq", [P, T + 2, HB])
        with ExitStack() as ctx:
            S = sb(ctx, "S", [P, 2, 2, HS])
            sk = sb(ctx, "sk", [P, 2, HS])
            outer = sb(ctx, "outer", [P, 2, HS])
            bS = sb(ctx, "bS", [P, 2, HS])
            upd = sb(ctx, "upd", [P, 2, HS])
            keep = sb(ctx, "keep", [P, 2, HS])
            sqq = sb(ctx, "sqq", [P, 2, HS])
            op = sb(ctx, "op", [P, 4, OPW])
            kn = sb(ctx, "kn", [P, 2, HB])
            nret = sb(ctx, "nret", [P, 2, NS])
            delta = sb(ctx, "delta", [P, 2, NS])

            op_in = [sem(f"op_in{s}") for s in range(4)]
            junk_ready, kn_ready, state_ready = sem("junk_ready"), sem("kn_ready"), primed["state_ready"]
            sk_ready, ret_ps, nret_ready, delta_ready = (sem("sk_ready"), sem("ret_ps"), sem("nret_ready"),
                                                         sem("delta_ready"))
            outer_ready, bS_ready, arg_ready = sem("outer_ready"), sem("bS_ready"), sem("arg_ready")
            upd_ready, keep_ready = sem("upd_ready"), sem("keep_ready")
            sqq_ready, sq_ps, sq_ready = primed["sqq_ready"], primed["sq_ps"], sem("sq_ready")


            def mat(a):
                return a.rearrange("p (i j) -> p i j", j=NS)

            def along_i(a):
                return a.unsqueeze(1).to_broadcast([P, NS, NS])

            def along_j(a):
                return a.unsqueeze(2).to_broadcast([P, NS, NS])

            def step_scalar(t, c):
                return scal[:, ds(t, 1), c:c + 1].rearrange("p o f -> p (o f)")

            with nc.Block() as block:
                @block.sync
                def _(sp):
                    def load(t, s):
                        sp.dma_start(op[:, s, :], opnd[ds(t, 1)].rearrange("o h b f -> (o h b) f")).then_inc(op_in[s], 16)

                    for t in range(3):
                        load(t, t)
                    with sp.Fori(0, T // 4 - 1) as i:
                        for u in range(4):
                            sp.wait_ge(sqq_ready, i * 8 + (2 * u + 2) + PRIMED)
                            load(i * 4 + (u + 3), (u + 3) % 4)
                    sp.wait_ge(sqq_ready, 2 * (T - 4) + 2 + PRIMED)
                    load(T - 1, 3)

                @block.gpsimd
                def _(pool):
                    def q_product(t, u, q_slot):
                        for m in range(2):
                            pool.wait_ge(state_ready, t * 2 + (m + 1) + PRIMED)
                            pool.wait_ge(sq_ps, t * 2 + PRIMED)
                            nc.gpsimd.tensor_tensor(mat(sqq[:, m]), mat(S[:, u % 2, m]),
                                                    along_i(op[:, q_slot, 3 * HB:OPW]),
                                                    ALU.mult).then_inc(sqq_ready, 1)

                    nc.gpsimd.memset(op[:, 3], 0.0).then_inc(junk_ready, 1)
                    pool.wait_ge(junk_ready, 1)
                    with pool.Fori(0, T // 4) as i:
                        for u in range(4):
                            t = i * 4 + u
                            pool.wait_ge(op_in[u], i * 16 + 16)
                            pool.wait_ge(state_ready, t * 2 + PRIMED)
                            nc.gpsimd.tensor_tensor(
                                kn[:, u % 2].rearrange("p (n j) -> p n j", n=2),
                                op[:, u, 0:HB].rearrange("p (n j) -> p n j", n=2),
                                scal[:, ds(t, 1), 6:8].rearrange("p o f -> p (o f)").unsqueeze(2).to_broadcast(
                                    [P, 2, NS]), ALU.mult).then_inc(kn_ready, 1)
                            for m in range(2):
                                pool.wait_ge(state_ready, t * 2 + (m + 1) + PRIMED)
                                nc.gpsimd.tensor_tensor(
                                    mat(bS[:, m]), mat(S[:, u % 2, m]),
                                    along_j(op[:, u, 2 * HB + m * NS:2 * HB + (m + 1) * NS]),
                                    ALU.mult).then_inc(bS_ready, 1)
                            q_product(t, u, (u + 3) % 4)
                    q_product(T, T, 3)

                @block.scalar
                def _(act):
                    with act.Fori(0, T // 2) as i:
                        for u in range(2):
                            t = i * 2 + u
                            for m in range(2):
                                act.wait_ge(state_ready, t * 2 + (m + 1) + PRIMED)
                                nc.scalar.activation(keep[:, m], S[:, u, m], ACT.Copy,
                                                     scale=step_scalar(t, 2 + m)).then_inc(keep_ready, 1)
                            for m in range(2):
                                act.wait_ge(arg_ready, t * 2 + (m + 1))
                                nc.scalar.activation(upd[:, m], outer[:, m], ACT.Tanh).then_inc(upd_ready, 1)

                @block.tensor
                def _(pe):
                    def row_sums(dst, src):
                        for c in range(NS // JQ):
                            mm = nc.tensor.matmul(dst, ident[:], mat(src)[:, :, c * JQ:(c + 1) * JQ],
                                                  start=(c == 0), stop=(c == NS // JQ - 1))
                        return mm

                    def q_sums(t):
                        for m in range(2):
                            pe.wait_ge(sqq_ready, t * 2 + (m + 1) + PRIMED)
                            pe.wait_ge(sq_ready, t * 2 + (m + 1))
                            row_sums(ps[:, 2 + m, 0:NS * JQ], sqq[:, m]).then_inc(sq_ps, 1)

                    with pe.Fori(0, T) as t:
                        for m in range(2):
                            pe.wait_ge(sk_ready, t * 2 + (m + 1))
                            row_sums(ps[:, m, 0:NS * JQ], sk[:, m]).then_inc(ret_ps, 1)
                        q_sums(t)
                    q_sums(T)

                @block.vector
                def _(dve):
                    def partial(b):
                        return ps[:, b, 0:NS * JQ].rearrange("p (i j) -> p i j", j=JQ)

                    def q_reduce(t):
                        dve.wait_ge(sq_ps, t * 2 + PRIMED)
                        for m in range(2):
                            nc.vector.tensor_reduce(
                                sq[:, ds(t, 1), m * NS:(m + 1) * NS].rearrange("p o f -> p (o f)"),
                                partial(2 + m), AX.X, ALU.add).then_inc(sq_ready, 1)

                    for m in range(2):
                        nc.vector.memset(ps[:, 2 + m, 0:NS * JQ], 0.0)
                        nc.vector.memset(S[:, 0, m], 0.0).then_inc(state_ready, 1)
                    with dve.Fori(0, T // 4) as i:
                        for u in range(4):
                            t = i * 4 + u
                            dve.wait_ge(kn_ready, t + 1)
                            for m in range(2):
                                dve.wait_ge(state_ready, t * 2 + (m + 1) + PRIMED)
                                nc.vector.tensor_tensor(mat(sk[:, m]), mat(S[:, u % 2, m]),
                                                        along_i(kn[:, u % 2, m * NS:(m + 1) * NS]),
                                                        ALU.mult).then_inc(sk_ready, 1)
                            q_reduce(t)
                            for m in range(2):
                                dve.wait_ge(ret_ps, t * 2 + (m + 1))
                                nc.vector.tensor_reduce(nret[:, m], partial(m), AX.X, ALU.add,
                                                        negate=True).then_inc(nret_ready, 1)
                                dve.wait_ge(nret_ready, t * 2 + (m + 1))
                                nc.vector.tensor_tensor(delta[:, m], nret[:, m],
                                                        op[:, u, HB + m * NS:HB + (m + 1) * NS],
                                                        ALU.add).then_inc(delta_ready, 1)
                                dve.wait_ge(delta_ready, t * 2 + (m + 1))
                                nc.vector.tensor_tensor(mat(outer[:, m]), along_j(delta[:, m]),
                                                        along_i(kn[:, u % 2, m * NS:(m + 1) * NS]),
                                                        ALU.mult).then_inc(outer_ready, 1)
                                dve.wait_ge(outer_ready, t * 2 + (m + 1))
                                dve.wait_ge(bS_ready, t * 2 + (m + 1))
                                nc.vector.tensor_tensor(outer[:, m], outer[:, m], bS[:, m],
                                                        ALU.add).then_inc(arg_ready, 1)
                            dve.wait_ge(sqq_ready, t * 2 + PRIMED)
                            for m in range(2):
                                dve.wait_ge(keep_ready, t * 2 + (m + 1))
                                dve.wait_ge(upd_ready, t * 2 + (m + 1))
                                nc.vector.scalar_tensor_tensor(
                                    S[:, (u + 1) % 2, m], upd[:, m], step_scalar(t, m), keep[:, m],
                                    ALU.mult, ALU.add).then_inc(state_ready, 1)
                    q_reduce(T)
                    q_reduce(T + 1)

        XT = sb(after, "XT", [P, DK, B, T])
        with ExitStack() as ctx:
            wout_sb = sb(ctx, "wout_sb", [P, D])
            z = sb(ctx, "z", [P, TG, HB])
            zsum = sb(ctx, "zsum", [P, TG, NS])
            zT = sb(ctx, "zT", [P, 2, B])
            stats = sb(ctx, "stats_m", [P, NT, 6])
            mv = sb(ctx, "mv_m", [P, NT, 2])
            std = sb(ctx, "std_m", [P, NT])
            rstd = sb(ctx, "rstd_m", [P, NT])
            xn = sb(ctx, "xn_m", [P, NT, D])

            wout_in, sig_ready, z_step, zsum_ready = sem("wout_in"), sem("sig_ready"), sem("z_step"), sem("zsum_ready")
            zT_ps, zT_ready, y_ps, h2_ready = sem("zT_ps"), sem("zT_ready"), sem("y_ps"), sem("h2_ready")
            stats2, mv2, std2, rstd2, xn2 = sem("stats2"), sem("mv2"), sem("std2"), sem("rstd2"), sem("xn2")
            xt_ps, xt_read = primed["xt_ps"], primed["xt_read"]

            with nc.Block() as block:
                @block.sync
                def _(sp):
                    sp.dma_start(wout_sb[:], w_out).then_inc(wout_in, 16)

                @block.scalar
                def _(act):
                    def gate(g):
                        act.wait_ge(zsum_ready, g)
                        nc.scalar.activation(z[:], sq[:, ds(g * TG + 2, TG), :], ACT.Sigmoid).then_inc(sig_ready, 1)

                    def fold_out(g):
                        act.wait_ge(zT_ps, g + 1)
                        act.wait_ge(y_ps, g)
                        nc.scalar.activation(zT[:], ps[:, 0, 0:2 * B].rearrange("p (c b) -> p c b", c=2),
                                             ACT.Copy).then_inc(zT_ready, 1)

                    def finish(g):
                        act.wait_ge(mv2, g + 1)
                        nc.scalar.activation(std[:], mv[:, :, 1], ACT.Sqrt, bias=eps_t[:]).then_inc(std2, 1)
                        act.wait_ge(xt_ps, g + 1 + PRIMED)
                        for k in range(DK):
                            nc.scalar.activation(XT[:, k, :, ds(g * TG, TG)].rearrange("p b t -> p t b"),
                                                 ps[:, 4 + k, :].rearrange("p (t b) -> p t b", b=B),
                                                 ACT.Copy).then_inc(xt_read, 1)

                    gate(0)
                    fold_out(0)
                    with act.Fori(1, NG) as g:
                        gate(g)
                        fold_out(g)
                        finish(g - 1)
                    finish(NG - 1)

                @block.vector
                def _(dve):
                    def block_out(g):
                        s = sq[:, ds(g * TG + 2, TG), :]
                        dve.wait_ge(sig_ready, g + 1)
                        nc.vector.tensor_tensor(z[:], z[:], s, ALU.mult).then_inc(z_step, 1)
                        dve.wait_ge(z_step, g * 3 + 1)
                        nc.vector.tensor_tensor(z[:], z[:], s, ALU.mult).then_inc(z_step, 1)
                        dve.wait_ge(z_step, g * 3 + 2)
                        z4 = z[:].rearrange("p t (n i) -> p t n i", n=2)
                        nc.vector.tensor_tensor(z4, z4, scal[:, ds(g * TG, TG), 4:6].unsqueeze(3).to_broadcast(
                            [P, TG, 2, NS]), ALU.mult).then_inc(z_step, 1)
                        dve.wait_ge(z_step, g * 3 + 3)
                        dve.wait_ge(zT_ps, g)
                        nc.vector.tensor_tensor(zsum[:], z[:, :, 0:NS], z[:, :, NS:HB], ALU.add).then_inc(zsum_ready, 1)

                    def finish(g):
                        hg = H[:, ds(g * NT, NT), :].rearrange("p (q k) d -> p q k d", k=2)
                        dve.wait_ge(y_ps, g + 1)
                        nc.vector.tensor_tensor(hg, hg, ps[:, 2:4, :].rearrange("p k (q d) -> p q k d", d=D),
                                                ALU.add).then_inc(h2_ready, 1)
                        dve.wait_ge(h2_ready, g + 1)
                        dve.sem_inc(turns_dve, 1)
                        for j in range(NT):
                            ins = nc.vector.bn_stats(stats[:, j, :], H[:, ds(g * NT + j, 1), :].rearrange(
                                "p o d -> p (o d)"))
                        ins.then_inc(stats2, 1)
                        dve.wait_ge(stats2, g + 1)
                        dve.sem_inc(turns_dve, 1)
                        for j in range(NT):
                            ins = nc.vector.bn_aggr(mv[:, j, :], stats[:, j, :])
                        ins.then_inc(mv2, 1)
                        dve.wait_ge(mv2, g + 1)
                        dve.wait_ge(std2, g + 1)
                        nc.vector.reciprocal(rstd[:], std[:]).then_inc(rstd2, 1)
                        dve.wait_ge(rstd2, g + 1)
                        dve.wait_ge(xt_ps, g + PRIMED)
                        for j in range(NT):
                            ins = nc.vector.tensor_scalar(
                                xn[:, j, :], H[:, ds(g * NT + j, 1), :].rearrange("p o d -> p (o d)"),
                                mv[:, j, 0:1], rstd[:, j:j + 1], ALU.subtract, ALU.mult)
                        ins.then_inc(xn2, 1)

                    block_out(0)
                    with dve.Fori(1, NG) as g:
                        block_out(g)
                        finish(g - 1)
                    finish(NG - 1)

                @block.tensor
                def _(pe):
                    def mix(g):
                        pe.wait_ge(zsum_ready, g + 1)
                        pe.wait_ge(zT_ready, g)
                        for c in range(2):
                            mm = nc.tensor.matmul(ps[:, 0, c * B:(c + 1) * B],
                                                  zsum[:, 4 * c:4 * c + 4, :].rearrange("p t i -> p (t i)"),
                                                  fold[:], start=True, stop=True)
                        mm.then_inc(zT_ps, 1)
                        pe.wait_ge(zT_ready, g + 1)
                        pe.wait_ge(h2_ready, g)
                        for t in range(TG):
                            r, j, tp = t % 4, t // 2, t % 2
                            mm = nc.tensor.matmul(
                                ps[B * tp:B * tp + B, 2 + j % 2, (j // 2) * D:(j // 2) * D + D],
                                zT[NS * r:NS * r + NS, t // 4, :], wout_sb[NS * r:NS * r + NS, :],
                                start=True, stop=True)
                        mm.then_inc(y_ps, 1)

                    def turn(g):
                        pe.wait_ge(xn2, g + 1)
                        pe.wait_ge(xt_read, g * DK + PRIMED)
                        for j in range(NT):
                            for k in range(DK):
                                mm = nc.tensor.transpose(ps[:, 4 + k, j * P:(j + 1) * P],
                                                         xn[:, j, k * P:(k + 1) * P], ident[:])
                        mm.then_inc(xt_ps, 1)

                    pe.wait_ge(wout_in, 16)
                    mix(0)
                    with pe.Fori(1, NG) as g:
                        mix(g)
                        turn(g - 1)
                    turn(NG - 1)

        with ExitStack() as ctx:
            spare = sq[:].rearrange("p t f -> p (t f)")
            used = [0]

            def reuse(pattern, *shape):
                n = 1
                for k in shape:
                    n *= k
                at = used[0]
                used[0] += n
                a = spare[:, at:at + n]
                names = pattern.split()
                return a.rearrange(f"p ({pattern}) -> p {pattern}", **dict(zip(names, shape))) if len(names) > 1 else a

            wd_sb = reuse("e k c", E, DK, C)
            wu_sb = reuse("e d", E, D + 1)
            upb_sb = sb(ctx, "upb_sb", [E, D])
            gw_sb = sb(ctx, "gw_sb", [P, DK, E])
            iota_sb = sb(ctx, "iota_sb", [B, E])
            pooled = sb(ctx, "pooled", [P, DK, B])
            glog = sb(ctx, "glog", [B, E])
            top8 = sb(ctx, "top8", [B, 8])
            topx = sb(ctx, "topx", [B, 8], U32)
            topf = sb(ctx, "topf", [B, 2])
            nmax = sb(ctx, "nmax", [B, 1])
            gex = sb(ctx, "gex", [B, E])
            gsum = sb(ctx, "gsum", [B, 1])
            tex = sb(ctx, "tex", [B, 2])
            tsum = sb(ctx, "tsum", [B, 1])
            tw_rep = sb(ctx, "tw_rep", [B, 2, C])
            dense = sb(ctx, "dense", [B, 2, E])
            denseT = sb(ctx, "denseT", [E, B])
            twcol = sb(ctx, "twcol", [P, B])
            ubT = sb(ctx, "ubT", [P, DK, B])
            idx_row = sb(ctx, "idx_row", [1, 2 * B], U32)

            gate_in, pooled_ready, glog_ps, gate_step = (sem("gate_in"), sem("pooled_ready"), sem("glog_ps"),
                                                         sem("gate_step"))
            nmax_ready, gate_exp, topx_ready, topi_out, idx_row_in = (sem("nmax_ready"), sem("gate_exp"),
                                                                     sem("topx_ready"), sem("topi_out"),
                                                                     sem("idx_row_in"))
            dense_ready, dense_ps, denseT_ready, cols_ps = (sem("dense_ready"), sem("dense_ps"),
                                                            sem("denseT_ready"), sem("cols_ps"))
            with nc.Block() as block:
                @block.sync
                def _(sp):
                    for dst, src in ((wd_sb, w_down), (wu_sb, w_up), (upb_sb[:], up_b), (gw_sb[:], gate_w), (iota_sb[:], iota8)):
                        sp.dma_start(dst, src).then_inc(gate_in, 16)
                    sp.wait_ge(topx_ready, 1)
                    sp.dma_start(topi, topx[:, 0:2]).then_inc(topi_out, 16)
                    sp.wait_ge(topi_out, 16)
                    sp.dma_start(idx_row[:], topi.rearrange("b k -> (b k)").unsqueeze(0)).then_inc(idx_row_in, 16)
                    sp.wait_ge(idx_row_in, 16)

                @block.scalar
                def _(act):
                    act.wait_ge(nmax_ready, 1)
                    nc.scalar.activation(gex[:], glog[:], ACT.Exp, bias=nmax[:]).then_inc(gate_exp, 1)
                    nc.scalar.activation(tex[:], top8[:, 0:2], ACT.Exp, bias=nmax[:]).then_inc(gate_exp, 1)

                @block.tensor
                def _(pe):
                    pe.wait_ge(gate_in, 16 * 5)
                    pe.wait_ge(pooled_ready, 1)
                    for k in range(DK):
                        mm = nc.tensor.matmul(ps[0:B, 0, 0:E], pooled[:, k, :], gw_sb[:, k, :],
                                              start=(k == 0), stop=(k == DK - 1))
                    mm.then_inc(glog_ps, 1)
                    pe.wait_ge(dense_ready, 1)
                    nc.tensor.transpose(ps[0:E, 1, 0:B], dense[:, 0, :], ident[0:B, 0:B]).then_inc(dense_ps, 1)
                    nc.tensor.matmul(ps[:, 2, 0:B], tw_rep[:].rearrange("p k c -> p (k c)"), ident[0:B, 0:B],
                                     start=True, stop=True)
                    pe.wait_ge(denseT_ready, 1)
                    for k in range(DK):
                        mm = nc.tensor.matmul(ps[:, 3, k * B:(k + 1) * B], upb_sb[:, k * P:(k + 1) * P],
                                              denseT[:], start=True, stop=True)
                    mm.then_inc(cols_ps, 1)

                @block.vector
                def _(dve):
                    steps = [0]

                    def link(ins):
                        steps[0] += 1
                        ins.then_inc(gate_step, 1)
                        dve.wait_ge(gate_step, steps[0])

                    nc.vector.tensor_reduce(pooled[:].rearrange("p k b -> p (k b)"),
                                            XT[:].rearrange("p k b t -> p (k b) t"), AX.X,
                                            ALU.add).then_inc(pooled_ready, 1)
                    dve.wait_ge(glog_ps, 1)
                    link(nc.vector.tensor_scalar(glog[:], ps[0:B, 0, 0:E], 1.0 / T, None, ALU.mult))
                    link(nc.vector.max(top8[:], glog[:]))
                    link(nc.vector.max_index(topx[:], top8[:], glog[:]))
                    nc.vector.tensor_scalar(nmax[:], top8[:, 0:1], -1.0, None, ALU.mult).then_inc(nmax_ready, 1)
                    nc.vector.tensor_copy(topf[:], topx[:, 0:2]).then_inc(topx_ready, 1)
                    dve.wait_ge(gate_in, 16 * 5)
                    dve.wait_ge(gate_exp, 2)
                    link(nc.vector.tensor_reduce(gsum[:], gex[:], AX.X, ALU.add))
                    link(nc.vector.reciprocal(gsum[:], gsum[:]))
                    link(nc.vector.tensor_scalar(tex[:], tex[:], gsum[:], None, ALU.mult))
                    link(nc.vector.tensor_reduce(tsum[:], tex[:], AX.X, ALU.add))
                    link(nc.vector.tensor_scalar(tsum[:], tsum[:], 1e-8, None, ALU.add))
                    link(nc.vector.reciprocal(tsum[:], tsum[:]))
                    link(nc.vector.tensor_scalar(tex[:], tex[:], tsum[:], None, ALU.mult))
                    link(nc.vector.tensor_copy(tw_rep[:], tex[:].unsqueeze(2).to_broadcast([B, 2, C])))
                    for k in range(2):
                        link(nc.vector.tensor_scalar(dense[:, k, :], iota_sb[:], topf[:, k:k + 1], tex[:, k:k + 1],
                                                     ALU.is_equal, ALU.mult))
                    nc.vector.tensor_tensor(dense[:, 0, :], dense[:, 0, :], dense[:, 1, :],
                                            ALU.add).then_inc(dense_ready, 1)
                    dve.wait_ge(dense_ps, 1)
                    nc.vector.tensor_copy(denseT[:], ps[0:E, 1, 0:B]).then_inc(denseT_ready, 1)
                    dve.wait_ge(cols_ps, 1)
                    nc.vector.tensor_copy(twcol[:], ps[:, 2, 0:B])
                    nc.vector.tensor_copy(ubT[:], ps[:, 3, 0:DK * B].rearrange("p (k b) -> p k b", k=DK))

            wd_st = reuse("s k e c", 2, DK, 2, C)
            wu_st = reuse("s d", 2, D + 1)
            act_g = reuse("s t", 2, T)
            act_s = reuse("s t", 2, T)
            stg = reuse("s k n", 2, DK, GT)

            wd_ready, wu_ready, down_ps, gelu_ready = sem("wd_ready"), sem("wu_ready"), sem("down_ps"), sem("gelu_ready")
            scaled_ready, up_ps, out_read_act, out_read_dve = (sem("scaled_ready"), sem("up_ps"),
                                                               sem("out_read_act"), sem("out_read_dve"))

            def expert(eng, b, k):
                return eng.value_load(idx_row[0:1, ds(b * 2 + k, 1)], min_val=0, max_val=E - 1)

            def column(a, b):
                return a[:, ds(b, 1)]

            def peeled(eng, step):
                for u in range(2):
                    step(u, u, u == 0, False)
                with eng.Fori(1, B // 2 - 1) as i:
                    for u in range(2):
                        step(i * 2 + u, u, False, False)
                for u in range(2):
                    step(B - 2 + u, u, False, u == 1)

            with nc.Block() as block:
                @block.gpsimd
                def _(pool):
                    def stage(b, s, before):
                        chosen = [expert(pool, b, k) for k in range(2)]
                        if before is not None:
                            pool.wait_ge(up_ps, before)
                        for k, e in enumerate(chosen):
                            ins = nc.gpsimd.tensor_copy(
                                wu_st[C * k:C * k + C, s, :],
                                wu_sb[C * k:C * k + C, ds(e, 1), :].rearrange("p o d -> p (o d)"))
                            ins.then_inc(wu_ready, 1)

                    def step(b, u, first, last):
                        if not last:
                            stage(b + 1, 1 - u, b)

                    stage(0, 0, None)
                    peeled(pool, step)

                @block.vector
                def _(dve):
                    def stage(b, s, before):
                        chosen = [expert(dve, b, k) for k in range(2)]
                        if before is not None:
                            dve.wait_ge(down_ps, before)
                        for k, e in enumerate(chosen):
                            nc.vector.tensor_copy(
                                wd_st[:, s, :, k, :],
                                wd_sb[:, ds(e, 1), :, :].rearrange("p o k c -> p (o k) c")).then_inc(wd_ready, 1)

                    def evacuate(b, s):
                        dve.wait_ge(up_ps, b + 1)
                        nc.vector.tensor_scalar(
                            XT[:, 1, ds(b, 1), :].rearrange("p o t -> p (o t)"), ps[:, 4 + 2 * s + 1, 0:T],
                            column(ubT[:, 1], b), None, ALU.add).then_inc(out_read_dve, 1)

                    def step(b, u, first, last):
                        if not last:
                            stage(b + 1, 1 - u, b)
                        dve.wait_ge(gelu_ready, b + 1)
                        nc.vector.tensor_scalar(act_s[:, u, :], act_g[:, u, :], column(twcol, b), None,
                                                ALU.mult).then_inc(scaled_ready, 1)
                        if not first:
                            evacuate(b - 1, 1 - u)

                    stage(0, 0, None)
                    peeled(dve, step)
                    evacuate(B - 1, 1)

                @block.scalar
                def _(act):
                    def evacuate(b, s):
                        act.wait_ge(up_ps, b + 1)
                        nc.scalar.activation(
                            XT[:, 0, ds(b, 1), :].rearrange("p o t -> p (o t)"), ps[:, 4 + 2 * s, 0:T],
                            ACT.Identity, bias=column(ubT[:, 0], b)).then_inc(out_read_act, 1)

                    def step(b, u, first, last):
                        act.wait_ge(wu_ready, b * 2 + 2)
                        act.wait_ge(down_ps, b + 1)
                        act.wait_ge(scaled_ready, b)
                        nc.scalar.activation(act_g[:, u, :], ps[:, u, 0:T], ACT.Gelu,
                                             bias=wu_st[:, u, D:D + 1]).then_inc(gelu_ready, 1)
                        if not first:
                            evacuate(b - 1, 1 - u)

                    peeled(act, step)
                    evacuate(B - 1, 1)

                @block.tensor
                def _(pe):
                    def down(b, s):
                        pe.wait_ge(wd_ready, b * 2 + 2)
                        for k in range(DK):
                            mm = nc.tensor.matmul(ps[:, s, 0:T], wd_st[:, s, k].rearrange("p e c -> p (e c)"),
                                                  XT[:, k, ds(b, 1), :].rearrange("p o t -> p (o t)"),
                                                  start=(k == 0), stop=(k == DK - 1))
                        mm.then_inc(down_ps, 1)

                    def step(b, u, first, last):
                        if not last:
                            pe.wait_ge(gelu_ready, b)
                            down(b + 1, 1 - u)
                        pe.wait_ge(scaled_ready, b + 1)
                        pe.wait_ge(wu_ready, b * 2 + 2)
                        if not first:
                            pe.wait_ge(out_read_act, b - 1)
                            pe.wait_ge(out_read_dve, b - 1)
                        for k in range(DK):
                            mm = nc.tensor.matmul(ps[:, 4 + 2 * u + k, 0:T], wu_st[:, u, k * P:(k + 1) * P],
                                                  act_s[:, u, :], start=True, stop=True)
                        mm.then_inc(up_ps, 1)

                    down(0, 0)
                    peeled(pe, step)

        staged_act, staged_dve, out_ps, sum_ready, stored = (sem("staged_act"), sem("staged_dve"), sem("out_ps"),
                                                             primed["sum_ready"], sem("stored"))

        with nc.Block() as block:
            def stage_src(g, k):
                return XT[:, k, :, ds(g * TG, TG)].rearrange("p b t -> p t b")

            def stage_dst(u, k):
                return stg[:, u, k].rearrange("p (t b) -> p t b", b=B)

            @block.scalar
            def _(act):
                def stage(g, u):
                    act.wait_ge(sum_ready, g + PRIMED)
                    nc.scalar.activation(stage_dst(u, 0), stage_src(g, 0), ACT.Copy).then_inc(staged_act, 1)
                    nc.scalar.activation(stage_dst(u, 1), stage_src(g, 1), ACT.Copy).then_inc(staged_act, 1)

                with act.Fori(0, NG // 2) as i:
                    for u in range(2):
                        stage(i * 2 + u, u)

            @block.tensor
            def _(pe):
                with pe.Fori(0, NG // 2) as i:
                    for u in range(2):
                        g = i * 2 + u
                        pe.wait_ge(staged_act, g * 2 + 2)
                        for j in range(NT):
                            for k in range(DK):
                                mm = nc.tensor.transpose(
                                    ps[:, 2 * u + j // 2, (j % 2) * D + k * P:(j % 2) * D + (k + 1) * P],
                                    stg[:, u, k, j * P:(j + 1) * P], ident[:])
                        mm.then_inc(out_ps, 1)

            @block.vector
            def _(dve):
                with dve.Fori(0, NG // 2) as i:
                    for u in range(2):
                        g = i * 2 + u
                        hg = H[:, ds(g * NT, NT), :]
                        dve.wait_ge(out_ps, g + 1)
                        nc.vector.tensor_tensor(
                            hg, hg, ps[:, 2 * u:2 * u + 2, :].rearrange("p k (j d) -> p (k j) d", d=D),
                            ALU.add).then_inc(sum_ready, 1)

            @block.sync
            def _(sp):
                with sp.Fori(0, NG) as g:
                    sp.wait_ge(sum_ready, g + 1 + PRIMED)
                    for tp in range(2):
                        sp.dma_start(
                            out[:, ds(g * TG, TG), :].rearrange("b (j tp) d -> tp b j d", tp=2)[tp],
                            H[B * tp:B * tp + B, ds(g * NT, NT), :]).then_inc(stored, 16)
                sp.wait_ge(stored, 16 * 2 * NG)


def kernel(x, x_txt, L0_tok_W, L0_txt_emb0, L0_txt_emb1, L0_txt_emb2, L0_txt_emb3, L0_txt_W0, L0_txt_W1,
           L0_txt_W2, L0_txt_W3, L0_attn_W_in, L0_attn_W_router, L0_attn_W_kv, L0_attn_W_beta, L0_attn_b_beta,
           L0_attn_W_q, L0_attn_W_out, L0_ffn_gate_w, L0_ffn_down_w, L0_ffn_down_b, L0_ffn_up_w, L0_ffn_up_b):
    import numpy as np
    import concourse.bacc as bacc
    from concourse.bass_utils import run_bass_kernel_spmd

    A = np.asarray
    x, x_txt = A(x), A(x_txt)
    B, CI, IM, _ = x.shape
    PA = 16
    G = IM // PA
    D = L0_tok_W.shape[0]
    T = G * G + x_txt.shape[1]
    NB, NS = L0_attn_b_beta.shape
    E, C, _ = L0_ffn_down_w.shape

    def chunks(w):
        return w.reshape(-1, 128, w.shape[1]).transpose(1, 0, 2)

    feat = x.reshape(B, CI, G, PA, G, PA).transpose(1, 3, 5, 2, 4, 0).reshape(CI * PA * PA, G * G * B)
    feat = feat.reshape(-1, 128, (G * G) // 8, 8 * B).transpose(2, 1, 0, 3)
    kv = A(L0_attn_W_kv).reshape(NB, 2, NS, -1)
    wb = A(L0_attn_W_beta).reshape(NB, NS, -1)
    rows = []
    for h in range(2):
        n = slice(2 * h, 2 * h + 2)
        rows += [kv[n, 0].reshape(2 * NS, -1), kv[n, 1].reshape(2 * NS, -1), wb[n].reshape(2 * NS, -1)]
    proj = np.concatenate(rows + [A(L0_attn_W_q), A(L0_attn_W_router)], 0).T
    up = np.concatenate([A(L0_ffn_up_w).transpose(2, 0, 1), A(L0_ffn_down_b).T[:, :, None]], 2)
    arrays = {
        "patches": feat,
        "wtok": chunks(A(L0_tok_W).T),
        "idx": x_txt.T.reshape(-1, 128).T,
        "emb0": A(L0_txt_emb0), "emb1": A(L0_txt_emb1), "emb2": A(L0_txt_emb2), "emb3": A(L0_txt_emb3),
        "wtxt": np.concatenate([A(w).T for w in (L0_txt_W0, L0_txt_W1, L0_txt_W2, L0_txt_W3)], 0),
        "w_in": chunks(A(L0_attn_W_in).T),
        "w_proj": chunks(proj),
        "b_beta": np.broadcast_to(A(L0_attn_b_beta).reshape(1, 2, 2 * NS), (128, 2, 2 * NS)),
        "w_out": np.concatenate([A(L0_attn_W_out).T] * 4, 0),
        "gate_w": chunks(A(L0_ffn_gate_w).T),
        "w_down": A(L0_ffn_down_w).transpose(2, 0, 1).reshape(D // 128, 128, E, C).transpose(1, 2, 0, 3),
        "w_up": np.concatenate([up, up], 0),
        "up_b": A(L0_ffn_up_b),
        "iota8": np.tile(np.arange(E, dtype=np.float32), (B, 1)),
    }
    nc = bacc.Bacc("TRN2", target_bir_lowering=False, num_devices=1)
    feed, aps = {}, {}
    for name, a in arrays.items():
        a = np.ascontiguousarray(a)
        feed[f"{name}_dram"] = a
        aps[name] = nc.dram_tensor(f"{name}_dram", a.shape, mybir.dt.from_np(a.dtype), kind="ExternalInput").ap()
    out = nc.dram_tensor("out_dram", (B, T, D), F32, kind="ExternalOutput").ap()
    aps["embs"] = [aps.pop(f"emb{i}") for i in range(4)]
    early_fusion_kernel(nc, out=out, **aps)
    got = run_bass_kernel_spmd(nc, [feed], core_ids=[0])
    return got.results[0]["out_dram"]
```

```python
from contextlib import ExitStack

import concourse.bass as bass
from concourse import mybir

P = 128
ALU = mybir.AluOpType
ACT = mybir.ActivationFunctionType
AX = mybir.AxisListType
F32 = mybir.dt.float32
I32 = mybir.dt.int32
U32 = mybir.dt.uint32
ds = bass.ds

EPS_LN = 1e-5
PRIMED = 1


def early_fusion_kernel(nc, patches, wtok, idx, embs, wtxt, w_in, w_proj, b_beta, w_out,
                        gate_w, w_down, w_up, up_b, down_b, iota8, out):
    IG, _, FK, GT = patches.shape
    TXT_TILES = idx.shape[1]
    B, T, D = out.shape
    DK = D // P
    NS = w_out.shape[1 - 1] // 4
    NP = w_proj.shape[2]
    TG = GT // B
    NT = GT // P
    NG = T // TG
    TG_TXT = TXT_TILES // NT
    TILES = NG * NT
    HB = 2 * NS
    OPW = 3 * HB + NS
    QO, LO = 6 * HB, 6 * HB + NS
    E = up_b.shape[0]
    C = w_down.shape[3]
    ROWS = [e.shape[0] for e in embs]
    WID = [e.shape[1] for e in embs]
    COL = [sum(WID[:i]) for i in range(5)]
    XW = COL[4]
    LOW = [sum(ROWS[:i]) for i in range(4)]
    XK = [(0, P), (P, P), (2 * P, XW - 2 * P)]
    HS = NS * NS
    JQ = 4
    ZB = 4
    SPLIT = HS // 2

    opnd = nc.dram_tensor("operands_dram", [T, 2, B, OPW], F32).ap()
    topi = nc.dram_tensor("top_index_dram", [B, 2], U32).ap()

    with ExitStack() as whole:
        def sb(ctx, name, shape, dt=F32):
            return ctx.enter_context(nc.sbuf_tensor(name, shape, dt))

        def sem(name):
            return whole.enter_context(nc.semaphore(name))

        ps = whole.enter_context(nc.psum_tensor("ps", [P, 8, 512], F32))
        H = sb(whole, "H", [P, TILES, D])
        scal = sb(whole, "scal", [P, T, 8])
        primed = {name: sem(name) for name in (
            "h_ps", "xnT_ps", "xcatT_ready", "p2_ps", "opb_ready", "p1_ps",
            "xpT_ready", "kss_ready", "p2_read_act", "p2_read_dve", "sq_ps", "sqq_ready",
            "state_ready", "zsum_ready", "xt_ps", "xt_read", "pool_ps", "sum_ready",
            "opb_stored0", "opb_stored1")}
        with nc.Block() as block:
            @block.sync
            def _(sp):
                for s in primed.values():
                    sp.sem_inc(s, PRIMED)

        turns_dve, turns_pool = sem("turns_dve"), sem("turns_pool")
        ident = sb(whole, "ident", [P, P])
        fold = sb(whole, "fold", [P, B])
        sel = sb(whole, "sel", [P, 2, P])
        eps_t = sb(whole, "eps_t", [P, 1])

        with ExitStack() as ctx:
            patch_sb = sb(ctx, "patch_sb", [P, IG, FK, GT])
            wtok_sb = sb(ctx, "wtok_sb", [P, FK, D])
            wtxt_sb = sb(ctx, "wtxt_sb", [P, 3, D])
            win_sb = sb(ctx, "win_sb", [P, DK, D])
            wproj_sb = sb(ctx, "wproj_sb", [P, DK, NP])
            bb_sb = sb(ctx, "bb_sb", [P, 2, HB])
            idx_sb = sb(ctx, "idx_sb", [P, TXT_TILES], I32)
            idx_f = sb(ctx, "idx_f", [P, TXT_TILES])
            below = sb(ctx, "below", [P, TXT_TILES])
            rel = sb(ctx, "rel", [P, 4, TXT_TILES], I32)
            rel_g = sb(ctx, "rel_g", [P, 2, 4, NT], I32)
            xcat = sb(ctx, "xcat", [P, 2, NT, XW])
            xcatT = sb(ctx, "xcatT", [P, NT, 3, P])
            stats = sb(ctx, "stats", [P, NT, 6])
            mv = sb(ctx, "mv", [P, NT, 2])
            std = sb(ctx, "std", [P, NT])
            rstd = sb(ctx, "rstd", [P, NT])
            xn = sb(ctx, "xn", [P, NT, D])
            xnT = sb(ctx, "xnT", [P, DK, GT])
            sg = sb(ctx, "sg", [P, DK, GT])
            xpT = sb(ctx, "xpT", [P, DK, GT])
            beta_in = sb(ctx, "beta_in", [P, NT, 2, HB])
            ksq = sb(ctx, "ksq", [P, NT, 2, HB])
            opb = sb(ctx, "opb", [P, 2, NT, 2, OPW])
            router_lg = sb(ctx, "router_lg", [P, TILES, 4])
            kss = sb(ctx, "kss", [P, TILES, 4])
            mx = sb(ctx, "mx", [P, TILES])
            ex = sb(ctx, "ex", [P, TILES, 4])
            tot = sb(ctx, "tot", [P, TILES])
            rank = sb(ctx, "rank", [P, TILES, 4])
            cmp = sb(ctx, "cmp", [P, TILES])
            knorm = sb(ctx, "knorm", [P, TILES, 4])
            wide = sb(ctx, "wide", [P, TILES, 2, 8])

            H_PS = ps[:, 0:2, :].rearrange("p k (j d) -> p (k j) d", d=D)
            XNT_PS = ps[:, 2:2 + DK, :]
            P1_PS = ps[:, 6:6 + DK, :]
            P2_PS = ps[:, 4:4 + NT, :]

            weights_in, idx_in, patch_in = sem("weights_in"), sem("idx_in"), sem("patch_in")
            masks_step, masks_ready = sem("masks_step"), sem("masks_ready")
            idx_step, rel_ready = sem("idx_step"), sem("rel_ready")
            patch_h = sem("patch_h")
            xcat_clear, rel_staged = sem("xcat_clear"), sem("rel_staged")
            gathered = [sem(f"gathered{u}") for u in range(2)]
            xcatT_ps, xcatT_ready = sem("xcatT_ps"), primed["xcatT_ready"]
            h_ps, h_ready = primed["h_ps"], sem("h_ready")
            stats_ready, mv_ready, std_ready, rstd_ready = (sem("stats_ready"), sem("mv_ready"),
                                                            sem("std_ready"), sem("rstd_ready"))
            xn_ready, xnT_ps, xnT_ready = sem("xn_ready"), primed["xnT_ps"], sem("xnT_ready")
            p1_ps, sg_ready, xpT_ready = primed["p1_ps"], sem("sg_ready"), primed["xpT_ready"]
            p2_ps, p2_read_act, p2_read_dve = primed["p2_ps"], primed["p2_read_act"], primed["p2_read_dve"]
            ksq_ready, kss_ready, beta_in_ready = sem("ksq_ready"), primed["kss_ready"], sem("beta_in_ready")
            opb_ready = primed["opb_ready"]
            opb_stored = [primed[f"opb_stored{u}"] for u in range(2)]

            with nc.Block() as block:
                @block.sync
                def _(sp):
                    sp.dma_start(idx_sb[:], idx).then_inc(idx_in, 16)
                    for g in range(IG):
                        sp.dma_start(patch_sb[:, g], patches[g]).then_inc(patch_in, 16)
                    sp.dma_start(wtok_sb[:], wtok).then_inc(patch_in, 16)
                    for k, (c0, n) in enumerate(XK):
                        sp.dma_start(wtxt_sb[0:n, k, :], wtxt[c0:c0 + n, :]).then_inc(weights_in, 16)
                    sp.dma_start(win_sb[:], w_in).then_inc(weights_in, 16)
                    sp.dma_start(wproj_sb[:], w_proj).then_inc(weights_in, 16)
                    sp.dma_start(bb_sb[:], b_beta).then_inc(weights_in, 16)

                    def store(n, u):
                        sp.wait_ge(opb_ready, n + 1 + PRIMED)
                        for tp in range(2):
                            dst = opnd[ds(n * TG, TG)].rearrange("(j tp) h b f -> tp b j h f", tp=2)[tp]
                            for j in range(NT):
                                sp.dma_start(dst[:, j], opb[64 * tp:64 * tp + 64, u, j]).then_inc(opb_stored[u], 16)

                    with sp.Fori(0, NG // 2) as i:
                        for u in range(2):
                            store(i * 2 + u, u)
                    for u in range(2):
                        sp.wait_ge(opb_stored[u], 16 * 2 * NT * (NG // 2) + PRIMED)

                @block.gpsimd
                def _(pool):
                    nc.gpsimd.memset(ident[:], 0.0).then_inc(masks_step, 1)
                    nc.gpsimd.memset(fold[:], 0.0).then_inc(masks_step, 1)
                    nc.gpsimd.memset(sel[:], 0.0).then_inc(masks_step, 1)
                    nc.gpsimd.memset(eps_t[:], EPS_LN).then_inc(masks_ready, 1)
                    pool.wait_ge(masks_step, 3)
                    nc.gpsimd.affine_select(out=ident[:], in_=ident[:], compare_op=ALU.not_equal, fill=1.0,
                                            base=0, pattern=[[-1, P]], channel_multiplier=1).then_inc(masks_ready, 1)
                    nc.gpsimd.affine_select(out=fold[:], in_=fold[:], compare_op=ALU.not_equal, fill=1.0,
                                            base=0, pattern=[[-1, B]], channel_multiplier=1).then_inc(masks_step, 1)
                    pool.wait_ge(masks_step, 4)
                    nc.gpsimd.affine_select(out=fold[:], in_=fold[:], compare_op=ALU.not_equal, fill=1.0,
                                            base=-B, pattern=[[-1, B]], channel_multiplier=1).then_inc(masks_ready, 1)
                    for tp in range(2):
                        s = sel[:, tp, :].rearrange("p (h b) -> p h b", h=2)
                        nc.gpsimd.affine_select(out=s, in_=s, compare_op=ALU.not_equal, fill=1.0, base=-64 * tp,
                                                pattern=[[0, 2], [-1, B]], channel_multiplier=1).then_inc(masks_ready, 1)

                    def gather(n, u, reused):
                        if reused:
                            pool.wait_ge(h_ps, n - 1 + PRIMED)
                            pool.sem_inc(turns_pool, 1)
                        nc.gpsimd.memset(xcat[:, u], 0.0).then_inc(xcat_clear, 1)
                        nc.gpsimd.tensor_copy(rel_g[:, u], rel[:, :, ds(n * NT, NT)]).then_inc(rel_staged, 1)
                        pool.wait_ge(xcat_clear, n + 1)
                        pool.wait_ge(rel_staged, n + 1)
                        pool.sem_inc(turns_pool, 1)
                        for j in range(NT):
                            for t in range(4):
                                nc.gpsimd.indirect_dma_start(
                                    xcat[:, u, j, COL[t]:COL[t + 1]], None, embs[t],
                                    bass.IndirectOffsetOnAxis(ap=rel_g[:, u, t, j:j + 1], axis=0),
                                    bounds_check=ROWS[t] - 1, oob_is_err=False).then_inc(gathered[u], 16)

                    pool.wait_ge(rel_ready, 4)
                    for u in range(2):
                        gather(u, u, False)
                    with pool.Fori(1, TG_TXT // 2) as i:
                        for u in range(2):
                            gather(i * 2 + u, u, True)

                @block.vector
                def _(dve):
                    dve.wait_ge(idx_in, 16)
                    nc.vector.tensor_copy(idx_f[:], idx_sb[:]).then_inc(idx_step, 1)
                    dve.wait_ge(idx_step, 1)
                    for t in range(4):
                        nc.vector.tensor_scalar(below[:], idx_f[:], float(LOW[t]), float(1 << 22),
                                                ALU.is_lt, ALU.mult).then_inc(idx_step, 1)
                        dve.wait_ge(idx_step, 2 + t)
                        nc.vector.scalar_tensor_tensor(rel[:, t, :], idx_f[:], float(LOW[t]), below[:],
                                                       ALU.subtract, ALU.add).then_inc(rel_ready, 1)
                        dve.wait_ge(rel_ready, t + 1)

                    def norm_stats(n):
                        dve.wait_ge(h_ready, n + 1)
                        dve.wait_ge(xn_ready, n)
                        dve.sem_inc(turns_dve, 1)
                        for j in range(NT):
                            nc.vector.bn_stats(stats[:, j, :], H[:, ds(n * NT + j, 1), :].rearrange(
                                "p o d -> p (o d)")).then_inc(stats_ready, 1)
                        dve.wait_ge(stats_ready, n * NT + NT)
                        dve.sem_inc(turns_dve, 1)
                        for j in range(NT):
                            ins = nc.vector.bn_aggr(mv[:, j, :], stats[:, j, :])
                        ins.then_inc(mv_ready, 1)

                    def norm_apply(n):
                        dve.wait_ge(std_ready, n + 1)
                        nc.vector.reciprocal(rstd[:], std[:]).then_inc(rstd_ready, 1)
                        dve.wait_ge(rstd_ready, n + 1)
                        dve.wait_ge(xnT_ps, n + PRIMED)
                        for j in range(NT):
                            ins = nc.vector.tensor_scalar(
                                xn[:, j, :], H[:, ds(n * NT + j, 1), :].rearrange("p o d -> p (o d)"),
                                mv[:, j, 0:1], rstd[:, j:j + 1], ALU.subtract, ALU.mult)
                        ins.then_inc(xn_ready, 1)

                    def text_evacuate(n, j):
                        dve.wait_ge(xcatT_ps, n * NT + j + 1)
                        dve.wait_ge(h_ps, n + PRIMED)
                        nc.vector.tensor_copy(xcatT[:, j, 0:2, :], ps[:, 2 + j % 2, 0:2 * P].rearrange(
                            "p (k c) -> p k c", k=2))
                        nc.vector.tensor_copy(xcatT[0:XK[2][1], j, 2, :],
                                              ps[0:XK[2][1], 2 + j % 2, 2 * P:3 * P]).then_inc(xcatT_ready, 1)

                    def group(n, text, last):
                        if text:
                            text_evacuate(n, 0)
                            text_evacuate(n, 1)
                        if not last:
                            norm_stats(n + 1)
                        if text:
                            text_evacuate(n, 2)
                            text_evacuate(n, 3)
                        dve.wait_ge(sg_ready, n + 1)
                        dve.wait_ge(p2_ps, n + PRIMED)
                        nc.vector.tensor_tensor(xpT[:], P1_PS, sg[:], ALU.mult).then_inc(xpT_ready, 1)
                        if not last:
                            norm_apply(n + 1)
                        dve.wait_ge(p2_read_act, n + 1 + PRIMED)
                        dve.wait_ge(opb_ready, n + PRIMED)
                        for h in range(2):
                            c0 = (3 * h + 2) * HB
                            nc.vector.tensor_tensor(
                                beta_in[:, :, h, :], P2_PS[:, :, c0:c0 + HB],
                                bb_sb[:, h, :].unsqueeze(1).to_broadcast([P, NT, HB]),
                                ALU.add).then_inc(beta_in_ready, 1)
                        nc.vector.tensor_copy(router_lg[:, ds(n * NT, NT), :],
                                              P2_PS[:, :, LO:LO + 4]).then_inc(p2_read_dve, 1)
                        dve.wait_ge(ksq_ready, 2 * n + 2)
                        nc.vector.tensor_reduce(
                            kss[:, ds(n * NT, NT), :].rearrange("p j n -> p (j n)"),
                            ksq[:].rearrange("p j h (n i) -> p (j h n) i", n=2), AX.X,
                            ALU.add).then_inc(kss_ready, 1)

                    norm_stats(0)
                    norm_apply(0)
                    with dve.Fori(0, TG_TXT) as n:
                        group(n, True, False)
                    for n in range(TG_TXT, NG):
                        group(n, False, n == NG - 1)

                @block.scalar
                def _(act):
                    for g in range(IG):
                        act.wait_ge(patch_h, g + 1)
                        nc.scalar.activation(
                            H[:, g * NT:(g + 1) * NT, :],
                            ps[:, 2 * g:2 * g + 2, :].rearrange("p k (j d) -> p (k j) d", d=D),
                            ACT.Copy).then_inc(h_ready, 1)

                    def norm_std(n):
                        act.wait_ge(mv_ready, n + 1)
                        nc.scalar.activation(std[:], mv[:, :, 1], ACT.Sqrt, bias=eps_t[:]).then_inc(std_ready, 1)

                    def turned(n):
                        act.wait_ge(xnT_ps, n + 1 + PRIMED)
                        act.wait_ge(p1_ps, n + PRIMED)
                        nc.scalar.activation(xnT[:], XNT_PS, ACT.Copy).then_inc(xnT_ready, 1)

                    def group(n, u, text, last):
                        act.wait_ge(p1_ps, n + 1 + PRIMED)
                        act.wait_ge(xpT_ready, n + PRIMED)
                        nc.scalar.activation(sg[:], P1_PS, ACT.Sigmoid).then_inc(sg_ready, 1)
                        if not last:
                            norm_std(n + 1)
                        act.wait_ge(p2_ps, n + 1 + PRIMED)
                        act.wait_ge(kss_ready, n + PRIMED)
                        for h in range(2):
                            nc.scalar.activation(ksq[:, :, h, :], P2_PS[:, :, 3 * h * HB:3 * h * HB + HB],
                                                 ACT.Square).then_inc(ksq_ready, 1)
                        act.wait_ge(opb_stored[u], (n - u) * (16 * NT) + PRIMED)
                        for h in range(2):
                            nc.scalar.activation(opb[:, u, :, h, 0:2 * HB],
                                                 P2_PS[:, :, 3 * h * HB:3 * h * HB + 2 * HB], ACT.Copy)
                        for h in range(2):
                            ins = nc.scalar.activation(opb[:, u, :, h, 3 * HB:OPW], P2_PS[:, :, QO:QO + NS], ACT.Copy)
                        ins.then_inc(p2_read_act, 1)
                        if not last:
                            turned(n + 1)
                        act.wait_ge(beta_in_ready, 2 * n + 2)
                        nc.scalar.activation(
                            opb[:, u, :, :, 2 * HB:3 * HB].rearrange("p j h f -> p (j h) f"),
                            beta_in[:].rearrange("p j h f -> p (j h) f"), ACT.Sigmoid).then_inc(opb_ready, 1)
                        if text:
                            act.wait_ge(h_ps, n + 1 + PRIMED)
                            nc.scalar.activation(H[:, ds((n + IG) * NT, NT), :], H_PS, ACT.Copy).then_inc(h_ready, 1)

                    act.wait_ge(masks_ready, 5)
                    norm_std(0)
                    turned(0)
                    with act.Fori(0, TG_TXT // 2) as i:
                        for u in range(2):
                            group(i * 2 + u, u, True, False)
                    for n in range(TG_TXT, NG):
                        group(n, n % 2, False, n == NG - 1)

                @block.tensor
                def _(pe):
                    pe.wait_ge(patch_in, 16 * (IG + 1))
                    for g in range(IG):
                        for j in range(NT):
                            for k in range(FK):
                                mm = nc.tensor.matmul(ps[:, 2 * g + j // 2, (j % 2) * D:(j % 2) * D + D],
                                                      patch_sb[:, g, k, j * P:(j + 1) * P], wtok_sb[:, k, :],
                                                      start=(k == 0), stop=(k == FK - 1))
                        mm.then_inc(patch_h, 1)
                    pe.wait_ge(masks_ready, 5)
                    pe.wait_ge(weights_in, 16 * (len(XK) + 3))
                    pe.wait_ge(h_ready, IG)

                    def text_transpose(n, j, u):
                        pe.wait_ge(xcatT_ready, n * NT + max(j - 1, 0) + PRIMED)
                        for k, (c0, w) in enumerate(XK):
                            mm = nc.tensor.transpose(ps[0:w, 2 + j % 2, k * P:(k + 1) * P],
                                                     xcat[:, u, j, c0:c0 + w], ident[:])
                        mm.then_inc(xcatT_ps, 1)

                    def text_product(n, j):
                        pe.wait_ge(xcatT_ready, n * NT + j + 1 + PRIMED)
                        for k, (c0, w) in enumerate(XK):
                            mm = nc.tensor.matmul(ps[:, j // 2, (j % 2) * D:(j % 2) * D + D],
                                                  xcatT[0:w, j, k, :], wtxt_sb[0:w, k, :],
                                                  start=(k == 0), stop=(k == len(XK) - 1))
                        return mm

                    def norm_transpose(n, text_before):
                        pe.wait_ge(xn_ready, n + 1)
                        if text_before:
                            pe.wait_ge(xcatT_ready, n * NT + PRIMED)
                        for j in range(NT):
                            for k in range(DK):
                                mm = nc.tensor.transpose(ps[:, 2 + k, j * P:(j + 1) * P],
                                                         xn[:, j, k * P:(k + 1) * P], ident[:])
                        mm.then_inc(xnT_ps, 1)

                    def text_start(n, u):
                        pe.wait_ge(gathered[u], (n - u + 2) * (16 * NT * 4 // 2))
                        pe.wait_ge(xnT_ready, n + 1)
                        text_transpose(n, 0, u)
                        text_transpose(n, 1, u)

                    def group(n, u, text, text_after, last):
                        pe.wait_ge(xnT_ready, n + 1)
                        pe.wait_ge(p2_read_act, n + PRIMED)
                        pe.wait_ge(p2_read_dve, n + PRIMED)
                        for m in range(DK):
                            for k in range(DK):
                                mm = nc.tensor.matmul(ps[:, 6 + m, :], win_sb[:, k, m * P:(m + 1) * P],
                                                      xnT[:, k, :], start=(k == 0), stop=(k == DK - 1))
                        mm.then_inc(p1_ps, 1)
                        if text:
                            text_transpose(n, 2, u)
                            text_transpose(n, 3, u)
                            pe.wait_ge(h_ready, n + IG)
                            text_product(n, 0)
                            text_product(n, 1)
                        pe.wait_ge(xpT_ready, n + 1 + PRIMED)
                        for j in range(NT):
                            for k in range(DK):
                                mm = nc.tensor.matmul(ps[:, 4 + j, 0:NP], xpT[:, k, j * P:(j + 1) * P],
                                                      wproj_sb[:, k, :], start=(k == 0), stop=(k == DK - 1))
                        mm.then_inc(p2_ps, 1)
                        if not last:
                            norm_transpose(n + 1, text)
                        if text:
                            text_product(n, 2)
                            text_product(n, 3).then_inc(h_ps, 1)
                        if text_after:
                            text_start(n + 1, 1 - u)

                    norm_transpose(0, False)
                    text_start(0, 0)
                    with pe.Fori(0, TG_TXT // 2 - 1) as i:
                        for u in range(2):
                            group(i * 2 + u, u, True, True, False)
                    for n in range(TG_TXT - 2, NG):
                        group(n, n % 2, n < TG_TXT, n + 1 < TG_TXT, n == NG - 1)

            router_step, wide_ready, wide_moved = sem("router_step"), sem("wide_ready"), sem("wide_moved")
            logits_centred, exp_ready, knorm_ready = sem("logits_centred"), sem("exp_ready"), sem("knorm_ready")
            CT = TILES // 3
            with nc.Block() as block:
                @block.scalar
                def _(act):
                    nc.scalar.activation(knorm[:], kss[:], ACT.Sqrt).then_inc(knorm_ready, 1)
                    act.wait_ge(logits_centred, 1)
                    nc.scalar.activation(ex[:], ex[:], ACT.Exp).then_inc(exp_ready, 1)

                @block.vector
                def _(dve):
                    steps = [0]

                    def link(ins):
                        steps[0] += 1
                        ins.then_inc(router_step, 1)
                        dve.wait_ge(router_step, steps[0])

                    def per_tile(a):
                        return a.unsqueeze(2).to_broadcast([P, TILES, 4])

                    def halves(c):
                        return wide[:].rearrange("p t h f -> p (t h) f")[:, :, c:c + 2]

                    def pairs(a):
                        return a[:].rearrange("p t (h n) -> p (t h) n", h=2)

                    link(nc.vector.tensor_reduce(mx[:], router_lg[:], AX.X, ALU.max))
                    nc.vector.tensor_tensor(ex[:], router_lg[:], per_tile(mx[:]),
                                            ALU.subtract).then_inc(logits_centred, 1)
                    link(nc.vector.memset(rank[:], 0.0))
                    for m in range(4):
                        for n in range(m + 1, 4):
                            link(nc.vector.tensor_tensor(cmp[:], router_lg[:, :, m], router_lg[:, :, n], ALU.is_ge))
                            link(nc.vector.tensor_tensor(rank[:, :, n], rank[:, :, n], cmp[:], ALU.add))
                            link(nc.vector.scalar_tensor_tensor(rank[:, :, m], rank[:, :, m], 1.0, cmp[:],
                                                                ALU.add, ALU.subtract))
                    link(nc.vector.tensor_scalar(rank[:], rank[:], 2.0, None, ALU.is_lt))
                    dve.wait_ge(exp_ready, 1)
                    link(nc.vector.tensor_reduce(tot[:], ex[:], AX.X, ALU.add))
                    link(nc.vector.reciprocal(tot[:], tot[:]))
                    link(nc.vector.tensor_tensor(ex[:], ex[:], per_tile(tot[:]), ALU.mult))
                    link(nc.vector.tensor_copy(halves(4), pairs(ex)))
                    link(nc.vector.tensor_tensor(ex[:], ex[:], rank[:], ALU.mult))
                    link(nc.vector.tensor_reduce(tot[:], ex[:], AX.X, ALU.add))
                    link(nc.vector.tensor_scalar(tot[:], tot[:], 1e-8, None, ALU.add))
                    link(nc.vector.reciprocal(tot[:], tot[:]))
                    link(nc.vector.tensor_tensor(ex[:], ex[:], per_tile(tot[:]), ALU.mult))
                    link(nc.vector.tensor_copy(halves(0), pairs(ex)))
                    link(nc.vector.tensor_scalar(halves(2), pairs(ex), -1.0, 1.0, ALU.mult, ALU.add))
                    dve.wait_ge(knorm_ready, 1)
                    link(nc.vector.tensor_scalar(knorm[:], knorm[:], 1e-6, None, ALU.add))
                    link(nc.vector.reciprocal(knorm[:], knorm[:]))
                    nc.vector.tensor_copy(halves(6), pairs(knorm)).then_inc(wide_ready, 1)
                    dve.wait_ge(wide_moved, 1)
                    for tp in range(2):
                        for c in range(3):
                            for h in range(2):
                                src = ps[64 * h:64 * h + 64, 3 * tp + c, 0:16 * CT].rearrange(
                                    "p (t h f) -> p t h f", h=2, f=8)[:, :, h, :]
                                dst = scal[64 * h:64 * h + 64, :, :].rearrange("p (t tp) f -> p t tp f", tp=2)[
                                    :, c * CT:(c + 1) * CT, tp, :]
                                nc.vector.tensor_copy(dst, src)

                @block.tensor
                def _(pe):
                    pe.wait_ge(wide_ready, 1)
                    for tp in range(2):
                        for c in range(3):
                            mm = nc.tensor.matmul(ps[:, 3 * tp + c, 0:16 * CT], sel[:, tp, :],
                                                  wide[:, c * CT:(c + 1) * CT].rearrange("p t h f -> p (t h f)"),
                                                  start=True, stop=True)
                    mm.then_inc(wide_moved, 1)

        after = whole.enter_context(ExitStack())
        zsum = sb(after, "zsum", [P, T, NS])
        with ExitStack() as ctx:
            sq = sb(ctx, "sq", [P, T + 2, HB])
            S = sb(ctx, "S", [P, 2, 2, HS])
            sk = sb(ctx, "sk", [P, 2, HS])
            outer = sb(ctx, "outer", [P, 2, HS])
            bS = sb(ctx, "bS", [P, 2, HS])
            sqq = sb(ctx, "sqq", [P, 2, HS])
            op = sb(ctx, "op", [P, 4, OPW])
            kn = sb(ctx, "kn", [P, 2, HB])
            delta = sb(ctx, "delta", [P, 2, NS])
            minus_ident = sb(ctx, "minus_ident", [P, P])
            z = sb(ctx, "z", [P, ZB, HB])

            op_in = [sem(f"op_in{s}") for s in range(4)]
            junk_ready, kn_ready, state_ready = sem("junk_ready"), sem("kn_ready"), primed["state_ready"]
            sk_ready, ret_ps, delta_ready, arg_ps = sem("sk_ready"), sem("ret_ps"), sem("delta_ready"), sem("arg_ps")
            outer_ready, bS_ready, arg_ready = sem("outer_ready"), sem("bS_ready"), sem("arg_ready")
            upd_ready, keep_ready = sem("upd_ready"), sem("keep_ready")
            sqq_ready, sq_ps, sq_ready = primed["sqq_ready"], primed["sq_ps"], sem("sq_ready")
            silu_ready, z_step, zsum_ready = sem("silu_ready"), sem("z_step"), primed["zsum_ready"]


            def mat(a):
                return a.rearrange("p (i j) -> p i j", j=NS)

            def along_i(a):
                return a.unsqueeze(1).to_broadcast([P, NS, NS])

            def along_j(a):
                return a.unsqueeze(2).to_broadcast([P, NS, NS])

            def step_scalar(t, c):
                return scal[:, ds(t, 1), c:c + 1].rearrange("p o f -> p (o f)")

            with nc.Block() as block:
                @block.sync
                def _(sp):
                    def load(t, s):
                        sp.dma_start(op[:, s, :], opnd[ds(t, 1)].rearrange("o h b f -> (o h b) f")).then_inc(op_in[s], 16)

                    for t in range(3):
                        load(t, t)
                    with sp.Fori(0, T // 4 - 1) as i:
                        for u in range(4):
                            sp.wait_ge(sqq_ready, i * 8 + (2 * u + 2) + PRIMED)
                            load(i * 4 + (u + 3), (u + 3) % 4)
                    sp.wait_ge(sqq_ready, 2 * (T - 4) + 2 + PRIMED)
                    load(T - 1, 3)

                @block.gpsimd
                def _(pool):
                    def unit_key(t, u, loads):
                        pool.wait_ge(op_in[u], loads)
                        nc.gpsimd.tensor_tensor(
                            kn[:, u % 2].rearrange("p (n j) -> p n j", n=2),
                            op[:, u, 0:HB].rearrange("p (n j) -> p n j", n=2),
                            scal[:, ds(t, 1), 6:8].rearrange("p o f -> p (o f)").unsqueeze(2).to_broadcast(
                                [P, 2, NS]), ALU.mult).then_inc(kn_ready, 1)

                    def decay_product(t, u, m):
                        pool.wait_ge(state_ready, t * 2 + (m + 1) + PRIMED)
                        nc.gpsimd.tensor_tensor(
                            mat(bS[:, m]), mat(S[:, u % 2, m]),
                            along_j(op[:, u, 2 * HB + m * NS:2 * HB + (m + 1) * NS]),
                            ALU.mult).then_inc(bS_ready, 1)

                    def q_product(t, u, q_slot, m):
                        pool.wait_ge(state_ready, t * 2 + (m + 1) + PRIMED)
                        pool.wait_ge(sq_ps, t * 2 + PRIMED)
                        nc.gpsimd.tensor_tensor(mat(sqq[:, m]), mat(S[:, u % 2, m]),
                                                along_i(op[:, q_slot, 3 * HB:OPW]),
                                                ALU.mult).then_inc(sqq_ready, 1)

                    def block_output(n, part):
                        z4 = z[:].rearrange("p t (n i) -> p t n i", n=2)
                        if part == 0:
                            pool.wait_ge(silu_ready, n + 1)
                            nc.gpsimd.tensor_tensor(z[:], z[:], sq[:, ds(n * ZB + 2, ZB), :],
                                                    ALU.mult).then_inc(z_step, 1)
                        elif part == 1:
                            pool.wait_ge(z_step, n * 2 + 1)
                            nc.gpsimd.tensor_tensor(
                                z4, z4, scal[:, ds(n * ZB, ZB), 4:6].unsqueeze(3).to_broadcast([P, ZB, 2, NS]),
                                ALU.mult).then_inc(z_step, 1)
                        else:
                            pool.wait_ge(z_step, n * 2 + 2)
                            nc.gpsimd.tensor_tensor(zsum[:, ds(n * ZB, ZB), :], z[:, :, 0:NS], z[:, :, NS:HB],
                                                    ALU.add).then_inc(zsum_ready, 1)

                    def turn(i, first, last):
                        for u in range(4):
                            t = i * 4 + u
                            for m in range(2):
                                decay_product(t, u, m)
                                q_product(t, u, (u + 3) % 4, m)
                            if not (last and u == 3):
                                unit_key(t + 1, (u + 1) % 4, i * 16 + (32 if u == 3 else 16))
                            if not first and u == 2:
                                block_output(i - 1, 0)
                            if not first and u == 3:
                                block_output(i - 1, 1)
                                block_output(i - 1, 2)

                    nc.gpsimd.memset(op[:, 3], 0.0).then_inc(junk_ready, 1)
                    pool.wait_ge(junk_ready, 1)
                    unit_key(0, 0, 16)
                    turn(0, True, False)
                    with pool.Fori(1, T // 4 - 1) as i:
                        turn(i, False, False)
                    turn(T // 4 - 1, False, True)
                    for m in range(2):
                        q_product(T, T, 3, m)
                    for part in range(3):
                        block_output(T // ZB - 1, part)

                @block.scalar
                def _(act):
                    def silu(n):
                        act.wait_ge(zsum_ready, n + PRIMED)
                        nc.scalar.activation(z[:], sq[:, ds(n * ZB + 2, ZB), :], ACT.Silu).then_inc(silu_ready, 1)

                    def turn(i, first):
                        for u in range(4):
                            t = i * 4 + u
                            for m in range(2):
                                act.wait_ge(state_ready, t * 2 + (m + 1) + PRIMED)
                                act.wait_ge(sqq_ready, t * 2 + PRIMED)
                                nc.scalar.activation(S[:, (u + 1) % 2, m], S[:, u % 2, m], ACT.Copy,
                                                     scale=step_scalar(t, 2 + m)).then_inc(keep_ready, 1)
                            if not first and u == 2:
                                act.wait_ge(sq_ready, t * 2 - 1)
                                silu(i - 1)
                            act.wait_ge(arg_ready, t * 2 + 1)
                            nc.scalar.activation(outer[:, 0], outer[:, 0], ACT.Tanh).then_inc(upd_ready, 1)
                            act.wait_ge(arg_ready, t * 2 + 2)
                            nc.scalar.activation(outer[:, 1, 0:SPLIT], outer[:, 1, 0:SPLIT],
                                                 ACT.Tanh).then_inc(upd_ready, 1)
                            act.wait_ge(arg_ps, t + 1)
                            nc.scalar.activation(outer[:, 1, SPLIT:HS], ps[:, 4, 0:HS - SPLIT],
                                                 ACT.Tanh).then_inc(upd_ready, 1)

                    turn(0, True)
                    with act.Fori(1, T // 4) as i:
                        turn(i, False)
                    act.wait_ge(sq_ready, 2 * T + 3)
                    silu(T // ZB - 1)

                @block.tensor
                def _(pe):
                    def row_sums(dst, weights, src, value=None):
                        for c in range(NS // JQ):
                            mm = nc.tensor.matmul(dst, weights[:], mat(src)[:, :, c * JQ:(c + 1) * JQ],
                                                  start=(c == 0), stop=(c == NS // JQ - 1))
                            if value is not None and c == 0:
                                nc.tensor.matmul(dst.rearrange("p (i j) -> p i j", j=JQ)[:, :, 0], ident[:],
                                                 value, start=False, stop=False)
                        return mm

                    def residual(t, u, m):
                        pe.wait_ge(sk_ready, t * 2 + (m + 1))
                        row_sums(ps[:, m, 0:NS * JQ], minus_ident, sk[:, m],
                                 op[:, u, HB + m * NS:HB + (m + 1) * NS]).then_inc(ret_ps, 1)

                    def q_sums(t, m):
                        pe.wait_ge(sqq_ready, t * 2 + (m + 1) + PRIMED)
                        if m == 1:
                            pe.wait_ge(sq_ready, t * 2 + 1)
                        row_sums(ps[:, 2 + m, 0:NS * JQ], ident, sqq[:, m]).then_inc(sq_ps, 1)

                    with pe.Fori(0, T // 4) as i:
                        for u in range(4):
                            t = i * 4 + u
                            residual(t, u, 0)
                            residual(t, u, 1)
                            q_sums(t, 0)
                            pe.wait_ge(bS_ready, t * 2 + 2)
                            nc.tensor.matmul(ps[:, 4, 0:HS - SPLIT], ident[:], bS[:, 1, SPLIT:HS],
                                             start=True, stop=False)
                            pe.wait_ge(outer_ready, t * 3 + 3)
                            nc.tensor.matmul(ps[:, 4, 0:HS - SPLIT], ident[:], outer[:, 1, SPLIT:HS],
                                             start=False, stop=True).then_inc(arg_ps, 1)
                            q_sums(t, 1)
                    pe.wait_ge(sq_ready, 2 * T)
                    q_sums(T, 0)
                    q_sums(T, 1)

                @block.vector
                def _(dve):
                    def partial(b):
                        return ps[:, b, 0:NS * JQ].rearrange("p (i j) -> p i j", j=JQ)

                    def q_reduce(slot, m, sums):
                        dve.wait_ge(sq_ps, sums + PRIMED)
                        nc.vector.tensor_reduce(
                            sq[:, ds(slot, 1), m * NS:(m + 1) * NS].rearrange("p o f -> p (o f)"),
                            partial(2 + m), AX.X, ALU.add).then_inc(sq_ready, 1)

                    def key_product(t, u, m):
                        dve.wait_ge(state_ready, t * 2 + (m + 1) + PRIMED)
                        nc.vector.tensor_tensor(mat(sk[:, m]), mat(S[:, u % 2, m]),
                                                along_i(kn[:, u % 2, m * NS:(m + 1) * NS]),
                                                ALU.mult).then_inc(sk_ready, 1)

                    def residual(t, m):
                        dve.wait_ge(ret_ps, t * 2 + (m + 1))
                        nc.vector.tensor_reduce(delta[:, m], partial(m), AX.X, ALU.add).then_inc(delta_ready, 1)

                    def outer_product(u, m, i0, i1):
                        nc.vector.tensor_tensor(
                            mat(outer[:, m])[:, i0:i1, :],
                            delta[:, m, i0:i1].unsqueeze(2).to_broadcast([P, i1 - i0, NS]),
                            kn[:, u % 2, m * NS:(m + 1) * NS].unsqueeze(1).to_broadcast([P, i1 - i0, NS]),
                            ALU.mult).then_inc(outer_ready, 1)

                    def new_state(t, u, m):
                        dve.wait_ge(keep_ready, t * 2 + (m + 1))
                        dve.wait_ge(upd_ready, t * 3 + 2 * m + 1)
                        nc.vector.scalar_tensor_tensor(
                            S[:, (u + 1) % 2, m], outer[:, m], step_scalar(t, m), S[:, (u + 1) % 2, m],
                            ALU.mult, ALU.add).then_inc(state_ready, 1)

                    def step(t, u, last):
                        residual(t, 0)
                        q_reduce(t, 1, t * 2)
                        dve.wait_ge(delta_ready, t * 2 + 1)
                        outer_product(u, 0, 0, NS)
                        dve.wait_ge(outer_ready, t * 3 + 1)
                        dve.wait_ge(bS_ready, t * 2 + 1)
                        nc.vector.tensor_tensor(outer[:, 0], outer[:, 0], bS[:, 0], ALU.add).then_inc(arg_ready, 1)
                        residual(t, 1)
                        dve.wait_ge(delta_ready, t * 2 + 2)
                        outer_product(u, 1, 0, SPLIT // NS)
                        outer_product(u, 1, SPLIT // NS, NS)
                        dve.wait_ge(outer_ready, t * 3 + 2)
                        dve.wait_ge(bS_ready, t * 2 + 2)
                        nc.vector.tensor_tensor(outer[:, 1, 0:SPLIT], outer[:, 1, 0:SPLIT], bS[:, 1, 0:SPLIT],
                                                ALU.add).then_inc(arg_ready, 1)
                        new_state(t, u, 0)
                        q_reduce(t + 1, 0, t * 2 + 1)
                        if not last:
                            dve.wait_ge(kn_ready, t + 2)
                            key_product(t + 1, u + 1, 0)
                        new_state(t, u, 1)
                        if not last:
                            key_product(t + 1, u + 1, 1)

                    nc.vector.tensor_scalar(minus_ident[:], ident[:], -1.0, None, ALU.mult)
                    for m in range(2):
                        nc.vector.memset(ps[:, 2 + m, 0:NS * JQ], 0.0)
                        nc.vector.memset(S[:, 0, m], 0.0).then_inc(state_ready, 1)
                    dve.wait_ge(kn_ready, 1)
                    for m in range(2):
                        key_product(0, 0, m)
                    with dve.Fori(0, T // 4 - 1) as i:
                        for u in range(4):
                            step(i * 4 + u, u, False)
                    for u in range(4):
                        step(T - 4 + u, u, u == 3)
                    q_reduce(T, 1, 2 * T)
                    q_reduce(T + 1, 0, 2 * T + 1)
                    q_reduce(T + 1, 1, 2 * T + 2)

        XT = sb(after, "XT", [P, DK, B, T])
        wd_sb = sb(after, "wd_sb", [P, E, DK, C])
        wu_sb = sb(after, "wu_sb", [P, E, D])
        gate_in = sem("gate_in")
        with ExitStack() as ctx:
            wout_sb = sb(ctx, "wout_sb", [P, D])
            zc = sb(ctx, "zc", [P, 2, TG, NS])
            zT = sb(ctx, "zT", [P, 2, B])
            stats = sb(ctx, "stats_m", [P, NT, 6])
            mv = sb(ctx, "mv_m", [P, NT, 2])
            std = sb(ctx, "std_m", [P, NT])
            rstd = sb(ctx, "rstd_m", [P, NT])
            xn = sb(ctx, "xn_m", [P, NT, D])

            wout_in, zc_ready, zT_ps, zT_ready, y_ps, h2_ready = (sem("wout_in"), sem("zc_ready"), sem("zT_ps"),
                                                                  sem("zT_ready"), sem("y_ps"), sem("h2_ready"))
            stats2, mv2, std2, rstd2, xn2 = sem("stats2"), sem("mv2"), sem("std2"), sem("rstd2"), sem("xn2")
            xt_ps, xt_read, pool_ps = primed["xt_ps"], primed["xt_read"], primed["pool_ps"]

            def groups(eng, turn):
                for g in range(2):
                    turn(g, g, g == 0, False)
                with eng.Fori(1, NG // 2 - 1) as i:
                    for u in range(2):
                        turn(i * 2 + u, u, False, False)
                for u in range(2):
                    turn(NG - 2 + u, u, False, u == 1)

            with nc.Block() as block:
                @block.sync
                def _(sp):
                    sp.dma_start(wout_sb[:], w_out).then_inc(wout_in, 16)
                    sp.dma_start(wd_sb[:], w_down).then_inc(gate_in, 16)
                    sp.dma_start(wu_sb[:], w_up).then_inc(gate_in, 16)
                    sp.wait_ge(gate_in, 16 * 2)

                @block.gpsimd
                def _(pool):
                    def stage(g, u, first):
                        if not first:
                            pool.wait_ge(zT_ps, g - 1)
                        nc.gpsimd.tensor_copy(zc[:, u], zsum[:, ds(g * TG, TG), :]).then_inc(zc_ready, 1)

                    for g in range(2):
                        stage(g, g, True)
                    with pool.Fori(1, NG // 2) as i:
                        for u in range(2):
                            stage(i * 2 + u, u, False)

                @block.scalar
                def _(act):
                    def fold_out(g):
                        act.wait_ge(zT_ps, g + 1)
                        act.wait_ge(y_ps, g)
                        nc.scalar.activation(zT[:], ps[:, 0, 0:2 * B].rearrange("p (c b) -> p c b", c=2),
                                             ACT.Copy).then_inc(zT_ready, 1)

                    def turned(g):
                        act.wait_ge(xt_ps, g + 1 + PRIMED)
                        for k in range(DK):
                            nc.scalar.activation(XT[:, k, :, ds(g * TG, TG)].rearrange("p b t -> p t b"),
                                                 ps[:, 6 + k, :].rearrange("p (t b) -> p t b", b=B),
                                                 ACT.Copy).then_inc(xt_read, 1)

                    def turn(g, u, first, last):
                        if not last:
                            fold_out(g + 1)
                        if not first:
                            turned(g - 1)
                        act.wait_ge(mv2, g + 1)
                        nc.scalar.activation(std[:], mv[:, :, 1], ACT.Sqrt, bias=eps_t[:]).then_inc(std2, 1)

                    fold_out(0)
                    groups(act, turn)
                    turned(NG - 1)

                @block.vector
                def _(dve):
                    def turn(g, u, first, last):
                        hg = H[:, ds(g * NT, NT), :].rearrange("p (q k) d -> p q k d", k=2)
                        dve.wait_ge(y_ps, g + 1)
                        nc.vector.tensor_tensor(hg, hg, ps[:, 2 + 2 * u:4 + 2 * u, :].rearrange(
                            "p k (q d) -> p q k d", d=D), ALU.add).then_inc(h2_ready, 1)
                        dve.wait_ge(h2_ready, g + 1)
                        dve.sem_inc(turns_dve, 1)
                        for j in range(NT):
                            ins = nc.vector.bn_stats(stats[:, j, :], H[:, ds(g * NT + j, 1), :].rearrange(
                                "p o d -> p (o d)"))
                        ins.then_inc(stats2, 1)
                        dve.wait_ge(stats2, g + 1)
                        dve.sem_inc(turns_dve, 1)
                        for j in range(NT):
                            ins = nc.vector.bn_aggr(mv[:, j, :], stats[:, j, :])
                        ins.then_inc(mv2, 1)
                        dve.wait_ge(std2, g + 1)
                        nc.vector.reciprocal(rstd[:], std[:]).then_inc(rstd2, 1)
                        dve.wait_ge(rstd2, g + 1)
                        dve.wait_ge(pool_ps, g + PRIMED)
                        for j in range(NT):
                            ins = nc.vector.tensor_scalar(
                                xn[:, j, :], H[:, ds(g * NT + j, 1), :].rearrange("p o d -> p (o d)"),
                                mv[:, j, 0:1], rstd[:, j:j + 1], ALU.subtract, ALU.mult)
                        ins.then_inc(xn2, 1)

                    groups(dve, turn)

                @block.tensor
                def _(pe):
                    def fold_in(g, u, first):
                        pe.wait_ge(zc_ready, g + 1)
                        if not first:
                            pe.wait_ge(zT_ready, g)
                        for c in range(2):
                            mm = nc.tensor.matmul(ps[:, 0, c * B:(c + 1) * B],
                                                  zc[:, u, 4 * c:4 * c + 4, :].rearrange("p t i -> p (t i)"),
                                                  fold[:], start=True, stop=True)
                        mm.then_inc(zT_ps, 1)

                    def product(g, u, free):
                        pe.wait_ge(zT_ready, g + 1)
                        if not free:
                            pe.wait_ge(h2_ready, g - 1)
                        for t in range(TG):
                            r, j, tp = t % 4, t // 2, t % 2
                            mm = nc.tensor.matmul(
                                ps[B * tp:B * tp + B, 2 + 2 * u + j % 2, (j // 2) * D:(j // 2) * D + D],
                                zT[NS * r:NS * r + NS, t // 4, :], wout_sb[NS * r:NS * r + NS, :],
                                start=True, stop=True)
                        mm.then_inc(y_ps, 1)

                    def transposes(g, first, last):
                        pe.wait_ge(xn2, g + 1)
                        pe.wait_ge(xt_read, g * DK + PRIMED)
                        for j in range(NT):
                            for k in range(DK):
                                mm = nc.tensor.transpose(ps[:, 6 + k, j * P:(j + 1) * P],
                                                         xn[:, j, k * P:(k + 1) * P], ident[:])
                        mm.then_inc(xt_ps, 1)
                        for j in range(NT):
                            mm = nc.tensor.matmul(ps[0:B, 1, 0:D], fold[:], xn[:, j, :],
                                                  start=(first and j == 0), stop=(last and j == NT - 1))
                        mm.then_inc(pool_ps, 1)

                    def turn(g, u, first, last):
                        if not last:
                            fold_in(g + 1, 1 - u, False)
                        if not first:
                            transposes(g - 1, isinstance(g, int) and g == 1, False)
                        if not last:
                            product(g + 1, 1 - u, first)

                    pe.wait_ge(wout_in, 16)
                    fold_in(0, 0, True)
                    product(0, 0, True)
                    groups(pe, turn)
                    transposes(NG - 1, False, True)

        with ExitStack() as ctx:
            spare = zsum[:].rearrange("p t i -> p (t i)")
            used = [0]

            def reuse(pattern, *shape):
                n = 1
                for k in shape:
                    n *= k
                at = used[0]
                used[0] += n
                a = spare[:, at:at + n]
                names = pattern.split()
                return a.rearrange(f"p ({pattern}) -> p {pattern}", **dict(zip(names, shape)))

            upb_sb = sb(ctx, "upb_sb", [E, D])
            downb_sb = sb(ctx, "downb_sb", [E, C])
            gw_sb = sb(ctx, "gw_sb", [P, DK, E])
            iota_sb = sb(ctx, "iota_sb", [B, E])
            pooled = sb(ctx, "pooled", [B, D])
            pooledT = sb(ctx, "pooledT", [P, DK, B])
            glog = sb(ctx, "glog", [B, E])
            top8 = sb(ctx, "top8", [B, 8])
            topx = sb(ctx, "topx", [B, 8], U32)
            topf = sb(ctx, "topf", [B, 2])
            nmax = sb(ctx, "nmax", [B, 1])
            gex = sb(ctx, "gex", [B, E])
            gsum = sb(ctx, "gsum", [B, 1])
            tex = sb(ctx, "tex", [B, 2])
            tsum = sb(ctx, "tsum", [B, 1])
            tw_rep = sb(ctx, "tw_rep", [B, 2, C])
            hot = sb(ctx, "hot", [B, 2, E])
            hotT = sb(ctx, "hotT", [E, 2, B])
            dense = sb(ctx, "dense", [B, 2, E])
            denseT = sb(ctx, "denseT", [E, B])
            twcol = sb(ctx, "twcol", [P, B])
            dbcol = sb(ctx, "dbcol", [P, B])
            ubT = sb(ctx, "ubT", [P, DK, B])
            idx_row = sb(ctx, "idx_row", [1, 2 * B], U32)

            small_in, pooled_step, glog_ps, gate_step = (sem("small_in"), sem("pooled_step"), sem("glog_ps"),
                                                         sem("gate_step"))
            pooledT_ps, hot_ready, hotT_ready = sem("pooledT_ps"), sem("hot_ready"), sem("hotT_ready")
            nmax_ready, gate_exp, topx_ready, topi_out, idx_row_in = (sem("nmax_ready"), sem("gate_exp"),
                                                                     sem("topx_ready"), sem("topi_out"),
                                                                     sem("idx_row_in"))
            dense_ready, dense_ps, denseT_ready, cols_ps = (sem("dense_ready"), sem("dense_ps"),
                                                            sem("denseT_ready"), sem("cols_ps"))
            with nc.Block() as block:
                @block.sync
                def _(sp):
                    for dst, src in ((gw_sb, gate_w), (iota_sb, iota8), (upb_sb, up_b), (downb_sb, down_b)):
                        sp.dma_start(dst[:], src).then_inc(small_in, 16)
                    sp.wait_ge(topx_ready, 1)
                    sp.dma_start(topi, topx[:, 0:2]).then_inc(topi_out, 16)
                    sp.wait_ge(topi_out, 16)
                    sp.dma_start(idx_row[:], topi.rearrange("b k -> (b k)").unsqueeze(0)).then_inc(idx_row_in, 16)
                    sp.wait_ge(idx_row_in, 16)

                @block.scalar
                def _(act):
                    act.wait_ge(nmax_ready, 1)
                    nc.scalar.activation(gex[:], glog[:], ACT.Exp, bias=nmax[:]).then_inc(gate_exp, 1)
                    nc.scalar.activation(tex[:], top8[:, 0:2], ACT.Exp, bias=nmax[:]).then_inc(gate_exp, 1)

                @block.tensor
                def _(pe):
                    pe.wait_ge(pooled_step, 1)
                    for k in range(DK):
                        mm = nc.tensor.transpose(ps[:, 4, k * B:(k + 1) * B], pooled[:, k * P:(k + 1) * P],
                                                 ident[0:B, 0:B])
                    mm.then_inc(pooledT_ps, 1)
                    pe.wait_ge(small_in, 16 * 4)
                    pe.wait_ge(pooled_step, 2)
                    for k in range(DK):
                        mm = nc.tensor.matmul(ps[0:B, 0, 0:E], pooledT[:, k, :], gw_sb[:, k, :],
                                              start=(k == 0), stop=(k == DK - 1))
                    mm.then_inc(glog_ps, 1)
                    pe.wait_ge(hot_ready, 1)
                    for k in range(2):
                        mm = nc.tensor.transpose(ps[0:E, 5, k * B:(k + 1) * B], hot[:, k, :], ident[0:B, 0:B])
                    mm.then_inc(dense_ps, 1)
                    pe.wait_ge(hotT_ready, 1)
                    for k in range(2):
                        mm = nc.tensor.matmul(ps[C * k:C * k + C, 6, 0:B], downb_sb[:], hotT[:, k, :],
                                              start=True, stop=True)
                    pe.wait_ge(dense_ready, 1)
                    nc.tensor.transpose(ps[0:E, 1, 0:B], dense[:, 0, :], ident[0:B, 0:B]).then_inc(dense_ps, 1)
                    nc.tensor.matmul(ps[:, 2, 0:B], tw_rep[:].rearrange("p k c -> p (k c)"), ident[0:B, 0:B],
                                     start=True, stop=True)
                    pe.wait_ge(denseT_ready, 1)
                    for k in range(DK):
                        mm = nc.tensor.matmul(ps[:, 3, k * B:(k + 1) * B], upb_sb[:, k * P:(k + 1) * P],
                                              denseT[:], start=True, stop=True)
                    mm.then_inc(cols_ps, 1)

                @block.vector
                def _(dve):
                    steps = [0]

                    def link(ins):
                        steps[0] += 1
                        ins.then_inc(gate_step, 1)
                        dve.wait_ge(gate_step, steps[0])

                    nc.vector.tensor_copy(pooled[:], ps[0:B, 1, 0:D]).then_inc(pooled_step, 1)
                    dve.wait_ge(pooledT_ps, 1)
                    nc.vector.tensor_copy(pooledT[:], ps[:, 4, 0:DK * B].rearrange(
                        "p (k b) -> p k b", k=DK)).then_inc(pooled_step, 1)
                    dve.wait_ge(glog_ps, 1)
                    link(nc.vector.tensor_scalar(glog[:], ps[0:B, 0, 0:E], 1.0 / T, None, ALU.mult))
                    link(nc.vector.max(top8[:], glog[:]))
                    nc.vector.tensor_scalar(nmax[:], top8[:, 0:1], -1.0, None, ALU.mult).then_inc(nmax_ready, 1)
                    link(nc.vector.max_index(topx[:], top8[:], glog[:]))
                    nc.vector.tensor_copy(topf[:], topx[:, 0:2]).then_inc(topx_ready, 1)
                    dve.wait_ge(topx_ready, 1)
                    dve.wait_ge(small_in, 16 * 4)
                    for k in range(2):
                        ins = nc.vector.tensor_scalar(hot[:, k, :], iota_sb[:], topf[:, k:k + 1], None, ALU.is_equal)
                    ins.then_inc(hot_ready, 1)
                    dve.wait_ge(gate_exp, 2)
                    link(nc.vector.tensor_reduce(gsum[:], gex[:], AX.X, ALU.add))
                    link(nc.vector.reciprocal(gsum[:], gsum[:]))
                    link(nc.vector.tensor_scalar(tex[:], tex[:], gsum[:], None, ALU.mult))
                    link(nc.vector.tensor_reduce(tsum[:], tex[:], AX.X, ALU.add))
                    link(nc.vector.tensor_scalar(tsum[:], tsum[:], 1e-8, None, ALU.add))
                    link(nc.vector.reciprocal(tsum[:], tsum[:]))
                    link(nc.vector.tensor_scalar(tex[:], tex[:], tsum[:], None, ALU.mult))
                    dve.wait_ge(dense_ps, 1)
                    nc.vector.tensor_copy(hotT[:], ps[0:E, 5, 0:2 * B].rearrange(
                        "e (k b) -> e k b", k=2)).then_inc(hotT_ready, 1)
                    nc.vector.tensor_copy(tw_rep[:], tex[:].unsqueeze(2).to_broadcast([B, 2, C]))
                    for k in range(2):
                        link(nc.vector.tensor_scalar(dense[:, k, :], hot[:, k, :], tex[:, k:k + 1], None, ALU.mult))
                    nc.vector.tensor_tensor(dense[:, 0, :], dense[:, 0, :], dense[:, 1, :],
                                            ALU.add).then_inc(dense_ready, 1)
                    dve.wait_ge(dense_ps, 2)
                    nc.vector.tensor_copy(denseT[:], ps[0:E, 1, 0:B]).then_inc(denseT_ready, 1)
                    dve.wait_ge(cols_ps, 1)
                    nc.vector.tensor_copy(twcol[:], ps[:, 2, 0:B])
                    nc.vector.tensor_copy(dbcol[:], ps[:, 6, 0:B])
                    nc.vector.tensor_copy(ubT[:], ps[:, 3, 0:DK * B].rearrange("p (k b) -> p k b", k=DK))

            SL = 4
            wd_st = reuse("s k e c", SL, DK, 2, C)
            wu_st = reuse("s d", SL, D)
            stg = reuse("s k n", 2, DK, GT)
            act_g = sb(ctx, "act_g", [P, SL, T])

            wd_ready, wu_dve, wu_pool, down_ps = sem("wd_ready"), sem("wu_dve"), sem("wu_pool"), sem("down_ps")
            gelu_ready, up_ps, out_read_act, out_read_dve = (sem("gelu_ready"), sem("up_ps"),
                                                             sem("out_read_act"), sem("out_read_dve"))

            def experts(engine, b, n, k):
                _, values = nc.values_load_multi_w_load_instructions(
                    idx_row[:].rearrange("o (b k) -> o b k", k=2)[:, ds(b, n), k], engines=[engine],
                    min_val=0, max_val=E - 1)
                return values

            def column(a, b):
                return a[:, ds(b, 1)]

            def up_operands(b, s, k, e):
                rows = slice(C * k, C * k + C)
                return (wu_st[rows, s, :], wu_sb[rows, ds(e, 1), :].rearrange("p o d -> p (o d)"),
                        twcol[rows, ds(b, 1)])

            def rows_of_batch(eng, step, choose=lambda b, n: [()] * n):
                chosen = choose(SL - 1, SL)
                for u in range(SL):
                    step(u, u, u, None, chosen[u])
                with eng.Fori(1, B // SL - 1) as i:
                    chosen = choose(i * SL + (SL - 1), SL)
                    for u in range(SL):
                        step(i * SL + u, u, None, None, chosen[u])
                chosen = choose(B - 1, 1)
                for u in range(SL):
                    step(B - SL + u, u, None, SL - 1 - u, chosen[0] if u == 0 else None)

            with nc.Block() as block:
                @block.gpsimd
                def _(pool):
                    def choose(b, n):
                        return experts(mybir.EngineType.Pool, b, n, 1)

                    def stage(b, s, e, before):
                        if before is not None:
                            pool.wait_ge(up_ps, before)
                        slot, weights, top = up_operands(b, s, 1, e)
                        nc.gpsimd.tensor_tensor(slot, weights, top.to_broadcast([C, D]), ALU.mult).then_inc(wu_pool, 1)

                    def step(b, u, row, left, e):
                        if e is not None:
                            stage(b + (SL - 1), (u + SL - 1) % SL, e, None if row == 0 else b)

                    for b, e in enumerate(choose(0, SL - 1)):
                        stage(b, b, e, None)
                    rows_of_batch(pool, step, choose)

                @block.vector
                def _(dve):
                    def choose(b, n):
                        return list(zip(*(experts(mybir.EngineType.DVE, b, n, k) for k in range(2))))

                    def stage(b, s, chosen, before):
                        if before is not None:
                            dve.wait_ge(up_ps, before)
                        for k, e in enumerate(chosen):
                            nc.vector.tensor_copy(
                                wd_st[:, s, :, k, :],
                                wd_sb[:, ds(e, 1), :, :].rearrange("p o k c -> p (o k) c")).then_inc(wd_ready, 1)
                        slot, weights, top = up_operands(b, s, 0, chosen[0])
                        nc.vector.tensor_scalar(slot, weights, top, None, ALU.mult).then_inc(wu_dve, 1)

                    def evacuate(b, s):
                        dve.wait_ge(up_ps, b + 1)
                        nc.vector.tensor_scalar(
                            XT[:, 1, ds(b, 1), :].rearrange("p o t -> p (o t)"), ps[:, 4 + 2 * (s % 2) + 1, 0:T],
                            column(ubT[:, 1], b), None, ALU.add).then_inc(out_read_dve, 1)

                    def step(b, u, row, left, chosen):
                        if row != 0:
                            evacuate(b - 1, u + SL - 1)
                        if chosen is not None:
                            stage(b + (SL - 1), (u + SL - 1) % SL, chosen, None if row == 0 else b)

                    for b, chosen in enumerate(choose(0, SL - 1)):
                        stage(b, b, chosen, None)
                    rows_of_batch(dve, step, choose)
                    evacuate(B - 1, 1)

                @block.scalar
                def _(act):
                    def gelu(b, s):
                        act.wait_ge(down_ps, b + 1)
                        nc.scalar.activation(act_g[:, s, :], ps[:, s, 0:T], ACT.Gelu,
                                             bias=column(dbcol, b)).then_inc(gelu_ready, 1)

                    def evacuate(b, s):
                        act.wait_ge(up_ps, b + 1)
                        nc.scalar.activation(
                            XT[:, 0, ds(b, 1), :].rearrange("p o t -> p (o t)"), ps[:, 4 + 2 * (s % 2), 0:T],
                            ACT.Identity, bias=column(ubT[:, 0], b)).then_inc(out_read_act, 1)

                    def step(b, u, row, left, _):
                        if left is None or left >= 1:
                            gelu(b + 1, (u + 1) % SL)
                        if row != 0:
                            evacuate(b - 1, u + SL - 1)

                    gelu(0, 0)
                    rows_of_batch(act, step)
                    evacuate(B - 1, 1)

                @block.tensor
                def _(pe):
                    def down(b, s):
                        pe.wait_ge(wd_ready, b * 2 + 2)
                        for k in range(DK):
                            mm = nc.tensor.matmul(ps[:, s, 0:T], wd_st[:, s, k].rearrange("p e c -> p (e c)"),
                                                  XT[:, k, ds(b, 1), :].rearrange("p o t -> p (o t)"),
                                                  start=(k == 0), stop=(k == DK - 1))
                        mm.then_inc(down_ps, 1)

                    def step(b, u, row, left, _):
                        if left is None or left >= 2:
                            down(b + 2, (u + 2) % SL)
                        pe.wait_ge(gelu_ready, b + 1)
                        pe.wait_ge(wu_dve, b + 1)
                        pe.wait_ge(wu_pool, b + 1)
                        if row is None or row >= 2:
                            pe.wait_ge(out_read_act, b - 1)
                            pe.wait_ge(out_read_dve, b - 1)
                        for k in range(DK):
                            mm = nc.tensor.matmul(ps[:, 4 + 2 * (u % 2) + k, 0:T], wu_st[:, u, k * P:(k + 1) * P],
                                                  act_g[:, u, :], start=True, stop=True)
                        mm.then_inc(up_ps, 1)

                    for b in range(2):
                        down(b, b)
                    rows_of_batch(pe, step)

        staged_act, staged_dve, out_ps, sum_ready, stored = (sem("staged_act"), sem("staged_dve"), sem("out_ps"),
                                                             primed["sum_ready"], sem("stored"))

        with nc.Block() as block:
            def stage_src(g, k):
                return XT[:, k, :, ds(g * TG, TG)].rearrange("p b t -> p t b")

            def stage_dst(u, k):
                return stg[:, u, k].rearrange("p (t b) -> p t b", b=B)

            @block.scalar
            def _(act):
                def stage(g, u):
                    act.wait_ge(sum_ready, g + PRIMED)
                    nc.scalar.activation(stage_dst(u, 0), stage_src(g, 0), ACT.Copy).then_inc(staged_act, 1)
                    nc.scalar.activation(stage_dst(u, 1), stage_src(g, 1), ACT.Copy).then_inc(staged_act, 1)

                with act.Fori(0, NG // 2) as i:
                    for u in range(2):
                        stage(i * 2 + u, u)

            @block.tensor
            def _(pe):
                with pe.Fori(0, NG // 2) as i:
                    for u in range(2):
                        g = i * 2 + u
                        pe.wait_ge(staged_act, g * 2 + 2)
                        for j in range(NT):
                            for k in range(DK):
                                mm = nc.tensor.transpose(
                                    ps[:, 2 * u + j // 2, (j % 2) * D + k * P:(j % 2) * D + (k + 1) * P],
                                    stg[:, u, k, j * P:(j + 1) * P], ident[:])
                        mm.then_inc(out_ps, 1)

            @block.vector
            def _(dve):
                with dve.Fori(0, NG // 2) as i:
                    for u in range(2):
                        g = i * 2 + u
                        hg = H[:, ds(g * NT, NT), :]
                        dve.wait_ge(out_ps, g + 1)
                        nc.vector.tensor_tensor(
                            hg, hg, ps[:, 2 * u:2 * u + 2, :].rearrange("p k (j d) -> p (k j) d", d=D),
                            ALU.add).then_inc(sum_ready, 1)

            @block.sync
            def _(sp):
                with sp.Fori(0, NG) as g:
                    sp.wait_ge(sum_ready, g + 1 + PRIMED)
                    for tp in range(2):
                        sp.dma_start(
                            out[:, ds(g * TG, TG), :].rearrange("b (j tp) d -> tp b j d", tp=2)[tp],
                            H[B * tp:B * tp + B, ds(g * NT, NT), :]).then_inc(stored, 16)
                sp.wait_ge(stored, 16 * 2 * NG)


def kernel(x, x_txt, L0_tok_W, L0_txt_emb0, L0_txt_emb1, L0_txt_emb2, L0_txt_emb3, L0_txt_W0, L0_txt_W1,
           L0_txt_W2, L0_txt_W3, L0_attn_W_in, L0_attn_W_router, L0_attn_W_kv, L0_attn_W_beta, L0_attn_b_beta,
           L0_attn_W_q, L0_attn_W_out, L0_ffn_gate_w, L0_ffn_down_w, L0_ffn_down_b, L0_ffn_up_w, L0_ffn_up_b):
    import numpy as np
    import concourse.bacc as bacc
    from concourse.bass_utils import run_bass_kernel_spmd

    A = np.asarray
    x, x_txt = A(x), A(x_txt)
    B, CI, IM, _ = x.shape
    PA = 16
    G = IM // PA
    D = L0_tok_W.shape[0]
    T = G * G + x_txt.shape[1]
    NB, NS = L0_attn_b_beta.shape
    E, C, _ = L0_ffn_down_w.shape

    def chunks(w):
        return w.reshape(-1, 128, w.shape[1]).transpose(1, 0, 2)

    feat = x.reshape(B, CI, G, PA, G, PA).transpose(1, 3, 5, 2, 4, 0).reshape(CI * PA * PA, G * G * B)
    feat = feat.reshape(-1, 128, (G * G) // 8, 8 * B).transpose(2, 1, 0, 3)
    kv = A(L0_attn_W_kv).reshape(NB, 2, NS, -1)
    wb = A(L0_attn_W_beta).reshape(NB, NS, -1)
    rows = []
    for h in range(2):
        n = slice(2 * h, 2 * h + 2)
        rows += [kv[n, 0].reshape(2 * NS, -1), kv[n, 1].reshape(2 * NS, -1), wb[n].reshape(2 * NS, -1)]
    proj = np.concatenate(rows + [A(L0_attn_W_q), A(L0_attn_W_router)], 0).T
    up = A(L0_ffn_up_w).transpose(2, 0, 1)
    arrays = {
        "patches": feat,
        "wtok": chunks(A(L0_tok_W).T),
        "idx": x_txt.T.reshape(-1, 128).T,
        "emb0": A(L0_txt_emb0), "emb1": A(L0_txt_emb1), "emb2": A(L0_txt_emb2), "emb3": A(L0_txt_emb3),
        "wtxt": np.concatenate([A(w).T for w in (L0_txt_W0, L0_txt_W1, L0_txt_W2, L0_txt_W3)], 0),
        "w_in": chunks(A(L0_attn_W_in).T),
        "w_proj": chunks(proj),
        "b_beta": np.broadcast_to(A(L0_attn_b_beta).reshape(1, 2, 2 * NS), (128, 2, 2 * NS)),
        "w_out": np.concatenate([A(L0_attn_W_out).T] * 4, 0),
        "gate_w": chunks(A(L0_ffn_gate_w).T),
        "w_down": A(L0_ffn_down_w).transpose(2, 0, 1).reshape(D // 128, 128, E, C).transpose(1, 2, 0, 3),
        "w_up": np.concatenate([up, up], 0),
        "up_b": A(L0_ffn_up_b),
        "down_b": A(L0_ffn_down_b),
        "iota8": np.tile(np.arange(E, dtype=np.float32), (B, 1)),
    }
    nc = bacc.Bacc("TRN2", target_bir_lowering=False, num_devices=1)
    feed, aps = {}, {}
    for name, a in arrays.items():
        a = np.ascontiguousarray(a)
        feed[f"{name}_dram"] = a
        aps[name] = nc.dram_tensor(f"{name}_dram", a.shape, mybir.dt.from_np(a.dtype), kind="ExternalInput").ap()
    out = nc.dram_tensor("out_dram", (B, T, D), F32, kind="ExternalOutput").ap()
    aps["embs"] = [aps.pop(f"emb{i}") for i in range(4)]
    early_fusion_kernel(nc, out=out, **aps)
    got = run_bass_kernel_spmd(nc, [feed], core_ids=[0])
    return got.results[0]["out_dram"]
```

```python
from contextlib import ExitStack

import concourse.bass as bass
from concourse import mybir

P = 128
ALU = mybir.AluOpType
ACT = mybir.ActivationFunctionType
AX = mybir.AxisListType
F32 = mybir.dt.float32
I32 = mybir.dt.int32
U32 = mybir.dt.uint32
ds = bass.ds

EPS_LN = 1e-5
PRIMED = 1


def early_fusion_kernel(nc, patches, wtok, idx, embs, wtxt, w_in, w_proj, b_beta, w_out,
                        gate_w, w_down, w_up, up_b, down_b, iota8, out):
    IG, _, FK, GT = patches.shape
    TXT_TILES = idx.shape[1]
    B, T, D = out.shape
    DK = D // P
    NS = w_out.shape[1 - 1] // 4
    NP = w_proj.shape[2]
    TG = GT // B
    NT = GT // P
    NG = T // TG
    TG_TXT = TXT_TILES // NT
    TILES = NG * NT
    HB = 2 * NS
    OPW = 3 * HB + NS
    QO, LO = 6 * HB, 6 * HB + NS
    E = up_b.shape[0]
    C = w_down.shape[3]
    ROWS = [e.shape[0] for e in embs]
    WID = [e.shape[1] for e in embs]
    COL = [sum(WID[:i]) for i in range(5)]
    XW = COL[4]
    LOW = [sum(ROWS[:i]) for i in range(4)]
    XS = 4
    XK = [(0, P), (P, P), (2 * P, XW - 2 * P)]
    HS = NS * NS
    JQ = 4
    ZB = 4
    SPLIT = HS // 2

    opnd = nc.dram_tensor("operands_dram", [T, 2, B, OPW], F32).ap()
    topi = nc.dram_tensor("top_index_dram", [B, 2], U32).ap()

    with ExitStack() as whole:
        def sb(ctx, name, shape, dt=F32):
            return ctx.enter_context(nc.sbuf_tensor(name, shape, dt))

        def sem(name):
            return whole.enter_context(nc.semaphore(name))

        ps = whole.enter_context(nc.psum_tensor("ps", [P, 8, 512], F32))
        H = sb(whole, "H", [P, TILES, D])
        scal = sb(whole, "scal", [P, T, 8])
        primed = {name: sem(name) for name in (
            "h_ps", "xnT_ps", "xcatT_ready", "p2_ps", "opb_ready", "p1_ps",
            "xpT_ready", "kss_ready", "p2_read_act", "p2_read_dve", "sq_ps", "sqq_ready",
            "state_ready", "zsum_ready", "xt_ps", "xt_read", "sum_ready",
            "opb_stored0", "opb_stored1")}
        with nc.Block() as block:
            @block.sync
            def _(sp):
                for s in primed.values():
                    sp.sem_inc(s, PRIMED)

        turns_dve, turns_pool = sem("turns_dve"), sem("turns_pool")
        ident = sb(whole, "ident", [P, P])
        fold = sb(whole, "fold", [P, B])
        sel = sb(whole, "sel", [P, 2, P])
        eps_t = sb(whole, "eps_t", [P, 1])

        op = sb(whole, "op", [P, 4, OPW])
        op_in = [sem(f"op_in{s}") for s in range(4)]
        wout_sb, wout_in = sb(whole, "wout_sb", [P, D]), sem("wout_in")

        def load_operands(sp, t, s):
            sp.dma_start(op[:, s, :], opnd[ds(t, 1)].rearrange("o h b f -> (o h b) f")).then_inc(op_in[s], 16)

        with ExitStack() as ctx:
            patch_sb = sb(ctx, "patch_sb", [P, IG, FK, GT])
            wtok_sb = sb(ctx, "wtok_sb", [P, FK, D])
            wtxt_sb = sb(ctx, "wtxt_sb", [P, 3, D])
            win_sb = sb(ctx, "win_sb", [P, DK, D])
            wproj_sb = sb(ctx, "wproj_sb", [P, DK, NP])
            bb_sb = sb(ctx, "bb_sb", [P, 2, HB])
            idx_sb = sb(ctx, "idx_sb", [P, TXT_TILES], I32)
            idx_f = sb(ctx, "idx_f", [P, TXT_TILES])
            below = sb(ctx, "below", [P, TXT_TILES])
            rel = sb(ctx, "rel", [P, 4, TXT_TILES], I32)
            rel_g = sb(ctx, "rel_g", [P, XS, 4, NT], I32)
            xcat = sb(ctx, "xcat", [P, XS, NT, XW])
            xcatT = sb(ctx, "xcatT", [P, NT, 3, P])
            stats = sb(ctx, "stats", [P, NT, 6])
            mv = sb(ctx, "mv", [P, NT, 2])
            std = sb(ctx, "std", [P, NT])
            rstd = sb(ctx, "rstd", [P, NT])
            xn = sb(ctx, "xn", [P, NT, D])
            xnT = sb(ctx, "xnT", [P, DK, GT])
            sg = sb(ctx, "sg", [P, DK, GT])
            xpT = sb(ctx, "xpT", [P, DK, GT])
            beta_in = sb(ctx, "beta_in", [P, NT, 2, HB])
            ksq = sb(ctx, "ksq", [P, NT, 2, HB])
            opb = sb(ctx, "opb", [P, 2, NT, 2, OPW])
            router_lg = sb(ctx, "router_lg", [P, TILES, 4])
            kss = sb(ctx, "kss", [P, TILES, 4])
            mx = sb(ctx, "mx", [P, TILES])
            ex = sb(ctx, "ex", [P, TILES, 4])
            tot = sb(ctx, "tot", [P, TILES])
            rank = sb(ctx, "rank", [P, TILES, 4])
            cmp = sb(ctx, "cmp", [P, TILES])
            knorm = sb(ctx, "knorm", [P, TILES, 4])
            wide = sb(ctx, "wide", [P, TILES, 2, 8])

            H_PS = ps[:, 0:2, :].rearrange("p k (j d) -> p (k j) d", d=D)
            XNT_PS = ps[:, 2:2 + DK, :]
            P1_PS = ps[:, 6:6 + DK, :]
            P2_PS = ps[:, 4:4 + NT, :]

            weights_in, idx_in, wtok_in = sem("weights_in"), sem("idx_in"), sem("wtok_in")
            patch_in = [sem(f"patch_in{g}") for g in range(IG)]
            masks_step, masks_ready = sem("masks_step"), sem("masks_ready")
            idx_step, rel_ready = sem("idx_step"), sem("rel_ready")
            patch_h = sem("patch_h")
            xcat_clear, rel_staged = sem("xcat_clear"), sem("rel_staged")
            gathered = [sem(f"gathered{u}") for u in range(XS)]
            xcatT_ps, xcatT_ready = sem("xcatT_ps"), primed["xcatT_ready"]
            h_ps, h_ready = primed["h_ps"], sem("h_ready")
            stats_ready, mv_ready, std_ready, rstd_ready = (sem("stats_ready"), sem("mv_ready"),
                                                            sem("std_ready"), sem("rstd_ready"))
            xn_ready, xnT_ps, xnT_ready = sem("xn_ready"), primed["xnT_ps"], sem("xnT_ready")
            p1_ps, sg_ready, xpT_ready = primed["p1_ps"], sem("sg_ready"), primed["xpT_ready"]
            p2_ps, p2_read_act, p2_read_dve = primed["p2_ps"], primed["p2_read_act"], primed["p2_read_dve"]
            ksq_ready, kss_ready, beta_in_ready = sem("ksq_ready"), primed["kss_ready"], sem("beta_in_ready")
            opb_ready = primed["opb_ready"]
            opb_stored = [primed[f"opb_stored{u}"] for u in range(2)]

            def store(sp, n, u):
                sp.wait_ge(opb_ready, n + 1 + PRIMED)
                for tp in range(2):
                    dst = opnd[ds(n * TG, TG)].rearrange("(j tp) h b f -> tp b j h f", tp=2)[tp]
                    for j in range(NT):
                        sp.dma_start(dst[:, j], opb[64 * tp:64 * tp + 64, u, j]).then_inc(opb_stored[u], 16)

            with nc.Block() as block:
                @block.sync
                def _(sp):
                    sp.dma_start(idx_sb[:], idx).then_inc(idx_in, 16)
                    sp.dma_start(wtok_sb[:], wtok).then_inc(wtok_in, 16)
                    for g in range(IG):
                        sp.dma_start(patch_sb[:, g], patches[g]).then_inc(patch_in[g], 16)
                    for k, (c0, n) in enumerate(XK):
                        sp.dma_start(wtxt_sb[0:n, k, :], wtxt[c0:c0 + n, :]).then_inc(weights_in, 16)
                    sp.dma_start(win_sb[:], w_in).then_inc(weights_in, 16)
                    sp.dma_start(wproj_sb[:], w_proj).then_inc(weights_in, 16)
                    sp.dma_start(bb_sb[:], b_beta).then_inc(weights_in, 16)

                    with sp.Fori(0, NG // 2 - 1) as i:
                        for u in range(2):
                            store(sp, i * 2 + u, u)
                    store(sp, NG - 2, 0)

                @block.gpsimd
                def _(pool):
                    nc.gpsimd.memset(ident[:], 0.0).then_inc(masks_step, 1)
                    nc.gpsimd.memset(fold[:], 0.0).then_inc(masks_step, 1)
                    nc.gpsimd.memset(sel[:], 0.0).then_inc(masks_step, 1)
                    nc.gpsimd.memset(eps_t[:], EPS_LN).then_inc(masks_ready, 1)
                    pool.wait_ge(masks_step, 3)
                    nc.gpsimd.affine_select(out=ident[:], in_=ident[:], compare_op=ALU.not_equal, fill=1.0,
                                            base=0, pattern=[[-1, P]], channel_multiplier=1).then_inc(masks_ready, 1)
                    nc.gpsimd.affine_select(out=fold[:], in_=fold[:], compare_op=ALU.not_equal, fill=1.0,
                                            base=0, pattern=[[-1, B]], channel_multiplier=1).then_inc(masks_step, 1)
                    pool.wait_ge(masks_step, 4)
                    nc.gpsimd.affine_select(out=fold[:], in_=fold[:], compare_op=ALU.not_equal, fill=1.0,
                                            base=-B, pattern=[[-1, B]], channel_multiplier=1).then_inc(masks_ready, 1)
                    for tp in range(2):
                        s = sel[:, tp, :].rearrange("p (h b) -> p h b", h=2)
                        nc.gpsimd.affine_select(out=s, in_=s, compare_op=ALU.not_equal, fill=1.0, base=-64 * tp,
                                                pattern=[[0, 2], [-1, B]], channel_multiplier=1).then_inc(masks_ready, 1)

                    def gather(n, u):
                        pool.wait_ge(xcat_clear, n + 1)
                        pool.wait_ge(rel_staged, n + 1)
                        pool.sem_inc(turns_pool, 1)
                        for j in range(NT):
                            for t in range(4):
                                nc.gpsimd.indirect_dma_start(
                                    xcat[:, u, j, COL[t]:COL[t + 1]], None, embs[t],
                                    bass.IndirectOffsetOnAxis(ap=rel_g[:, u, t, j:j + 1], axis=0),
                                    bounds_check=ROWS[t] - 1, oob_is_err=False).then_inc(gathered[u], 16)

                    with pool.Fori(0, TG_TXT // XS) as i:
                        for u in range(XS):
                            gather(i * XS + u, u)

                @block.vector
                def _(dve):
                    nc.vector.memset(xcat[:, 0], 0.0).then_inc(xcat_clear, 1)
                    dve.wait_ge(idx_in, 16)
                    nc.vector.tensor_copy(idx_f[:], idx_sb[:]).then_inc(idx_step, 1)
                    dve.wait_ge(idx_step, 1)
                    for t in range(4):
                        nc.vector.tensor_scalar(below[:], idx_f[:], float(LOW[t]), float(1 << 22),
                                                ALU.is_lt, ALU.mult).then_inc(idx_step, 1)
                        dve.wait_ge(idx_step, 2 + t)
                        nc.vector.scalar_tensor_tensor(rel[:, t, :], idx_f[:], float(LOW[t]), below[:],
                                                       ALU.subtract, ALU.add).then_inc(rel_ready, 1)
                        dve.wait_ge(rel_ready, t + 1)
                    def clear_slot(u):
                        nc.vector.memset(xcat[:, u], 0.0).then_inc(xcat_clear, 1)

                    def stage_rows(n, u):
                        nc.vector.tensor_copy(rel_g[:, u], rel[:, :, ds(n * NT, NT)]).then_inc(rel_staged, 1)

                    for u in range(XS):
                        stage_rows(u, u)
                    for u in range(1, XS):
                        clear_slot(u)

                    def norm_stats(n):
                        dve.wait_ge(h_ready, n + 1)
                        dve.wait_ge(xn_ready, n)
                        dve.sem_inc(turns_dve, 1)
                        for j in range(NT):
                            nc.vector.bn_stats(stats[:, j, :], H[:, ds(n * NT + j, 1), :].rearrange(
                                "p o d -> p (o d)")).then_inc(stats_ready, 1)
                        dve.wait_ge(stats_ready, n * NT + NT)
                        dve.sem_inc(turns_dve, 1)
                        for j in range(NT):
                            ins = nc.vector.bn_aggr(mv[:, j, :], stats[:, j, :])
                        ins.then_inc(mv_ready, 1)

                    def norm_apply(n):
                        dve.wait_ge(std_ready, n + 1)
                        nc.vector.reciprocal(rstd[:], std[:]).then_inc(rstd_ready, 1)
                        dve.wait_ge(rstd_ready, n + 1)
                        dve.wait_ge(xnT_ps, n + PRIMED)
                        for j in range(NT):
                            ins = nc.vector.tensor_scalar(
                                xn[:, j, :], H[:, ds(n * NT + j, 1), :].rearrange("p o d -> p (o d)"),
                                mv[:, j, 0:1], rstd[:, j:j + 1], ALU.subtract, ALU.mult)
                        ins.then_inc(xn_ready, 1)

                    def text_evacuate(n, j):
                        dve.wait_ge(xcatT_ps, n * NT + j + 1)
                        dve.wait_ge(h_ps, n + PRIMED)
                        nc.vector.tensor_copy(xcatT[:, j, 0:2, :], ps[:, 2 + j % 2, 0:2 * P].rearrange(
                            "p (k c) -> p k c", k=2))
                        nc.vector.tensor_copy(xcatT[0:XK[2][1], j, 2, :],
                                              ps[0:XK[2][1], 2 + j % 2, 2 * P:3 * P]).then_inc(xcatT_ready, 1)

                    def group(n, u, text, again, last):
                        if text:
                            text_evacuate(n, 0)
                            text_evacuate(n, 1)
                        if not last:
                            norm_stats(n + 1)
                        if text:
                            text_evacuate(n, 2)
                            text_evacuate(n, 3)
                        dve.wait_ge(sg_ready, n + 1)
                        dve.wait_ge(p2_ps, n + PRIMED)
                        nc.vector.tensor_tensor(xpT[:], P1_PS, sg[:], ALU.mult).then_inc(xpT_ready, 1)
                        if not last:
                            norm_apply(n + 1)
                        if again:
                            stage_rows(n + XS, u)
                            clear_slot(u)
                        dve.wait_ge(p2_read_act, n + 1 + PRIMED)
                        dve.wait_ge(opb_ready, n + PRIMED)
                        for h in range(2):
                            c0 = (3 * h + 2) * HB
                            nc.vector.tensor_tensor(
                                beta_in[:, :, h, :], P2_PS[:, :, c0:c0 + HB],
                                bb_sb[:, h, :].unsqueeze(1).to_broadcast([P, NT, HB]),
                                ALU.add).then_inc(beta_in_ready, 1)
                        nc.vector.tensor_copy(router_lg[:, ds(n * NT, NT), :],
                                              P2_PS[:, :, LO:LO + 4]).then_inc(p2_read_dve, 1)
                        dve.wait_ge(ksq_ready, 2 * n + 2)
                        nc.vector.tensor_reduce(
                            kss[:, ds(n * NT, NT), :].rearrange("p j n -> p (j n)"),
                            ksq[:].rearrange("p j h (n i) -> p (j h n) i", n=2), AX.X,
                            ALU.add).then_inc(kss_ready, 1)

                    norm_stats(0)
                    norm_apply(0)
                    with dve.Fori(0, TG_TXT // XS - 1) as i:
                        for u in range(XS):
                            group(i * XS + u, u, True, True, False)
                    for n in range(TG_TXT - XS, NG):
                        group(n, n % XS, n < TG_TXT, False, n == NG - 1)

                @block.scalar
                def _(act):
                    def norm_std(n):
                        act.wait_ge(mv_ready, n + 1)
                        nc.scalar.activation(std[:], mv[:, :, 1], ACT.Sqrt, bias=eps_t[:]).then_inc(std_ready, 1)

                    def turned(n):
                        act.wait_ge(xnT_ps, n + 1 + PRIMED)
                        act.wait_ge(p1_ps, n + PRIMED)
                        nc.scalar.activation(xnT[:], XNT_PS, ACT.Copy).then_inc(xnT_ready, 1)

                    def group(n, u, text, last):
                        act.wait_ge(p1_ps, n + 1 + PRIMED)
                        act.wait_ge(xpT_ready, n + PRIMED)
                        nc.scalar.activation(sg[:], P1_PS, ACT.Sigmoid).then_inc(sg_ready, 1)
                        if not last:
                            norm_std(n + 1)
                        act.wait_ge(p2_ps, n + 1 + PRIMED)
                        act.wait_ge(kss_ready, n + PRIMED)
                        for h in range(2):
                            nc.scalar.activation(ksq[:, :, h, :], P2_PS[:, :, 3 * h * HB:3 * h * HB + HB],
                                                 ACT.Square).then_inc(ksq_ready, 1)
                        act.wait_ge(opb_stored[u], (n - u) * (16 * NT) + PRIMED)
                        for h in range(2):
                            nc.scalar.activation(opb[:, u, :, h, 0:2 * HB],
                                                 P2_PS[:, :, 3 * h * HB:3 * h * HB + 2 * HB], ACT.Copy)
                        for h in range(2):
                            ins = nc.scalar.activation(opb[:, u, :, h, 3 * HB:OPW], P2_PS[:, :, QO:QO + NS], ACT.Copy)
                        ins.then_inc(p2_read_act, 1)
                        if not last:
                            turned(n + 1)
                        act.wait_ge(beta_in_ready, 2 * n + 2)
                        nc.scalar.activation(
                            opb[:, u, :, :, 2 * HB:3 * HB].rearrange("p j h f -> p (j h) f"),
                            beta_in[:].rearrange("p j h f -> p (j h) f"), ACT.Sigmoid).then_inc(opb_ready, 1)
                        if text:
                            act.wait_ge(h_ps, n + 1 + PRIMED)
                            nc.scalar.activation(H[:, ds((n + IG) * NT, NT), :], H_PS, ACT.Copy).then_inc(h_ready, 1)

                    for g in range(IG):
                        act.wait_ge(patch_h, g + 1)
                        nc.scalar.activation(
                            H[:, g * NT:(g + 1) * NT, :],
                            ps[:, 4 * g:4 * g + 2, :].rearrange("p k (j d) -> p (k j) d", d=D),
                            ACT.Copy).then_inc(h_ready, 1)
                        if g == 0:
                            act.wait_ge(masks_ready, 5)
                            norm_std(0)

                    turned(0)
                    with act.Fori(0, TG_TXT // 2) as i:
                        for u in range(2):
                            group(i * 2 + u, u, True, False)
                    for n in range(TG_TXT, NG):
                        group(n, n % 2, False, n == NG - 1)

                @block.tensor
                def _(pe):
                    pe.wait_ge(wtok_in, 16)
                    for g in range(IG):
                        pe.wait_ge(patch_in[g], 16)
                        for j in range(NT):
                            for k in range(FK):
                                mm = nc.tensor.matmul(ps[:, 4 * g + j // 2, (j % 2) * D:(j % 2) * D + D],
                                                      patch_sb[:, g, k, j * P:(j + 1) * P], wtok_sb[:, k, :],
                                                      start=(k == 0), stop=(k == FK - 1))
                        mm.then_inc(patch_h, 1)
                    pe.wait_ge(masks_ready, 5)
                    pe.wait_ge(weights_in, 16 * (len(XK) + 3))

                    def text_transpose(n, j, u):
                        pe.wait_ge(xcatT_ready, n * NT + max(j - 1, 0) + PRIMED)
                        for k, (c0, w) in enumerate(XK):
                            mm = nc.tensor.transpose(ps[0:w, 2 + j % 2, k * P:(k + 1) * P],
                                                     xcat[:, u, j, c0:c0 + w], ident[:])
                        mm.then_inc(xcatT_ps, 1)

                    def text_product(n, j):
                        pe.wait_ge(xcatT_ready, n * NT + j + 1 + PRIMED)
                        for k, (c0, w) in enumerate(XK):
                            mm = nc.tensor.matmul(ps[:, j // 2, (j % 2) * D:(j % 2) * D + D],
                                                  xcatT[0:w, j, k, :], wtxt_sb[0:w, k, :],
                                                  start=(k == 0), stop=(k == len(XK) - 1))
                        return mm

                    def norm_transpose(n, text_before):
                        pe.wait_ge(xn_ready, n + 1)
                        if text_before:
                            pe.wait_ge(xcatT_ready, n * NT + PRIMED)
                        for j in range(NT):
                            for k in range(DK):
                                mm = nc.tensor.transpose(ps[:, 2 + k, j * P:(j + 1) * P],
                                                         xn[:, j, k * P:(k + 1) * P], ident[:])
                        mm.then_inc(xnT_ps, 1)

                    def text_start(n, u):
                        pe.wait_ge(gathered[u], (n - u + XS) * (16 * NT * 4 // XS))
                        pe.wait_ge(xnT_ready, n + 1)
                        text_transpose(n, 0, u)
                        text_transpose(n, 1, u)

                    def group(n, u, text, text_after, last):
                        pe.wait_ge(xnT_ready, n + 1)
                        pe.wait_ge(p2_read_act, n + PRIMED)
                        pe.wait_ge(p2_read_dve, n + PRIMED)
                        for m in range(DK):
                            for k in range(DK):
                                mm = nc.tensor.matmul(ps[:, 6 + m, :], win_sb[:, k, m * P:(m + 1) * P],
                                                      xnT[:, k, :], start=(k == 0), stop=(k == DK - 1))
                        mm.then_inc(p1_ps, 1)
                        if text:
                            text_transpose(n, 2, u)
                            text_transpose(n, 3, u)
                            pe.wait_ge(h_ready, n + IG)
                            text_product(n, 0)
                            text_product(n, 1)
                        pe.wait_ge(xpT_ready, n + 1 + PRIMED)
                        for j in range(NT):
                            for k in range(DK):
                                mm = nc.tensor.matmul(ps[:, 4 + j, 0:NP], xpT[:, k, j * P:(j + 1) * P],
                                                      wproj_sb[:, k, :], start=(k == 0), stop=(k == DK - 1))
                        mm.then_inc(p2_ps, 1)
                        if not last:
                            norm_transpose(n + 1, text)
                        if text:
                            text_product(n, 2)
                            text_product(n, 3).then_inc(h_ps, 1)
                        if text_after:
                            text_start(n + 1, (u + 1) % XS)

                    norm_transpose(0, False)
                    text_start(0, 0)
                    with pe.Fori(0, TG_TXT // XS - 1) as i:
                        for u in range(XS):
                            group(i * XS + u, u, True, True, False)
                    for n in range(TG_TXT - XS, NG):
                        group(n, n % XS, n < TG_TXT, n + 1 < TG_TXT, n == NG - 1)

            router_step, wide_ready, wide_moved = sem("router_step"), sem("wide_ready"), sem("wide_moved")
            logits_centred, exp_ready, knorm_ready = sem("logits_centred"), sem("exp_ready"), sem("knorm_ready")
            CT = TILES // 3

            def own_columns(n, h):
                tp, c = n // 3, n % 3
                src = ps[64 * h:64 * h + 64, n, 0:16 * CT].rearrange("p (t h f) -> p t h f", h=2, f=8)[:, :, h, :]
                dst = scal[64 * h:64 * h + 64, :, :].rearrange("p (t tp) f -> p t tp f", tp=2)[
                    :, c * CT:(c + 1) * CT, tp, :]
                return dst, src

            with nc.Block() as block:
                @block.sync
                def _(sp):
                    store(sp, NG - 1, 1)
                    sp.dma_start(wout_sb[:], w_out).then_inc(wout_in, 16)
                    for u in range(2):
                        sp.wait_ge(opb_stored[u], 16 * 2 * NT * (NG // 2) + PRIMED)
                    for t in range(3):
                        load_operands(sp, t, t)

                @block.scalar
                def _(act):
                    nc.scalar.activation(knorm[:], kss[:], ACT.Sqrt).then_inc(knorm_ready, 1)
                    act.wait_ge(logits_centred, 1)
                    nc.scalar.activation(ex[:], ex[:], ACT.Exp).then_inc(exp_ready, 1)
                    for n in range(6):
                        act.wait_ge(wide_moved, n + 1)
                        nc.scalar.activation(*own_columns(n, 1), ACT.Copy)

                @block.vector
                def _(dve):
                    steps = [0]

                    def link(ins):
                        steps[0] += 1
                        ins.then_inc(router_step, 1)
                        dve.wait_ge(router_step, steps[0])

                    def per_tile(a):
                        return a.unsqueeze(2).to_broadcast([P, TILES, 4])

                    def halves(c):
                        return wide[:].rearrange("p t h f -> p (t h) f")[:, :, c:c + 2]

                    def pairs(a):
                        return a[:].rearrange("p t (h n) -> p (t h) n", h=2)

                    link(nc.vector.tensor_reduce(mx[:], router_lg[:], AX.X, ALU.max))
                    nc.vector.tensor_tensor(ex[:], router_lg[:], per_tile(mx[:]),
                                            ALU.subtract).then_inc(logits_centred, 1)
                    link(nc.vector.memset(rank[:], 0.0))
                    for m in range(4):
                        for n in range(m + 1, 4):
                            link(nc.vector.tensor_tensor(cmp[:], router_lg[:, :, m], router_lg[:, :, n], ALU.is_ge))
                            link(nc.vector.tensor_tensor(rank[:, :, n], rank[:, :, n], cmp[:], ALU.add))
                            link(nc.vector.scalar_tensor_tensor(rank[:, :, m], rank[:, :, m], 1.0, cmp[:],
                                                                ALU.add, ALU.subtract))
                    link(nc.vector.tensor_scalar(rank[:], rank[:], 2.0, None, ALU.is_lt))
                    dve.wait_ge(exp_ready, 1)
                    link(nc.vector.tensor_reduce(tot[:], ex[:], AX.X, ALU.add))
                    link(nc.vector.reciprocal(tot[:], tot[:]))
                    link(nc.vector.tensor_tensor(ex[:], ex[:], per_tile(tot[:]), ALU.mult))
                    link(nc.vector.tensor_copy(halves(4), pairs(ex)))
                    link(nc.vector.tensor_tensor(ex[:], ex[:], rank[:], ALU.mult))
                    link(nc.vector.tensor_reduce(tot[:], ex[:], AX.X, ALU.add))
                    link(nc.vector.tensor_scalar(tot[:], tot[:], 1e-8, None, ALU.add))
                    link(nc.vector.reciprocal(tot[:], tot[:]))
                    link(nc.vector.tensor_tensor(ex[:], ex[:], per_tile(tot[:]), ALU.mult))
                    link(nc.vector.tensor_copy(halves(0), pairs(ex)))
                    link(nc.vector.tensor_scalar(halves(2), pairs(ex), -1.0, 1.0, ALU.mult, ALU.add))
                    dve.wait_ge(knorm_ready, 1)
                    link(nc.vector.tensor_scalar(knorm[:], knorm[:], 1e-6, None, ALU.add))
                    link(nc.vector.reciprocal(knorm[:], knorm[:]))
                    nc.vector.tensor_copy(halves(6), pairs(knorm)).then_inc(wide_ready, 1)
                    for n in range(6):
                        dve.wait_ge(wide_moved, n + 1)
                        nc.vector.tensor_copy(*own_columns(n, 0))

                @block.tensor
                def _(pe):
                    pe.wait_ge(wide_ready, 1)
                    for tp in range(2):
                        for c in range(3):
                            nc.tensor.matmul(ps[:, 3 * tp + c, 0:16 * CT], sel[:, tp, :],
                                             wide[:, c * CT:(c + 1) * CT].rearrange("p t h f -> p (t h f)"),
                                             start=True, stop=True).then_inc(wide_moved, 1)

        after = whole.enter_context(ExitStack())
        zsum = sb(after, "zsum", [P, T, NS])
        with ExitStack() as ctx:
            sq = sb(ctx, "sq", [P, T + 2, HB])
            S = sb(ctx, "S", [P, 2, 2, HS])
            sk = sb(ctx, "sk", [P, 2, HS])
            outer = sb(ctx, "outer", [P, 2, HS])
            bS = sb(ctx, "bS", [P, 2, HS])
            sqq = sb(ctx, "sqq", [P, 2, HS])
            kn = sb(ctx, "kn", [P, 2, HB])
            delta = sb(ctx, "delta", [P, 2, NS])
            minus_ident = sb(ctx, "minus_ident", [P, P])
            z = sb(ctx, "z", [P, ZB, HB])

            junk_ready, kn_ready, state_ready = sem("junk_ready"), sem("kn_ready"), primed["state_ready"]
            sk_ready, ret_ps, delta_ready, arg_ps = sem("sk_ready"), sem("ret_ps"), sem("delta_ready"), sem("arg_ps")
            outer_ready, bS_ready, arg_ready = sem("outer_ready"), sem("bS_ready"), sem("arg_ready")
            upd_ready, keep_ready = sem("upd_ready"), sem("keep_ready")
            sqq_ready, sq_ps, sq_ready = primed["sqq_ready"], primed["sq_ps"], sem("sq_ready")
            silu_ready, z_step, zsum_ready = sem("silu_ready"), sem("z_step"), primed["zsum_ready"]


            def mat(a):
                return a.rearrange("p (i j) -> p i j", j=NS)

            def along_i(a):
                return a.unsqueeze(1).to_broadcast([P, NS, NS])

            def along_j(a):
                return a.unsqueeze(2).to_broadcast([P, NS, NS])

            BANK = ps.shape[2]
            ARG_PARTS = [(at, min(at + BANK, HS)) for at in range(SPLIT, HS, BANK)]
            ARG_PS = ps[:, 4:4 + len(ARG_PARTS), :].rearrange("p k c -> p (k c)")[:, 0:HS - SPLIT]

            def step_scalar(t, c):
                return scal[:, ds(t, 1), c:c + 1].rearrange("p o f -> p (o f)")

            with nc.Block() as block:
                @block.sync
                def _(sp):
                    with sp.Fori(0, T // 4 - 1) as i:
                        for u in range(4):
                            sp.wait_ge(sqq_ready, i * 8 + (2 * u + 2) + PRIMED)
                            load_operands(sp, i * 4 + (u + 3), (u + 3) % 4)
                    sp.wait_ge(sqq_ready, 2 * (T - 4) + 2 + PRIMED)
                    load_operands(sp, T - 1, 3)

                @block.gpsimd
                def _(pool):
                    def unit_key(t, u, loads):
                        pool.wait_ge(op_in[u], loads)
                        nc.gpsimd.tensor_tensor(
                            kn[:, u % 2].rearrange("p (n j) -> p n j", n=2),
                            op[:, u, 0:HB].rearrange("p (n j) -> p n j", n=2),
                            scal[:, ds(t, 1), 6:8].rearrange("p o f -> p (o f)").unsqueeze(2).to_broadcast(
                                [P, 2, NS]), ALU.mult).then_inc(kn_ready, 1)

                    def decay_product(t, u, m):
                        pool.wait_ge(state_ready, t * 2 + (m + 1) + PRIMED)
                        nc.gpsimd.tensor_tensor(
                            mat(bS[:, m]), mat(S[:, u % 2, m]),
                            along_j(op[:, u, 2 * HB + m * NS:2 * HB + (m + 1) * NS]),
                            ALU.mult).then_inc(bS_ready, 1)

                    def q_product(t, u, q_slot, m):
                        pool.wait_ge(state_ready, t * 2 + (m + 1) + PRIMED)
                        pool.wait_ge(sq_ps, t * 2 + PRIMED)
                        nc.gpsimd.tensor_tensor(mat(sqq[:, m]), mat(S[:, u % 2, m]),
                                                along_i(op[:, q_slot, 3 * HB:OPW]),
                                                ALU.mult).then_inc(sqq_ready, 1)

                    def block_output(n, part):
                        z4 = z[:].rearrange("p t (n i) -> p t n i", n=2)
                        if part == 0:
                            pool.wait_ge(silu_ready, n + 1)
                            nc.gpsimd.tensor_tensor(z[:], z[:], sq[:, ds(n * ZB + 2, ZB), :],
                                                    ALU.mult).then_inc(z_step, 1)
                        elif part == 1:
                            pool.wait_ge(z_step, n * 2 + 1)
                            nc.gpsimd.tensor_tensor(
                                z4, z4, scal[:, ds(n * ZB, ZB), 4:6].unsqueeze(3).to_broadcast([P, ZB, 2, NS]),
                                ALU.mult).then_inc(z_step, 1)
                        else:
                            pool.wait_ge(z_step, n * 2 + 2)
                            nc.gpsimd.tensor_tensor(zsum[:, ds(n * ZB, ZB), :], z[:, :, 0:NS], z[:, :, NS:HB],
                                                    ALU.add).then_inc(zsum_ready, 1)

                    def turn(i, first, last):
                        for u in range(4):
                            t = i * 4 + u
                            for m in range(2):
                                decay_product(t, u, m)
                                q_product(t, u, (u + 3) % 4, m)
                            if not (last and u == 3):
                                unit_key(t + 1, (u + 1) % 4, i * 16 + (32 if u == 3 else 16))
                            if not first and u == 2:
                                block_output(i - 1, 0)
                            if not first and u == 3:
                                block_output(i - 1, 1)
                                block_output(i - 1, 2)

                    nc.gpsimd.memset(op[:, 3], 0.0).then_inc(junk_ready, 1)
                    pool.wait_ge(junk_ready, 1)
                    unit_key(0, 0, 16)
                    turn(0, True, False)
                    with pool.Fori(1, T // 4 - 1) as i:
                        turn(i, False, False)
                    turn(T // 4 - 1, False, True)
                    for m in range(2):
                        q_product(T, T, 3, m)
                    for part in range(3):
                        block_output(T // ZB - 1, part)

                @block.scalar
                def _(act):
                    def silu(n):
                        act.wait_ge(zsum_ready, n + PRIMED)
                        nc.scalar.activation(z[:], sq[:, ds(n * ZB + 2, ZB), :], ACT.Silu).then_inc(silu_ready, 1)

                    def turn(i, first):
                        for u in range(4):
                            t = i * 4 + u
                            for m in range(2):
                                act.wait_ge(state_ready, t * 2 + (m + 1) + PRIMED)
                                act.wait_ge(sqq_ready, t * 2 + PRIMED)
                                nc.scalar.activation(S[:, (u + 1) % 2, m], S[:, u % 2, m], ACT.Copy,
                                                     scale=step_scalar(t, 2 + m)).then_inc(keep_ready, 1)
                            if not first and u == 2:
                                act.wait_ge(sq_ready, t * 2 - 1)
                                silu(i - 1)
                            act.wait_ge(arg_ready, t * 2 + 1)
                            nc.scalar.activation(outer[:, 0], outer[:, 0], ACT.Tanh).then_inc(upd_ready, 1)
                            act.wait_ge(arg_ps, t + 1)
                            nc.scalar.activation(outer[:, 1, SPLIT:HS], ARG_PS,
                                                 ACT.Tanh).then_inc(upd_ready, 1)
                            act.wait_ge(arg_ready, t * 2 + 2)
                            nc.scalar.activation(outer[:, 1, 0:SPLIT], outer[:, 1, 0:SPLIT],
                                                 ACT.Tanh).then_inc(upd_ready, 1)

                    turn(0, True)
                    with act.Fori(1, T // 4) as i:
                        turn(i, False)
                    act.wait_ge(sq_ready, 2 * T + 3)
                    silu(T // ZB - 1)

                @block.tensor
                def _(pe):
                    def row_sums(dst, weights, src, value=None):
                        for c in range(NS // JQ):
                            mm = nc.tensor.matmul(dst, weights[:], mat(src)[:, :, c * JQ:(c + 1) * JQ],
                                                  start=(c == 0), stop=(c == NS // JQ - 1))
                            if value is not None and c == 0:
                                nc.tensor.matmul(dst.rearrange("p (i j) -> p i j", j=JQ)[:, :, 0], ident[:],
                                                 value, start=False, stop=False)
                        return mm

                    def residual(t, u, m):
                        pe.wait_ge(sk_ready, t * 2 + (m + 1))
                        row_sums(ps[:, m, 0:NS * JQ], minus_ident, sk[:, m],
                                 op[:, u, HB + m * NS:HB + (m + 1) * NS]).then_inc(ret_ps, 1)

                    def q_sums(t, m):
                        pe.wait_ge(sqq_ready, t * 2 + (m + 1) + PRIMED)
                        if m == 1:
                            pe.wait_ge(sq_ready, t * 2 + 1)
                        row_sums(ps[:, 2 + m, 0:NS * JQ], ident, sqq[:, m]).then_inc(sq_ps, 1)

                    with pe.Fori(0, T // 4) as i:
                        for u in range(4):
                            t = i * 4 + u
                            residual(t, u, 0)
                            residual(t, u, 1)
                            q_sums(t, 0)
                            pe.wait_ge(bS_ready, t * 2 + 2)
                            for c, (at, to) in enumerate(ARG_PARTS):
                                nc.tensor.matmul(ps[:, 4 + c, 0:to - at], ident[:], bS[:, 1, at:to],
                                                 start=True, stop=False)
                            pe.wait_ge(outer_ready, t * 2 + 2)
                            for c, (at, to) in enumerate(ARG_PARTS):
                                mm = nc.tensor.matmul(ps[:, 4 + c, 0:to - at], ident[:], outer[:, 1, at:to],
                                                      start=False, stop=True)
                            mm.then_inc(arg_ps, 1)
                            q_sums(t, 1)
                    pe.wait_ge(sq_ready, 2 * T)
                    q_sums(T, 0)
                    q_sums(T, 1)

                @block.vector
                def _(dve):
                    def partial(b):
                        return ps[:, b, 0:NS * JQ].rearrange("p (i j) -> p i j", j=JQ)

                    def q_reduce(slot, m, sums):
                        dve.wait_ge(sq_ps, sums + PRIMED)
                        nc.vector.tensor_reduce(
                            sq[:, ds(slot, 1), m * NS:(m + 1) * NS].rearrange("p o f -> p (o f)"),
                            partial(2 + m), AX.X, ALU.add).then_inc(sq_ready, 1)

                    def key_product(t, u, m):
                        dve.wait_ge(state_ready, t * 2 + (m + 1) + PRIMED)
                        nc.vector.tensor_tensor(mat(sk[:, m]), mat(S[:, u % 2, m]),
                                                along_i(kn[:, u % 2, m * NS:(m + 1) * NS]),
                                                ALU.mult).then_inc(sk_ready, 1)

                    def residual(t, m):
                        dve.wait_ge(ret_ps, t * 2 + (m + 1))
                        nc.vector.tensor_reduce(delta[:, m], partial(m), AX.X, ALU.add).then_inc(delta_ready, 1)

                    def outer_product(u, m):
                        nc.vector.tensor_tensor(mat(outer[:, m]), along_j(delta[:, m]),
                                                along_i(kn[:, u % 2, m * NS:(m + 1) * NS]),
                                                ALU.mult).then_inc(outer_ready, 1)

                    def new_state(t, u, m):
                        dve.wait_ge(keep_ready, t * 2 + (m + 1))
                        dve.wait_ge(upd_ready, t * 3 + 2 * m + 1)
                        nc.vector.scalar_tensor_tensor(
                            S[:, (u + 1) % 2, m], outer[:, m], step_scalar(t, m), S[:, (u + 1) % 2, m],
                            ALU.mult, ALU.add).then_inc(state_ready, 1)

                    def step(t, u, last):
                        residual(t, 0)
                        q_reduce(t, 1, t * 2)
                        dve.wait_ge(delta_ready, t * 2 + 1)
                        outer_product(u, 0)
                        dve.wait_ge(outer_ready, t * 2 + 1)
                        dve.wait_ge(bS_ready, t * 2 + 1)
                        nc.vector.tensor_tensor(outer[:, 0], outer[:, 0], bS[:, 0], ALU.add).then_inc(arg_ready, 1)
                        residual(t, 1)
                        dve.wait_ge(delta_ready, t * 2 + 2)
                        outer_product(u, 1)
                        new_state(t, u, 0)
                        dve.wait_ge(outer_ready, t * 2 + 2)
                        dve.wait_ge(bS_ready, t * 2 + 2)
                        nc.vector.tensor_tensor(outer[:, 1, 0:SPLIT], outer[:, 1, 0:SPLIT], bS[:, 1, 0:SPLIT],
                                                ALU.add).then_inc(arg_ready, 1)
                        if not last:
                            dve.wait_ge(kn_ready, t + 2)
                            key_product(t + 1, u + 1, 0)
                        new_state(t, u, 1)
                        q_reduce(t + 1, 0, t * 2 + 1)
                        if not last:
                            key_product(t + 1, u + 1, 1)

                    nc.vector.tensor_scalar(minus_ident[:], ident[:], -1.0, None, ALU.mult)
                    for m in range(2):
                        nc.vector.memset(ps[:, 2 + m, 0:NS * JQ], 0.0)
                        nc.vector.memset(S[:, 0, m], 0.0).then_inc(state_ready, 1)
                    dve.wait_ge(kn_ready, 1)
                    for m in range(2):
                        key_product(0, 0, m)
                    with dve.Fori(0, T // 4 - 1) as i:
                        for u in range(4):
                            step(i * 4 + u, u, False)
                    for u in range(4):
                        step(T - 4 + u, u, u == 3)
                    q_reduce(T, 1, 2 * T)
                    q_reduce(T + 1, 0, 2 * T + 1)
                    q_reduce(T + 1, 1, 2 * T + 2)

        XT = sb(after, "XT", [P, DK, B, T])
        wd_sb = sb(after, "wd_sb", [P, E, DK, C])
        wu_sb = sb(after, "wu_sb", [P, E, D])
        upb_sb = sb(after, "upb_sb", [E, D])
        downb_sb = sb(after, "downb_sb", [E, C])
        gw_sb = sb(after, "gw_sb", [P, DK, E])
        iota_sb = sb(after, "iota_sb", [B, E])
        gate_in = sem("gate_in")
        with ExitStack() as ctx:
            zc = sb(ctx, "zc", [P, 2, TG, NS])
            zT = sb(ctx, "zT", [P, 2, B])
            stats = sb(ctx, "stats_m", [P, NT, 6])
            mv = sb(ctx, "mv_m", [P, NT, 2])
            std = sb(ctx, "std_m", [P, NT])
            rstd = sb(ctx, "rstd_m", [P, NT])
            shift = sb(ctx, "shift_m", [P, NT])
            xn = sb(ctx, "xn_m", [P, 2, NT, D])
            BY_ACT = NT // 2

            zc_ready, zT_ps, zT_ready, y_ps, h2_ready = (sem("zc_ready"), sem("zT_ps"), sem("zT_ready"),
                                                         sem("y_ps"), sem("h2_ready"))
            stats2, mv2, std2, rstd2, xn2 = sem("stats2"), sem("mv2"), sem("std2"), sem("rstd2"), sem("xn2")
            shift_ready, xn2_act = sem("shift_ready"), sem("xn2_act")
            xt_ps, xt_read, pool_ps = primed["xt_ps"], primed["xt_read"], sem("pool_ps")

            def groups(eng, turn):
                for g in range(2):
                    turn(g, g, g == 0, False)
                with eng.Fori(1, NG // 2 - 1) as i:
                    for u in range(2):
                        turn(i * 2 + u, u, False, False)
                for u in range(2):
                    turn(NG - 2 + u, u, False, u == 1)

            with nc.Block() as block:
                @block.sync
                def _(sp):
                    for dst, src in ((wd_sb, w_down), (wu_sb, w_up), (gw_sb, gate_w), (iota_sb, iota8),
                                     (upb_sb, up_b), (downb_sb, down_b)):
                        sp.dma_start(dst[:], src).then_inc(gate_in, 16)
                    sp.wait_ge(gate_in, 16 * 6)

                @block.gpsimd
                def _(pool):
                    def stage(g, u, first):
                        if not first:
                            pool.wait_ge(zT_ps, g - 1)
                        nc.gpsimd.tensor_copy(zc[:, u], zsum[:, ds(g * TG, TG), :]).then_inc(zc_ready, 1)

                    for g in range(2):
                        stage(g, g, True)
                    with pool.Fori(1, NG // 2) as i:
                        for u in range(2):
                            stage(i * 2 + u, u, False)

                @block.scalar
                def _(act):
                    def fold_out(g):
                        act.wait_ge(zT_ps, g + 1)
                        act.wait_ge(y_ps, g)
                        nc.scalar.activation(zT[:], ps[:, 0, 0:2 * B].rearrange("p (c b) -> p c b", c=2),
                                             ACT.Copy).then_inc(zT_ready, 1)

                    def turned(g):
                        act.wait_ge(xt_ps, g + 1 + PRIMED)
                        for k in range(DK):
                            nc.scalar.activation(XT[:, k, :, ds(g * TG, TG)].rearrange("p b t -> p t b"),
                                                 ps[:, 6 + k, :].rearrange("p (t b) -> p t b", b=B),
                                                 ACT.Copy).then_inc(xt_read, 1)

                    def turn(g, u, first, last):
                        if not last:
                            fold_out(g + 1)
                        if not first:
                            turned(g - 1)
                        act.wait_ge(mv2, g + 1)
                        nc.scalar.activation(std[:], mv[:, :, 1], ACT.Sqrt, bias=eps_t[:]).then_inc(std2, 1)
                        act.wait_ge(shift_ready, g + 1)
                        if not (isinstance(g, int) and g < 2):
                            act.wait_ge(pool_ps, g - 1)
                        for j in range(BY_ACT):
                            ins = nc.scalar.activation(
                                xn[:, u, j, :], H[:, ds(g * NT + j, 1), :].rearrange("p o d -> p (o d)"),
                                ACT.Identity, bias=shift[:, j:j + 1], scale=rstd[:, j:j + 1])
                        ins.then_inc(xn2_act, 1)

                    fold_out(0)
                    groups(act, turn)
                    turned(NG - 1)

                @block.vector
                def _(dve):
                    def turn(g, u, first, last):
                        hg = H[:, ds(g * NT, NT), :].rearrange("p (q k) d -> p q k d", k=2)
                        dve.wait_ge(y_ps, g + 1)
                        nc.vector.tensor_tensor(hg, hg, ps[:, 2 + 2 * u:4 + 2 * u, :].rearrange(
                            "p k (q d) -> p q k d", d=D), ALU.add).then_inc(h2_ready, 1)
                        dve.wait_ge(h2_ready, g + 1)
                        dve.sem_inc(turns_dve, 1)
                        for j in range(NT):
                            ins = nc.vector.bn_stats(stats[:, j, :], H[:, ds(g * NT + j, 1), :].rearrange(
                                "p o d -> p (o d)"))
                        ins.then_inc(stats2, 1)
                        dve.wait_ge(stats2, g + 1)
                        dve.sem_inc(turns_dve, 1)
                        for j in range(NT):
                            ins = nc.vector.bn_aggr(mv[:, j, :], stats[:, j, :])
                        ins.then_inc(mv2, 1)
                        dve.wait_ge(std2, g + 1)
                        nc.vector.reciprocal(rstd[:], std[:]).then_inc(rstd2, 1)
                        dve.wait_ge(rstd2, g + 1)
                        nc.vector.scalar_tensor_tensor(shift[:], mv[:, :, 0], -1.0, rstd[:], ALU.mult,
                                                       ALU.mult).then_inc(shift_ready, 1)
                        if not (isinstance(g, int) and g < 2):
                            dve.wait_ge(pool_ps, g - 1)
                        for j in range(BY_ACT, NT):
                            ins = nc.vector.tensor_scalar(
                                xn[:, u, j, :], H[:, ds(g * NT + j, 1), :].rearrange("p o d -> p (o d)"),
                                mv[:, j, 0:1], rstd[:, j:j + 1], ALU.subtract, ALU.mult)
                        ins.then_inc(xn2, 1)

                    groups(dve, turn)

                @block.tensor
                def _(pe):
                    def fold_in(g, u, first):
                        pe.wait_ge(zc_ready, g + 1)
                        if not first:
                            pe.wait_ge(zT_ready, g)
                        for c in range(2):
                            mm = nc.tensor.matmul(ps[:, 0, c * B:(c + 1) * B],
                                                  zc[:, u, 4 * c:4 * c + 4, :].rearrange("p t i -> p (t i)"),
                                                  fold[:], start=True, stop=True)
                        mm.then_inc(zT_ps, 1)

                    def product(g, u, free):
                        pe.wait_ge(zT_ready, g + 1)
                        if not free:
                            pe.wait_ge(h2_ready, g - 1)
                        for t in range(TG):
                            r, j, tp = t % 4, t // 2, t % 2
                            mm = nc.tensor.matmul(
                                ps[B * tp:B * tp + B, 2 + 2 * u + j % 2, (j // 2) * D:(j // 2) * D + D],
                                zT[NS * r:NS * r + NS, t // 4, :], wout_sb[NS * r:NS * r + NS, :],
                                start=True, stop=True)
                        mm.then_inc(y_ps, 1)

                    def transposes(g, u):
                        pe.wait_ge(xn2, g + 1)
                        pe.wait_ge(xn2_act, g + 1)
                        pe.wait_ge(xt_read, g * DK + PRIMED)
                        for j in range(NT):
                            for k in range(DK):
                                mm = nc.tensor.transpose(ps[:, 6 + k, j * P:(j + 1) * P],
                                                         xn[:, u, j, k * P:(k + 1) * P], ident[:])
                        mm.then_inc(xt_ps, 1)

                    def time_sum(u, first, last):
                        for j in range(NT):
                            mm = nc.tensor.matmul(ps[0:B, 1, 0:D], fold[:], xn[:, u, j, :],
                                                  start=(first and j == 0), stop=(last and j == NT - 1))
                        mm.then_inc(pool_ps, 1)

                    def turn(g, u, first, last):
                        if not last:
                            fold_in(g + 1, 1 - u, False)
                        if not first:
                            transposes(g - 1, 1 - u)
                        if not last:
                            product(g + 1, 1 - u, first)
                        if not first:
                            time_sum(1 - u, isinstance(g, int) and g == 1, False)

                    pe.wait_ge(wout_in, 16)
                    fold_in(0, 0, True)
                    product(0, 0, True)
                    groups(pe, turn)
                    transposes(NG - 1, (NG - 1) % 2)
                    time_sum((NG - 1) % 2, False, True)

        with ExitStack() as ctx:
            spare = zsum[:].rearrange("p t i -> p (t i)")
            used = [0]

            def reuse(pattern, *shape):
                n = 1
                for k in shape:
                    n *= k
                at = used[0]
                used[0] += n
                a = spare[:, at:at + n]
                names = pattern.split()
                return a.rearrange(f"p ({pattern}) -> p {pattern}", **dict(zip(names, shape)))

            pooled = sb(ctx, "pooled", [B, D])
            pooledT = sb(ctx, "pooledT", [P, DK, B])
            glog = sb(ctx, "glog", [B, E])
            top8 = sb(ctx, "top8", [B, 8])
            topx = sb(ctx, "topx", [B, 8], U32)
            topf = sb(ctx, "topf", [B, 2])
            nmax = sb(ctx, "nmax", [B, 1])
            gex = sb(ctx, "gex", [B, E])
            gsum = sb(ctx, "gsum", [B, 1])
            tex = sb(ctx, "tex", [B, 2])
            tsum = sb(ctx, "tsum", [B, 1])
            tw_rep = sb(ctx, "tw_rep", [B, 2, C])
            hot = sb(ctx, "hot", [B, 2, E])
            hotT = sb(ctx, "hotT", [E, 2, B])
            dense = sb(ctx, "dense", [B, 2, E])
            denseT = sb(ctx, "denseT", [E, B])
            twcol = sb(ctx, "twcol", [P, B])
            dbcol = sb(ctx, "dbcol", [P, B])
            ubT = sb(ctx, "ubT", [P, DK, B])
            idx_row = sb(ctx, "idx_row", [1, 2 * B], U32)

            pooled_step, glog_ps, gate_step = sem("pooled_step"), sem("glog_ps"), sem("gate_step")
            pooledT_ps, hot_ready, hotT_ready = sem("pooledT_ps"), sem("hot_ready"), sem("hotT_ready")
            nmax_ready, gate_exp, topx_ready, topi_out, idx_row_in = (sem("nmax_ready"), sem("gate_exp"),
                                                                     sem("topx_ready"), sem("topi_out"),
                                                                     sem("idx_row_in"))
            dense_ready, dense_ps, denseT_ready, cols_ps = (sem("dense_ready"), sem("dense_ps"),
                                                            sem("denseT_ready"), sem("cols_ps"))
            with nc.Block() as block:
                @block.sync
                def _(sp):
                    sp.wait_ge(topx_ready, 1)
                    sp.dma_start(topi, topx[:, 0:2]).then_inc(topi_out, 16)
                    sp.wait_ge(topi_out, 16)
                    sp.dma_start(idx_row[:], topi.rearrange("b k -> (b k)").unsqueeze(0)).then_inc(idx_row_in, 16)
                    sp.wait_ge(idx_row_in, 16)

                @block.scalar
                def _(act):
                    act.wait_ge(nmax_ready, 1)
                    nc.scalar.activation(gex[:], glog[:], ACT.Exp, bias=nmax[:]).then_inc(gate_exp, 1)
                    nc.scalar.activation(tex[:], top8[:, 0:2], ACT.Exp, bias=nmax[:]).then_inc(gate_exp, 1)

                @block.tensor
                def _(pe):
                    pe.wait_ge(pooled_step, 1)
                    for k in range(DK):
                        mm = nc.tensor.transpose(ps[:, 4, k * B:(k + 1) * B], pooled[:, k * P:(k + 1) * P],
                                                 ident[0:B, 0:B])
                    mm.then_inc(pooledT_ps, 1)
                    pe.wait_ge(pooled_step, 2)
                    for k in range(DK):
                        mm = nc.tensor.matmul(ps[0:B, 0, 0:E], pooledT[:, k, :], gw_sb[:, k, :],
                                              start=(k == 0), stop=(k == DK - 1))
                    mm.then_inc(glog_ps, 1)
                    pe.wait_ge(hot_ready, 1)
                    for k in range(2):
                        mm = nc.tensor.transpose(ps[0:E, 5, k * B:(k + 1) * B], hot[:, k, :], ident[0:B, 0:B])
                    mm.then_inc(dense_ps, 1)
                    pe.wait_ge(hotT_ready, 1)
                    for k in range(2):
                        mm = nc.tensor.matmul(ps[C * k:C * k + C, 6, 0:B], downb_sb[:], hotT[:, k, :],
                                              start=True, stop=True)
                    pe.wait_ge(dense_ready, 1)
                    nc.tensor.transpose(ps[0:E, 1, 0:B], dense[:, 0, :], ident[0:B, 0:B]).then_inc(dense_ps, 1)
                    nc.tensor.matmul(ps[:, 2, 0:B], tw_rep[:].rearrange("p k c -> p (k c)"), ident[0:B, 0:B],
                                     start=True, stop=True)
                    pe.wait_ge(denseT_ready, 1)
                    for k in range(DK):
                        mm = nc.tensor.matmul(ps[:, 3, k * B:(k + 1) * B], upb_sb[:, k * P:(k + 1) * P],
                                              denseT[:], start=True, stop=True)
                    mm.then_inc(cols_ps, 1)

                @block.vector
                def _(dve):
                    steps = [0]

                    def link(ins):
                        steps[0] += 1
                        ins.then_inc(gate_step, 1)
                        dve.wait_ge(gate_step, steps[0])

                    nc.vector.tensor_copy(pooled[:], ps[0:B, 1, 0:D]).then_inc(pooled_step, 1)
                    dve.wait_ge(pooledT_ps, 1)
                    nc.vector.tensor_copy(pooledT[:], ps[:, 4, 0:DK * B].rearrange(
                        "p (k b) -> p k b", k=DK)).then_inc(pooled_step, 1)
                    dve.wait_ge(glog_ps, 1)
                    link(nc.vector.tensor_scalar(glog[:], ps[0:B, 0, 0:E], 1.0 / T, None, ALU.mult))
                    link(nc.vector.max(top8[:], glog[:]))
                    nc.vector.tensor_scalar(nmax[:], top8[:, 0:1], -1.0, None, ALU.mult).then_inc(nmax_ready, 1)
                    link(nc.vector.max_index(topx[:], top8[:], glog[:]))
                    nc.vector.tensor_copy(topf[:], topx[:, 0:2]).then_inc(topx_ready, 1)
                    dve.wait_ge(topx_ready, 1)
                    for k in range(2):
                        ins = nc.vector.tensor_scalar(hot[:, k, :], iota_sb[:], topf[:, k:k + 1], None, ALU.is_equal)
                    ins.then_inc(hot_ready, 1)
                    dve.wait_ge(gate_exp, 2)
                    link(nc.vector.tensor_reduce(gsum[:], gex[:], AX.X, ALU.add))
                    link(nc.vector.reciprocal(gsum[:], gsum[:]))
                    link(nc.vector.tensor_scalar(tex[:], tex[:], gsum[:], None, ALU.mult))
                    link(nc.vector.tensor_reduce(tsum[:], tex[:], AX.X, ALU.add))
                    link(nc.vector.tensor_scalar(tsum[:], tsum[:], 1e-8, None, ALU.add))
                    link(nc.vector.reciprocal(tsum[:], tsum[:]))
                    link(nc.vector.tensor_scalar(tex[:], tex[:], tsum[:], None, ALU.mult))
                    dve.wait_ge(dense_ps, 1)
                    nc.vector.tensor_copy(hotT[:], ps[0:E, 5, 0:2 * B].rearrange(
                        "e (k b) -> e k b", k=2)).then_inc(hotT_ready, 1)
                    nc.vector.tensor_copy(tw_rep[:], tex[:].unsqueeze(2).to_broadcast([B, 2, C]))
                    for k in range(2):
                        link(nc.vector.tensor_scalar(dense[:, k, :], hot[:, k, :], tex[:, k:k + 1], None, ALU.mult))
                    nc.vector.tensor_tensor(dense[:, 0, :], dense[:, 0, :], dense[:, 1, :],
                                            ALU.add).then_inc(dense_ready, 1)
                    dve.wait_ge(dense_ps, 2)
                    nc.vector.tensor_copy(denseT[:], ps[0:E, 1, 0:B]).then_inc(denseT_ready, 1)
                    dve.wait_ge(cols_ps, 1)
                    nc.vector.tensor_copy(twcol[:], ps[:, 2, 0:B])
                    nc.vector.tensor_copy(dbcol[:], ps[:, 6, 0:B])
                    nc.vector.tensor_copy(ubT[:], ps[:, 3, 0:DK * B].rearrange("p (k b) -> p k b", k=DK))

            SL = 8
            LEAD = 5
            PICK = 4
            wd_st = reuse("s k e c", SL, DK, 2, C)
            wu_st = reuse("s d", SL, D)
            act_g = sb(ctx, "act_g", [P, SL, T])
            used[0] = 0
            stg = reuse("s k n", 2, DK, GT)

            wd_dve, wd_act, wu_dve, wu_pool, down_ps = (sem("wd_dve"), sem("wd_act"), sem("wu_dve"), sem("wu_pool"),
                                                        sem("down_ps"))
            gelu_ready, up_ps, out_read_act, out_read_dve = (sem("gelu_ready"), sem("up_ps"),
                                                             sem("out_read_act"), sem("out_read_dve"))

            def experts(engine, b, n, k):
                _, values = nc.values_load_multi_w_load_instructions(
                    idx_row[:].rearrange("o (b k) -> o b k", k=2)[:, ds(b, n), k], engines=[engine],
                    min_val=0, max_val=E - 1)
                return values

            def down_operands(s, k, e):
                return wd_st[:, s, :, k, :], wd_sb[:, ds(e, 1), :, :].rearrange("p o k c -> p (o k) c")

            def column(a, b):
                return a[:, ds(b, 1)]

            def freed(b, row):
                return None if row is not None and row + LEAD < SL else b + (LEAD + 1 - SL)

            def up_operands(b, s, k, e):
                rows = slice(C * k, C * k + C)
                return (wu_st[rows, s, :], wu_sb[rows, ds(e, 1), :].rearrange("p o d -> p (o d)"),
                        twcol[rows, ds(b, 1)])

            def rows_of_batch(eng, step, choose=None):
                def turn(b, row, left):
                    chosen = []
                    for u in range(SL):
                        if choose and not chosen:
                            n = PICK if left is None else min(PICK, left - u - LEAD)
                            chosen = choose(b + u + LEAD, n) if n > 0 else []
                        step(b + u, u, None if row is None else row + u, None if left is None else left - u - 1,
                             chosen.pop(0) if chosen else None)

                turn(0, 0, None)
                with eng.Fori(1, B // SL - 1) as i:
                    turn(i * SL, None, None)
                turn(B - SL, None, SL)

            with nc.Block() as block:
                @block.gpsimd
                def _(pool):
                    def choose(b, n):
                        return list(experts(mybir.EngineType.Pool, b, n, 1))

                    def stage(b, s, e, before):
                        if before is not None:
                            pool.wait_ge(up_ps, before)
                        slot, weights, top = up_operands(b, s, 1, e)
                        nc.gpsimd.tensor_tensor(slot, weights, top.to_broadcast([C, D]), ALU.mult).then_inc(wu_pool, 1)

                    def step(b, u, row, left, e):
                        if e is not None:
                            stage(b + LEAD, (u + LEAD) % SL, e, freed(b, row))

                    for b, e in enumerate(choose(0, LEAD)):
                        stage(b, b, e, None)
                    rows_of_batch(pool, step, choose)

                @block.vector
                def _(dve):
                    def choose(b, n):
                        return list(experts(mybir.EngineType.DVE, b, n, 0))

                    def stage(b, s, e, before):
                        if before is not None:
                            dve.wait_ge(up_ps, before)
                        nc.vector.tensor_copy(*down_operands(s, 0, e)).then_inc(wd_dve, 1)
                        slot, weights, top = up_operands(b, s, 0, e)
                        nc.vector.tensor_scalar(slot, weights, top, None, ALU.mult).then_inc(wu_dve, 1)

                    def evacuate(b, s):
                        dve.wait_ge(up_ps, b + 1)
                        nc.vector.tensor_scalar(
                            XT[:, 1, ds(b, 1), :].rearrange("p o t -> p (o t)"), ps[:, 4 + 2 * (s % 2) + 1, 0:T],
                            column(ubT[:, 1], b), None, ALU.add).then_inc(out_read_dve, 1)

                    def step(b, u, row, left, chosen):
                        if row != 0:
                            evacuate(b - 1, u + SL - 1)
                        if chosen is not None:
                            stage(b + LEAD, (u + LEAD) % SL, chosen, freed(b, row))

                    for b, chosen in enumerate(choose(0, LEAD)):
                        stage(b, b, chosen, None)
                    rows_of_batch(dve, step, choose)
                    evacuate(B - 1, 1)

                @block.scalar
                def _(act):
                    def gelu(b, s):
                        act.wait_ge(down_ps, b + 1)
                        nc.scalar.activation(act_g[:, s, :], ps[:, s % 4, 0:T], ACT.Gelu,
                                             bias=column(dbcol, b)).then_inc(gelu_ready, 1)

                    def evacuate(b, s):
                        act.wait_ge(up_ps, b + 1)
                        nc.scalar.activation(
                            XT[:, 0, ds(b, 1), :].rearrange("p o t -> p (o t)"), ps[:, 4 + 2 * (s % 2), 0:T],
                            ACT.Identity, bias=column(ubT[:, 0], b)).then_inc(out_read_act, 1)

                    def choose(b, n):
                        return list(experts(mybir.EngineType.Activation, b, n, 1))

                    def stage(s, e):
                        nc.scalar.activation(*down_operands(s, 1, e), ACT.Copy).then_inc(wd_act, 1)

                    def step(b, u, row, left, e):
                        if left is None or left >= 1:
                            gelu(b + 1, (u + 1) % SL)
                        if row != 0:
                            evacuate(b - 1, u + SL - 1)
                        if e is not None:
                            stage((u + LEAD) % SL, e)

                    for b, e in enumerate(choose(0, LEAD)):
                        stage(b, e)
                    gelu(0, 0)
                    rows_of_batch(act, step, choose)
                    evacuate(B - 1, 1)

                @block.tensor
                def _(pe):
                    def down(b, s):
                        pe.wait_ge(wd_dve, b + 1)
                        pe.wait_ge(wd_act, b + 1)
                        for k in range(DK):
                            mm = nc.tensor.matmul(ps[:, s % 4, 0:T], wd_st[:, s, k].rearrange("p e c -> p (e c)"),
                                                  XT[:, k, ds(b, 1), :].rearrange("p o t -> p (o t)"),
                                                  start=(k == 0), stop=(k == DK - 1))
                        mm.then_inc(down_ps, 1)

                    def step(b, u, row, left, _):
                        if left is None or left >= 2:
                            down(b + 2, (u + 2) % SL)
                        pe.wait_ge(gelu_ready, b + 1)
                        pe.wait_ge(wu_dve, b + 1)
                        pe.wait_ge(wu_pool, b + 1)
                        if row is None or row >= 2:
                            pe.wait_ge(out_read_act, b - 1)
                            pe.wait_ge(out_read_dve, b - 1)
                        for k in range(DK):
                            mm = nc.tensor.matmul(ps[:, 4 + 2 * (u % 2) + k, 0:T], wu_st[:, u, k * P:(k + 1) * P],
                                                  act_g[:, u, :], start=True, stop=True)
                        mm.then_inc(up_ps, 1)

                    for b in range(2):
                        down(b, b)
                    rows_of_batch(pe, step)

        staged, out_ps, sum_ready, stored = sem("staged"), sem("out_ps"), primed["sum_ready"], sem("stored")

        with nc.Block() as block:
            def stage_src(g, k):
                return XT[:, k, :, ds(g * TG, TG)].rearrange("p b t -> p t b")

            def stage_dst(u, k):
                return stg[:, u, k].rearrange("p (t b) -> p t b", b=B)

            @block.scalar
            def _(act):
                def stage(g, u, first):
                    if not first:
                        act.wait_ge(out_ps, g - 1)
                    for k in range(DK):
                        nc.scalar.activation(stage_dst(u, k), stage_src(g, k), ACT.Copy).then_inc(staged, 1)

                for g in range(2):
                    stage(g, g, True)
                with act.Fori(1, NG // 2) as i:
                    for u in range(2):
                        stage(i * 2 + u, u, False)

            @block.tensor
            def _(pe):
                def turn(g, u, first):
                    pe.wait_ge(staged, g * 2 + 2)
                    if not first:
                        pe.wait_ge(sum_ready, g - 1 + PRIMED)
                    for j in range(NT):
                        for k in range(DK):
                            mm = nc.tensor.transpose(
                                ps[:, 2 * u + j // 2, (j % 2) * D + k * P:(j % 2) * D + (k + 1) * P],
                                stg[:, u, k, j * P:(j + 1) * P], ident[:])
                    mm.then_inc(out_ps, 1)

                for g in range(2):
                    turn(g, g, True)
                with pe.Fori(1, NG // 2) as i:
                    for u in range(2):
                        turn(i * 2 + u, u, False)

            @block.vector
            def _(dve):
                with dve.Fori(0, NG // 2) as i:
                    for u in range(2):
                        g = i * 2 + u
                        hg = H[:, ds(g * NT, NT), :]
                        dve.wait_ge(out_ps, g + 1)
                        nc.vector.tensor_tensor(
                            hg, hg, ps[:, 2 * u:2 * u + 2, :].rearrange("p k (j d) -> p (k j) d", d=D),
                            ALU.add).then_inc(sum_ready, 1)

            @block.sync
            def _(sp):
                with sp.Fori(0, NG) as g:
                    sp.wait_ge(sum_ready, g + 1 + PRIMED)
                    for tp in range(2):
                        sp.dma_start(
                            out[:, ds(g * TG, TG), :].rearrange("b (j tp) d -> tp b j d", tp=2)[tp],
                            H[B * tp:B * tp + B, ds(g * NT, NT), :]).then_inc(stored, 16)
                sp.wait_ge(stored, 16 * 2 * NG)


def kernel(x, x_txt, L0_tok_W, L0_txt_emb0, L0_txt_emb1, L0_txt_emb2, L0_txt_emb3, L0_txt_W0, L0_txt_W1,
           L0_txt_W2, L0_txt_W3, L0_attn_W_in, L0_attn_W_router, L0_attn_W_kv, L0_attn_W_beta, L0_attn_b_beta,
           L0_attn_W_q, L0_attn_W_out, L0_ffn_gate_w, L0_ffn_down_w, L0_ffn_down_b, L0_ffn_up_w, L0_ffn_up_b):
    import numpy as np
    import concourse.bacc as bacc
    from concourse.bass_utils import run_bass_kernel_spmd

    A = np.asarray
    x, x_txt = A(x), A(x_txt)
    B, CI, IM, _ = x.shape
    PA = 16
    G = IM // PA
    D = L0_tok_W.shape[0]
    T = G * G + x_txt.shape[1]
    NB, NS = L0_attn_b_beta.shape
    E, C, _ = L0_ffn_down_w.shape

    def chunks(w):
        return w.reshape(-1, 128, w.shape[1]).transpose(1, 0, 2)

    feat = x.reshape(B, CI, G, PA, G, PA).transpose(1, 3, 5, 2, 4, 0).reshape(CI * PA * PA, G * G * B)
    feat = feat.reshape(-1, 128, (G * G) // 8, 8 * B).transpose(2, 1, 0, 3)
    kv = A(L0_attn_W_kv).reshape(NB, 2, NS, -1)
    wb = A(L0_attn_W_beta).reshape(NB, NS, -1)
    rows = []
    for h in range(2):
        n = slice(2 * h, 2 * h + 2)
        rows += [kv[n, 0].reshape(2 * NS, -1), kv[n, 1].reshape(2 * NS, -1), wb[n].reshape(2 * NS, -1)]
    proj = np.concatenate(rows + [A(L0_attn_W_q), A(L0_attn_W_router)], 0).T
    up = A(L0_ffn_up_w).transpose(2, 0, 1)
    arrays = {
        "patches": feat,
        "wtok": chunks(A(L0_tok_W).T),
        "idx": x_txt.T.reshape(-1, 128).T,
        "emb0": A(L0_txt_emb0), "emb1": A(L0_txt_emb1), "emb2": A(L0_txt_emb2), "emb3": A(L0_txt_emb3),
        "wtxt": np.concatenate([A(w).T for w in (L0_txt_W0, L0_txt_W1, L0_txt_W2, L0_txt_W3)], 0),
        "w_in": chunks(A(L0_attn_W_in).T),
        "w_proj": chunks(proj),
        "b_beta": np.broadcast_to(A(L0_attn_b_beta).reshape(1, 2, 2 * NS), (128, 2, 2 * NS)),
        "w_out": np.concatenate([A(L0_attn_W_out).T] * 4, 0),
        "gate_w": chunks(A(L0_ffn_gate_w).T),
        "w_down": A(L0_ffn_down_w).transpose(2, 0, 1).reshape(D // 128, 128, E, C).transpose(1, 2, 0, 3),
        "w_up": np.concatenate([up, up], 0),
        "up_b": A(L0_ffn_up_b),
        "down_b": A(L0_ffn_down_b),
        "iota8": np.tile(np.arange(E, dtype=np.float32), (B, 1)),
    }
    nc = bacc.Bacc("TRN2", target_bir_lowering=False, num_devices=1)
    feed, aps = {}, {}
    for name, a in arrays.items():
        a = np.ascontiguousarray(a)
        feed[f"{name}_dram"] = a
        aps[name] = nc.dram_tensor(f"{name}_dram", a.shape, mybir.dt.from_np(a.dtype), kind="ExternalInput").ap()
    out = nc.dram_tensor("out_dram", (B, T, D), F32, kind="ExternalOutput").ap()
    aps["embs"] = [aps.pop(f"emb{i}") for i in range(4)]
    early_fusion_kernel(nc, out=out, **aps)
    got = run_bass_kernel_spmd(nc, [feed], core_ids=[0])
    return got.results[0]["out_dram"]
```
